# Optimizing a Trainium2 kernel written in Bass

```python
import numpy as np
import jax
import jax.numpy as jnp

def _softmax(x, axis=-1):
    return jax.nn.softmax(x, axis=axis)

def _gelu(x):
    return jax.nn.gelu(x, approximate=True)

def _silu(x):
    return jax.nn.silu(x)

def _sigmoid(x):
    return jax.nn.sigmoid(x)

def _layernorm(x, axis=-1, eps=1e-05):
    m = jnp.mean(x, axis=axis, keepdims=True)
    v = jnp.var(x, axis=axis, keepdims=True)
    return (x - m) / jnp.sqrt(v + eps)

def _scatter_add(tgt, idx, src, axis=0):
    return tgt.at[idx].add(src)

def _segment_sum(src, seg, n):
    return jax.ops.segment_sum(src, seg, n)
kernel_name = 'mk_hybrid_d1_jaxref_r8_de881b'

def setup_inputs(seed: int=0):
    np.random.seed(seed)
    _w = jnp.asarray

    def _L0_attn_a_setup():
        import jax, jax.numpy as jnp
        import numpy as np
        import math
        B, L, D = (2, 512, 128)
        H, DK, DV = (4, 32, 32)
        CHUNK = 32
        PROB_FLOOR = 0.02

        def _l2norm(x, eps=1e-06):
            return x * jax.lax.rsqrt(jnp.sum(x * x, -1, keepdims=True) + eps)

        def _silu(x):
            return x * jax.nn.sigmoid(x)

        def _short_conv(x, w):
            K = w.shape[-1]
            xp = jnp.pad(x, ((0, 0), (K - 1, 0), (0, 0)))
            y = sum((xp[:, j:j + x.shape[1], :] * w[:, j] for j in range(K)))
            return _silu(y)

        def _fir_conv(x, filt):
            b, l, h, d = x.shape
            K = filt.shape[-1]
            xf = jnp.pad(x.reshape(b, l, h * d).transpose(0, 2, 1), ((0, 0), (0, 0), (K - 1, 0)))
            w = filt.reshape(h * d, 1, K)
            y = jax.lax.conv_general_dilated(xf, w, (1,), 'VALID', dimension_numbers=('NCH', 'OIH', 'NCH'), feature_group_count=h * d)
            return y.transpose(0, 2, 1).reshape(b, l, h, d)

        def _delta_rule_chunkwise(q, k, v, beta, chunk=CHUNK):
            b, h, Lq, dk = q.shape
            dv = v.shape[-1]
            n = Lq // chunk
            q = _l2norm(q)
            k = _l2norm(k)
            v = v * beta[..., None]
            kb = k * beta[..., None]
            rs = lambda t: t.reshape(b, h, n, chunk, t.shape[-1])
            qc, kc, vc, kbc = (rs(q), rs(k), rs(v), rs(kb))
            strict_lower = jnp.tril(jnp.ones((chunk, chunk), bool), -1)
            M = jnp.where(strict_lower, jnp.einsum('bhncd,bhnmd->bhncm', kbc, kc), 0.0)
            eye = jnp.eye(chunk, dtype=q.dtype)
            T = jax.scipy.linalg.solve_triangular(eye + M, jnp.broadcast_to(eye, M.shape), lower=True, unit_diagonal=True)
            u = T @ vc
            w = T @ kbc
            incl_lower = jnp.tril(jnp.ones((chunk, chunk), bool), 0)

            def step(S, xs):
                q_i, k_i, u_i, w_i = xs
                attn = jnp.where(incl_lower, q_i @ k_i.swapaxes(-1, -2), 0.0)
                u_adj = u_i - w_i @ S
                out_i = q_i @ S + attn @ u_adj
                S = S + k_i.swapaxes(-1, -2) @ u_adj
                return (S, out_i)
            S0 = jnp.zeros((b, h, dk, dv), q.dtype)
            xs = tuple((jnp.moveaxis(t, 2, 0) for t in (qc, kc, u, w)))
            S, out = jax.lax.scan(step, S0, xs)
            out = jnp.moveaxis(out, 0, 2).reshape(b, h, Lq, dv)
            return (out, S)

        def _rmsnorm(x, w, eps=1e-05):
            return x * jax.lax.rsqrt(jnp.mean(x * x, -1, keepdims=True) + eps) * w

        def _per_head_stats(x):
            mean = jnp.mean(x, -1, keepdims=True)
            var = jnp.var(x, -1, keepdims=True)
            am = jnp.mean(jnp.abs(x), -1, keepdims=True)
            l2 = jnp.sqrt(jnp.sum(x * x, -1, keepdims=True))
            return jnp.concatenate([mean, var, am, l2], -1)

        def _forward(hidden_states, q_w, k_w, v_w, b_w, q_cw, k_cw, v_cw, fir_short_w, fir_long_w, mlp1_w, mlp1_b, mlp2_w, mlp2_b, logit_temp, conv_res_logit, norm_w, o_w):
            b, l, _ = hidden_states.shape
            q_in = _short_conv(hidden_states @ q_w.T, q_cw)
            k_in = _short_conv(hidden_states @ k_w.T, k_cw)
            v_in = _short_conv(hidden_states @ v_w.T, v_cw)
            q = q_in.reshape(b, l, H, DK)
            k = k_in.reshape(b, l, H, DK)
            v_direct = v_in.reshape(b, l, H, DV)
            beta = jnp.maximum(jax.nn.sigmoid(hidden_states @ b_w.T), 1e-06)
            delta_out, _S = _delta_rule_chunkwise(q.transpose(0, 2, 1, 3), k.transpose(0, 2, 1, 3), v_direct.transpose(0, 2, 1, 3), beta.transpose(0, 2, 1))
            delta_out = delta_out.transpose(0, 2, 1, 3)
            local_short = _fir_conv(v_direct, fir_short_w)
            local_long = _fir_conv(v_direct, fir_long_w)
            stats = jnp.concatenate([_per_head_stats(local_short), _per_head_stats(local_long), _per_head_stats(delta_out), _per_head_stats(v_direct)], -1)
            hs_exp = jnp.broadcast_to(hidden_states[:, :, None, :], (b, l, H, hidden_states.shape[-1]))
            gate_in = jnp.concatenate([hs_exp, stats], -1)
            h1 = jax.nn.gelu(gate_in @ mlp1_w.T + mlp1_b)
            logits = h1 @ mlp2_w.T + mlp2_b
            temp = jax.nn.softplus(logit_temp)
            p = jax.nn.softmax(logits / temp, -1)
            p = jnp.maximum(p, PROB_FLOOR)
            p = p / jnp.sum(p, -1, keepdims=True)
            o = p[..., 0:1] * local_short + p[..., 1:2] * local_long + p[..., 2:3] * delta_out + p[..., 3:4] * v_direct
            o = o + jax.nn.sigmoid(conv_res_logit)[None, None, :, None] * local_short
            o = _rmsnorm(o, norm_w)
            o = o.reshape(b, l, H * DV) @ o_w.T
            return o
        key = jax.random.key(seed)
        ks = jax.random.split(key, 16)
        s = 0.02
        hidden_gate = D * 2 // 2
        gate_in_dim = D + 16
        inp = {'hidden_states': jax.random.normal(ks[0], (B, L, D), jnp.float32), 'q_w': jax.random.normal(ks[1], (D, D), jnp.float32) * s, 'k_w': jax.random.normal(ks[2], (D, D), jnp.float32) * s, 'v_w': jax.random.normal(ks[3], (D, D), jnp.float32) * s, 'b_w': jax.random.normal(ks[4], (H, D), jnp.float32) * s, 'q_cw': jax.random.normal(ks[5], (D, 4), jnp.float32) * s, 'k_cw': jax.random.normal(ks[6], (D, 4), jnp.float32) * s, 'v_cw': jax.random.normal(ks[7], (D, 4), jnp.float32) * s, 'fir_short_w': jax.random.normal(ks[8], (H, DV, 5), jnp.float32) * s, 'fir_long_w': jax.random.normal(ks[9], (H, DV, 64), jnp.float32) * s, 'mlp1_w': jax.random.normal(ks[10], (hidden_gate, gate_in_dim), jnp.float32) * s, 'mlp1_b': jnp.zeros((hidden_gate,), jnp.float32), 'mlp2_w': jax.random.normal(ks[11], (4, hidden_gate), jnp.float32) * s, 'mlp2_b': jnp.array([-0.5, -0.5, 1.0, 3.0], jnp.float32), 'logit_temp': jnp.full((1,), math.log(math.expm1(0.7)), jnp.float32), 'conv_res_logit': jnp.full((H,), -2.0, jnp.float32), 'norm_w': jnp.ones((DV,), jnp.float32), 'o_w': jax.random.normal(ks[12], (D, D), jnp.float32) * s}
        return inp
    _L0_attn_a_in = _L0_attn_a_setup()

    def _L0_attn_b_setup():
        import jax, jax.numpy as jnp
        import numpy as np
        import math
        D_MODEL = 128
        N_HEADS = 16
        THETA = 10000.0
        SEQ = 512
        BATCH = 1
        CLAMP = 100000.0

        def _apply_rope(t, cos, sin):
            te = t[..., 0::2]
            to = t[..., 1::2]
            re = te * cos - to * sin
            ro = te * sin + to * cos
            return jnp.stack([re, ro], axis=-1).reshape(t.shape)
        key = jax.random.key(seed)
        ks = jax.random.split(key, 5)
        std = math.sqrt(2.0 / (D_MODEL + D_MODEL))
        x = jax.random.normal(ks[0], (BATCH, SEQ, D_MODEL), dtype=jnp.float32)
        WQ = jax.random.normal(ks[1], (D_MODEL, D_MODEL), dtype=jnp.float32) * std
        WK = jax.random.normal(ks[2], (D_MODEL, D_MODEL), dtype=jnp.float32) * std
        WV = jax.random.normal(ks[3], (D_MODEL, D_MODEL), dtype=jnp.float32) * std
        WO = jax.random.normal(ks[4], (D_MODEL, D_MODEL), dtype=jnp.float32) * std
        return {'x': x, 'WQ': WQ, 'WK': WK, 'WV': WV, 'WO': WO}
    _L0_attn_b_in = _L0_attn_b_setup()

    def _L0_ffn_setup():
        import math
        import jax, jax.numpy as jnp
        import numpy as np
        CAPACITY_FACTOR = 1.25
        key = jax.random.key(seed)
        ks = jax.random.split(key, 5)
        B, S, H, F, E = (4, 512, 128, 128, 32)
        scale_in = 1.0 / math.sqrt(H)
        scale_mid = 1.0 / math.sqrt(F)
        return {'x': jax.random.normal(ks[0], (B, S, H), dtype=jnp.float32), 'w_router': jax.random.normal(ks[1], (H, E), dtype=jnp.float32) * scale_in, 'w_gate': jax.random.normal(ks[2], (E, H, F), dtype=jnp.float32) * scale_in, 'w_up': jax.random.normal(ks[3], (E, H, F), dtype=jnp.float32) * scale_in, 'w_down': jax.random.normal(ks[4], (E, F, H), dtype=jnp.float32) * scale_mid}
    _L0_ffn_in = _L0_ffn_setup()
    _d = {'L0_attn_a_hidden_states': _L0_attn_a_in['hidden_states'], 'L0_attn_a_q_w': _L0_attn_a_in['q_w'], 'L0_attn_a_k_w': _L0_attn_a_in['k_w'], 'L0_attn_a_v_w': _L0_attn_a_in['v_w'], 'L0_attn_a_b_w': _L0_attn_a_in['b_w'], 'L0_attn_a_q_cw': _L0_attn_a_in['q_cw'], 'L0_attn_a_k_cw': _L0_attn_a_in['k_cw'], 'L0_attn_a_v_cw': _L0_attn_a_in['v_cw'], 'L0_attn_a_fir_short_w': _L0_attn_a_in['fir_short_w'], 'L0_attn_a_fir_long_w': _L0_attn_a_in['fir_long_w'], 'L0_attn_a_mlp1_w': _L0_attn_a_in['mlp1_w'], 'L0_attn_a_mlp1_b': _L0_attn_a_in['mlp1_b'], 'L0_attn_a_mlp2_w': _L0_attn_a_in['mlp2_w'], 'L0_attn_a_mlp2_b': _L0_attn_a_in['mlp2_b'], 'L0_attn_a_logit_temp': _L0_attn_a_in['logit_temp'], 'L0_attn_a_conv_res_logit': _L0_attn_a_in['conv_res_logit'], 'L0_attn_a_norm_w': _L0_attn_a_in['norm_w'], 'L0_attn_a_o_w': _L0_attn_a_in['o_w'], 'L0_attn_b_WQ': _L0_attn_b_in['WQ'], 'L0_attn_b_WK': _L0_attn_b_in['WK'], 'L0_attn_b_WV': _L0_attn_b_in['WV'], 'L0_attn_b_WO': _L0_attn_b_in['WO'], 'L0_ffn_w_router': _L0_ffn_in['w_router'], 'L0_ffn_w_gate': _L0_ffn_in['w_gate'], 'L0_ffn_w_up': _L0_ffn_in['w_up'], 'L0_ffn_w_down': _L0_ffn_in['w_down']}
    _x0 = _d['L0_attn_a_hidden_states']
    _d['L0_attn_a_hidden_states'] = jax.random.normal(jax.random.fold_in(jax.random.key(seed), 1), (8, 512, 128), dtype=_x0.dtype)
    del _x0
    return _d

def reference(L0_attn_a_hidden_states, L0_attn_a_q_w, L0_attn_a_k_w, L0_attn_a_v_w, L0_attn_a_b_w, L0_attn_a_q_cw, L0_attn_a_k_cw, L0_attn_a_v_cw, L0_attn_a_fir_short_w, L0_attn_a_fir_long_w, L0_attn_a_mlp1_w, L0_attn_a_mlp1_b, L0_attn_a_mlp2_w, L0_attn_a_mlp2_b, L0_attn_a_logit_temp, L0_attn_a_conv_res_logit, L0_attn_a_norm_w, L0_attn_a_o_w, L0_attn_b_WQ, L0_attn_b_WK, L0_attn_b_WV, L0_attn_b_WO, L0_ffn_w_router, L0_ffn_w_gate, L0_ffn_w_up, L0_ffn_w_down):

    def _L0_attn_a_ref(hidden_states, q_w, k_w, v_w, b_w, q_cw, k_cw, v_cw, fir_short_w, fir_long_w, mlp1_w, mlp1_b, mlp2_w, mlp2_b, logit_temp, conv_res_logit, norm_w, o_w):
        import jax, jax.numpy as jnp
        import numpy as np
        import math
        B, L, D = (2, 512, 128)
        H, DK, DV = (4, 32, 32)
        CHUNK = 32
        PROB_FLOOR = 0.02

        def _l2norm(x, eps=1e-06):
            return x * jax.lax.rsqrt(jnp.sum(x * x, -1, keepdims=True) + eps)

        def _silu(x):
            return x * jax.nn.sigmoid(x)

        def _short_conv(x, w):
            K = w.shape[-1]
            xp = jnp.pad(x, ((0, 0), (K - 1, 0), (0, 0)))
            y = sum((xp[:, j:j + x.shape[1], :] * w[:, j] for j in range(K)))
            return _silu(y)

        def _fir_conv(x, filt):
            b, l, h, d = x.shape
            K = filt.shape[-1]
            xf = jnp.pad(x.reshape(b, l, h * d).transpose(0, 2, 1), ((0, 0), (0, 0), (K - 1, 0)))
            w = filt.reshape(h * d, 1, K)
            y = jax.lax.conv_general_dilated(xf, w, (1,), 'VALID', dimension_numbers=('NCH', 'OIH', 'NCH'), feature_group_count=h * d)
            return y.transpose(0, 2, 1).reshape(b, l, h, d)

        def _delta_rule_chunkwise(q, k, v, beta, chunk=CHUNK):
            b, h, Lq, dk = q.shape
            dv = v.shape[-1]
            n = Lq // chunk
            q = _l2norm(q)
            k = _l2norm(k)
            v = v * beta[..., None]
            kb = k * beta[..., None]
            rs = lambda t: t.reshape(b, h, n, chunk, t.shape[-1])
            qc, kc, vc, kbc = (rs(q), rs(k), rs(v), rs(kb))
            strict_lower = jnp.tril(jnp.ones((chunk, chunk), bool), -1)
            M = jnp.where(strict_lower, jnp.einsum('bhncd,bhnmd->bhncm', kbc, kc), 0.0)
            eye = jnp.eye(chunk, dtype=q.dtype)
            T = jax.scipy.linalg.solve_triangular(eye + M, jnp.broadcast_to(eye, M.shape), lower=True, unit_diagonal=True)
            u = T @ vc
            w = T @ kbc
            incl_lower = jnp.tril(jnp.ones((chunk, chunk), bool), 0)

            def step(S, xs):
                q_i, k_i, u_i, w_i = xs
                attn = jnp.where(incl_lower, q_i @ k_i.swapaxes(-1, -2), 0.0)
                u_adj = u_i - w_i @ S
                out_i = q_i @ S + attn @ u_adj
                S = S + k_i.swapaxes(-1, -2) @ u_adj
                return (S, out_i)
            S0 = jnp.zeros((b, h, dk, dv), q.dtype)
            xs = tuple((jnp.moveaxis(t, 2, 0) for t in (qc, kc, u, w)))
            S, out = jax.lax.scan(step, S0, xs)
            out = jnp.moveaxis(out, 0, 2).reshape(b, h, Lq, dv)
            return (out, S)

        def _rmsnorm(x, w, eps=1e-05):
            return x * jax.lax.rsqrt(jnp.mean(x * x, -1, keepdims=True) + eps) * w

        def _per_head_stats(x):
            mean = jnp.mean(x, -1, keepdims=True)
            var = jnp.var(x, -1, keepdims=True)
            am = jnp.mean(jnp.abs(x), -1, keepdims=True)
            l2 = jnp.sqrt(jnp.sum(x * x, -1, keepdims=True))
            return jnp.concatenate([mean, var, am, l2], -1)

        def _forward(hidden_states, q_w, k_w, v_w, b_w, q_cw, k_cw, v_cw, fir_short_w, fir_long_w, mlp1_w, mlp1_b, mlp2_w, mlp2_b, logit_temp, conv_res_logit, norm_w, o_w):
            b, l, _ = hidden_states.shape
            q_in = _short_conv(hidden_states @ q_w.T, q_cw)
            k_in = _short_conv(hidden_states @ k_w.T, k_cw)
            v_in = _short_conv(hidden_states @ v_w.T, v_cw)
            q = q_in.reshape(b, l, H, DK)
            k = k_in.reshape(b, l, H, DK)
            v_direct = v_in.reshape(b, l, H, DV)
            beta = jnp.maximum(jax.nn.sigmoid(hidden_states @ b_w.T), 1e-06)
            delta_out, _S = _delta_rule_chunkwise(q.transpose(0, 2, 1, 3), k.transpose(0, 2, 1, 3), v_direct.transpose(0, 2, 1, 3), beta.transpose(0, 2, 1))
            delta_out = delta_out.transpose(0, 2, 1, 3)
            local_short = _fir_conv(v_direct, fir_short_w)
            local_long = _fir_conv(v_direct, fir_long_w)
            stats = jnp.concatenate([_per_head_stats(local_short), _per_head_stats(local_long), _per_head_stats(delta_out), _per_head_stats(v_direct)], -1)
            hs_exp = jnp.broadcast_to(hidden_states[:, :, None, :], (b, l, H, hidden_states.shape[-1]))
            gate_in = jnp.concatenate([hs_exp, stats], -1)
            h1 = jax.nn.gelu(gate_in @ mlp1_w.T + mlp1_b)
            logits = h1 @ mlp2_w.T + mlp2_b
            temp = jax.nn.softplus(logit_temp)
            p = jax.nn.softmax(logits / temp, -1)
            p = jnp.maximum(p, PROB_FLOOR)
            p = p / jnp.sum(p, -1, keepdims=True)
            o = p[..., 0:1] * local_short + p[..., 1:2] * local_long + p[..., 2:3] * delta_out + p[..., 3:4] * v_direct
            o = o + jax.nn.sigmoid(conv_res_logit)[None, None, :, None] * local_short
            o = _rmsnorm(o, norm_w)
            o = o.reshape(b, l, H * DV) @ o_w.T
            return o
        return _forward(hidden_states, q_w, k_w, v_w, b_w, q_cw, k_cw, v_cw, fir_short_w, fir_long_w, mlp1_w, mlp1_b, mlp2_w, mlp2_b, logit_temp, conv_res_logit, norm_w, o_w)

    def _L0_attn_b_ref(x, WQ, WK, WV, WO):
        import jax, jax.numpy as jnp
        import numpy as np
        import math
        D_MODEL = 128
        N_HEADS = 16
        THETA = 10000.0
        SEQ = 512
        BATCH = 1
        CLAMP = 100000.0

        def _apply_rope(t, cos, sin):
            te = t[..., 0::2]
            to = t[..., 1::2]
            re = te * cos - to * sin
            ro = te * sin + to * cos
            return jnp.stack([re, ro], axis=-1).reshape(t.shape)
        B, S, D = x.shape
        h = N_HEADS
        d_k = D // h
        q = x @ WQ.T
        k = x @ WK.T
        v = x @ WV.T
        q = q.reshape(B, S, h, d_k).transpose(0, 2, 1, 3)
        k = k.reshape(B, S, h, d_k).transpose(0, 2, 1, 3)
        v = v.reshape(B, S, h, d_k).transpose(0, 2, 1, 3)
        d = d_k // 2
        inv_freq = THETA ** (-jnp.arange(d, dtype=jnp.float32) / d)
        pos = jnp.arange(S, dtype=jnp.float32)
        angles = pos[:, None] * inv_freq[None, :]
        cos = jnp.cos(angles)
        sin = jnp.sin(angles)
        q = _apply_rope(q, cos, sin)
        k = _apply_rope(k, cos, sin)
        scores = jnp.einsum('bhqd,bhkd->bhqk', q, k) / jnp.sqrt(jnp.float32(d_k))
        causal = jnp.tril(jnp.ones((S, S), dtype=bool))[None, None]
        scores = jnp.where(causal, scores, -jnp.inf)
        scores = jnp.clip(scores, -CLAMP, CLAMP)
        attn = jax.nn.softmax(scores, axis=-1)
        out = jnp.einsum('bhqk,bhkd->bhqd', attn, v)
        out = out.transpose(0, 2, 1, 3).reshape(B, S, D)
        return out @ WO.T

    def _L0_ffn_ref(x, w_router, w_gate, w_up, w_down):
        import math
        import jax, jax.numpy as jnp
        import numpy as np
        CAPACITY_FACTOR = 1.25
        B, S, H = x.shape
        E = w_gate.shape[0]
        T = B * S
        C = int(math.ceil(CAPACITY_FACTOR * T / E))
        xt = x.reshape(T, H)
        logits = xt @ w_router
        probs = jax.nn.softmax(logits, axis=-1)
        top1 = jnp.argmax(probs, axis=-1)
        gate = jnp.take_along_axis(probs, top1[:, None], axis=1)[:, 0]
        onehot = jax.nn.one_hot(top1, E, dtype=jnp.int32)
        pos = jnp.cumsum(onehot, axis=0)[jnp.arange(T), top1] - 1
        accepted = pos < C
        slot = jnp.where(accepted, top1 * C + pos, E * C)
        buf = jnp.zeros((E * C + 1, H), dtype=x.dtype).at[slot].set(xt)
        buf = buf[:E * C].reshape(E, C, H)
        g = jnp.einsum('ech,ehf->ecf', buf, w_gate)
        u = jnp.einsum('ech,ehf->ecf', buf, w_up)
        y = jnp.einsum('ecf,efh->ech', jax.nn.silu(g) * u, w_down)
        out_tok = y.reshape(E * C, H)[jnp.clip(slot, 0, E * C - 1)]
        out_tok = jnp.where(accepted[:, None], out_tok * gate[:, None], 0.0)
        return (xt + out_tok).reshape(B, S, H)
    x = L0_attn_a_hidden_states
    x = x + _L0_attn_a_ref(_layernorm(x, axis=-1), L0_attn_a_q_w, L0_attn_a_k_w, L0_attn_a_v_w, L0_attn_a_b_w, L0_attn_a_q_cw, L0_attn_a_k_cw, L0_attn_a_v_cw, L0_attn_a_fir_short_w, L0_attn_a_fir_long_w, L0_attn_a_mlp1_w, L0_attn_a_mlp1_b, L0_attn_a_mlp2_w, L0_attn_a_mlp2_b, L0_attn_a_logit_temp, L0_attn_a_conv_res_logit, L0_attn_a_norm_w, L0_attn_a_o_w)
    x = x + _L0_ffn_ref(_layernorm(x, axis=-1), L0_ffn_w_router, L0_ffn_w_gate, L0_ffn_w_up, L0_ffn_w_down)
    x = x + _L0_attn_b_ref(_layernorm(x, axis=-1), L0_attn_b_WQ, L0_attn_b_WK, L0_attn_b_WV, L0_attn_b_WO)
    x = x + _L0_ffn_ref(_layernorm(x, axis=-1), L0_ffn_w_router, L0_ffn_w_gate, L0_ffn_w_up, L0_ffn_w_down)
    return x

_drawn_inputs = setup_inputs


def setup_inputs(seed=0):
    import zlib

    import numpy as np

    out = dict(_drawn_inputs(seed))
    spreads = {'L0_attn_a_mlp1_b': (0.0, 0.8),
     'L0_attn_a_conv_res_logit': (-2.0, 0.6),
     'L0_attn_a_norm_w': (1.0, 0.2)}
    factors = {'L0_attn_a_q_w': 6.797,
     'L0_attn_a_k_w': 6.753,
     'L0_attn_a_b_w': 8.0,
     'L0_attn_a_q_cw': 7.069,
     'L0_attn_a_k_cw': 6.9,
     'L0_attn_a_fir_short_w': 26.263,
     'L0_attn_a_fir_long_w': 22.81,
     'L0_attn_a_mlp1_w': 8.0,
     'L0_attn_a_mlp2_w': 8.0}
    for name, (base, spread) in spreads.items():
        noise = np.random.default_rng([zlib.crc32(name.encode()), seed]).standard_normal(out[name].shape)
        drawn = base * np.exp(spread * noise) if base else spread * noise
        out[name] = jnp.asarray(drawn.astype(out[name].dtype))
    for name, factor in factors.items():
        out[name] = (out[name] * factor).astype(out[name].dtype)
    return out
```

```python
from contextlib import ExitStack

import numpy as np

import concourse.bass as bass
from concourse import mybir

F32 = mybir.dt.float32
BF16 = mybir.dt.bfloat16
I32 = mybir.dt.int32
ALU = mybir.AluOpType
ACT = mybir.ActivationFunctionType
AX = mybir.AxisListType

P = 128
B, L, D = 8, 512, 128
T = B * L
NT = T // P
TB = L // P
H, DK = 4, 32
C = 32
G = T // C
GB = L // C
TAPS = 4
PROB_FLOOR = 0.02
KL = 64
LN_EPS = 1e-5

RING = 4


class Jobs:

    def __init__(self):
        self.n = 0
        self.named = {}

    def next(self, *name):
        i = self.n
        self.n += 1
        if name:
            self.named[name] = i
        return i

    def done(self, *name):
        return self.named[name] + 1


def rows(dram, cols):
    return dram.rearrange("(t p) d -> p t d", p=P)


def attn_a(nc, sems, s_x, x_in, x_out, w, cst):
    ctx = ExitStack()
    with ctx:
        R = ctx.enter_context(nc.sbuf_tensor("a_regions", [P, 11, 4096], F32))
        xnT = ctx.enter_context(nc.sbuf_tensor("a_xnT", [P, B, L + TAPS - 1], F32))

        def reg(i, n=1):
            return R[:, i:i + n, :].rearrange("p a b -> p (a b)")

        small = lambda name, shape, dt=F32: ctx.enter_context(nc.sbuf_tensor("a_" + name, shape, dt))
        ident = small("ident", [P, P])
        eps = small("eps", [P, 4])
        mv = small("mv", [P, NT, 2])
        rstd = small("rstd", [P, NT])
        beta = small("beta", [P, G])
        wo = small("wo", [P, P])
        masks = small("masks", [P, 3, C])
        wbig = small("wbig", [P, 4, P])
        hdr = small("hdr", [P, 16])

        X = reg(9).rearrange("p (t d) -> p t d", t=NT)
        xn = reg(10).rearrange("p (t d) -> p t d", t=NT)
        stats6 = reg(6)[:, 0:NT * 6].rearrange("p (t s) -> p t s", s=6)
        WC = reg(8)[:, 0:12 * P].rearrange("p (s j c) -> p s j c", s=3, j=TAPS)
        CWB = reg(7)[:, 12 * P:24 * P].rearrange("p (s j c) -> p s j c", s=3, j=TAPS)
        WQKV = reg(7)[:, 24 * P:27 * P].rearrange("p (s c) -> p s c", s=3)
        bwT = reg(7)[:, 27 * P:27 * P + H]
        VT = reg(3)
        VH = reg(4).rearrange("p (g d) -> p g d", d=DK)
        vE = reg(5).rearrange("p (t c) -> p t c", c=P)
        vO = reg(6).rearrange("p (t c) -> p t c", c=P)
        FT = reg(1, 2).rearrange("p (f t c) -> p f t c", f=2, t=NT)
        TR = reg(8)[:, 16 * P:32 * P].rearrange("p (r c f m) -> p r c f m", r=2, c=8, f=2)
        LS = reg(9).rearrange("p (g d) -> p g d", d=DK)
        LLG = reg(10).rearrange("p (g d) -> p g d", d=DK)
        KQ = reg(1, 2).rearrange("p (g s c) -> p g s c", s=2, c=C)
        VK = reg(5, 2).rearrange("p (g s c) -> p g s c", s=2, c=C)
        AK = reg(7, 2).rearrange("p (g s c) -> p g s c", s=2, c=C)
        MS = reg(3).rearrange("p (g c) -> p g c", c=C)
        ME = reg(0).rearrange("p (h r c) -> p h r c", h=H, r=C)
        TI = reg(3).rearrange("p (r h c) -> p h r c", h=H, r=C)
        TIr = reg(3).rearrange("p (r n) -> p r n", r=C)
        TMP = reg(5).rearrange("p (h n) -> p h n", h=H)
        TT = reg(0).rearrange("p (g c) -> p g c", c=C)
        AT = reg(3).rearrange("p (g c) -> p g c", c=C)
        SS = reg(0).rearrange("p (g c) -> p g c", c=C)
        DH = reg(3).rearrange("p (g c) -> p g c", c=C)
        SQ = [reg(6)[:, i * 512:(i + 1) * 512] for i in range(4)]
        RN = [reg(6)[:, (4 + i) * 512:(5 + i) * 512] for i in range(4)]

        w1s = small("w1s", [P, H, P])
        w2p = small("w2p", [P, DK])
        NW = 9 + 3 + 2 * H + 1 + H
        XS = [LS, LLG, DH, VH]
        SQX = [reg(i).rearrange("p (g d) -> p g d", d=DK) for i in (0, 1, 2, 5)]
        ST = reg(6).rearrange("p (g s) -> p g s", s=DK)
        STT = reg(7)
        H1 = [reg(1)[:, i * L:(i + 1) * L] for i in range(8)]
        LG = reg(2).rearrange("p (g s) -> p g s", s=DK)
        OH = reg(0).rearrange("p (g d) -> p g d", d=DK)
        O2 = reg(5).rearrange("p (g d) -> p g d", d=DK)
        OSQ = reg(6).rearrange("p (g d) -> p g d", d=DK)
        OT = reg(7)
        OSCR = reg(7)[:, 3584:4096]
        XR = xnT[:, :, :].rearrange("p b l -> p (b l)")[:, 0:T].rearrange("p (t d) -> p t d", d=D)
        sm = reg(8)
        S1 = sm[:, 0:512].rearrange("p (k g) -> p k g", k=4)
        S2 = sm[:, 512:1024].rearrange("p (k g) -> p k g", k=4)
        MM = sm[:, 1024:1536].rearrange("p (k g) -> p k g", k=4)
        PR = sm[:, 1536:2048].rearrange("p (g k) -> p g k", k=4)
        R1 = sm[:, 2048:2048 + G]
        R2 = sm[:, 2176:2176 + G]
        RG = sm[:, 2304:2304 + G]
        O3 = sm[:, 2560:3072].rearrange("p (g d) -> p g d", d=DK)
        ones_h, w1x, bw, flip = (wbig[:, i, :] for i in range(4))

        banks_a = [ctx.enter_context(nc.psum_tensor(f"a_pa{i}", [P, 512], F32)) for i in range(RING)]
        banks_v = [ctx.enter_context(nc.psum_tensor(f"a_pv{i}", [P, 512], F32)) for i in range(RING)]
        sem = lambda name: sems.enter_context(nc.semaphore("a_" + name))
        pe_a, pe_v = sem("pe_a"), sem("pe_v")
        act_job, dve_job = sem("act_job"), sem("dve_job")
        s_w, s_out = sem("s_w"), sem("s_out")
        s_t = [sem(f"s_t{i}") for i in range(2)]
        s_pad, s_bw, s_wc, s_ln, s_sd, s_rs = (sem(n) for n in ("pad", "bw", "wc", "ln", "sd", "rs"))
        s_vo, s_voz, s_sq, s_nrm, s_kh, s_dve, s_pool, s_beta, s_vk, s_msb, s_el, s_elp, s_tz = (
            sem(n) for n in ("vo", "voz", "sq", "nrm", "kh", "dve", "pool", "beta", "vk", "msb", "el", "elp", "tz"))
        s_beta0, s_beta1, s_scan = (sem(n) for n in ("beta0", "beta1", "scan"))
        s_st, s_sqx, s_l2, s_stt, s_hdr2, s_e, s_ex, s_mix, s_ms, s_rms, s_o, s_oT, s_w1s, s_elim, s_bst, s_p, s_pl, s_o2 = (
            sem(n) for n in ("st", "sqx", "l2", "stt", "hdr2", "e", "ex", "mix", "ms", "rms", "o", "oT", "w1s", "elim", "bst", "p", "pl", "o2"))
        JA, JV = Jobs(), Jobs()
        NSLAB = P // 8

        block = ctx.enter_context(nc.Block())

        def eliminate(eng, hs, chain, last):
            n = hs.stop - hs.start
            eng.wait_ge(act_job, JA.done("me", C // 4 - 1))
            eng.wait_ge(s_tz, 1)
            for j in range(C - 1):
                r, c = C - 1 - j, j + 1
                tmp = TMP[:, hs, 0:r * c].rearrange("p h (r c) -> p h r c", c=c)
                if j:
                    eng.wait_ge(chain, 2 * j)
                eng.tensor_tensor(tmp, ME[:, hs, j + 1:C, j:j + 1].to_broadcast([P, n, r, c]),
                                  TI[:, hs, j:j + 1, 0:c].to_broadcast([P, n, r, c]), ALU.mult).then_inc(chain, 1)
                eng.wait_ge(chain, 2 * j + 1)
                ins = eng.tensor_tensor(TI[:, hs, j + 1:C, 0:c], TI[:, hs, j + 1:C, 0:c], tmp, ALU.add)
                if j < C - 2:
                    ins.then_inc(chain, 1)
            ins.then_inc(last, 1)

        def gate_pe(pe, bank_a, bank_v):
            def logits(b):
                bank = bank_v("lg", b)
                pe.wait_ge(act_job, JA.done("h1", b, H - 1))
                for h in range(H):
                    mm = pe.matmul(bank[DK * h:DK * h + DK, :], w2p[:, :], H1[(b * H + h) % 8], start=True, stop=True)
                mm.then_inc(pe_v, 1)

            for b in range(B):
                for h in range(H):
                    bank = bank_a("h1", b, h)
                    if h == 0:
                        pe.wait_ge(s_stt, b + 1)
                    pe.matmul(bank[:, :], w1x, xnT[:, b, TAPS - 1:], start=True, stop=False)
                    pe.matmul(bank[:, :], w1s[:, h, :], STT[:, b * L:(b + 1) * L], start=False, stop=True).then_inc(pe_a, 1)
                if b:
                    logits(b - 1)
            logits(B - 1)
            for b in range(B):
                bank = bank_v("o", b)
                pe.wait_ge(s_oT, b + 1)
                for j in range(TB):
                    t = b * TB + j
                    mm = pe.matmul(bank[:, j * P:(j + 1) * P], OT[:, t * P:(t + 1) * P], wo[:, :], start=True, stop=True)
                mm.then_inc(pe_v, 1)

        def gate_act(act, bank, copy):
            act.wait_ge(act_job, JA.done("dh", B - 1))
            for k in range(4):
                act.activation(SQX[k], XS[k], ACT.Square).then_inc(s_sqx, 1)
            act.wait_ge(s_st, 1)
            for k in range(4):
                act.activation(ST[:, :, 4 * k + 3], S2[:, k, :], ACT.Sqrt).then_inc(s_l2, 1)
            act.activation(hdr[:, 8:9], hdr[:, 4:5], ACT.Abs).then_inc(s_hdr2, 1)
            act.wait_ge(s_hdr2, 1)
            act.activation(hdr[:, 8:9], hdr[:, 8:9], ACT.Exp, scale=-1.0).then_inc(s_hdr2, 1)
            act.wait_ge(s_hdr2, 2)
            act.activation(hdr[:, 8:9], hdr[:, 8:9], ACT.Ln, bias=eps[:, 2:3]).then_inc(s_hdr2, 1)
            act.activation(hdr[:, 9:10], hdr[:, 5:6], ACT.Sigmoid).then_inc(s_hdr2, 1)
            for b in range(B):
                for h in range(H):
                    if b >= 2 and h == 0:
                        act.wait_ge(pe_v, JV.done("lg", b - 2))
                    act.activation(H1[(b * H + h) % 8], bank("h1", b, h)[:, :], ACT.Gelu_apprx_tanh,
                                   bias=hdr[:, 7:8]).then_inc(act_job, 1)
            act.wait_ge(s_e, 1)
            act.activation(PR, PR, ACT.Exp, scale=hdr[:, 10:11]).then_inc(s_ex, 1)
            for b in range(B):
                gs = slice(b * GB, b * GB + GB)
                act.wait_ge(s_mix, b + 1)
                act.activation(OSQ[:, gs, :], OH[:, gs, :], ACT.Square).then_inc(s_o, 1)
            act.wait_ge(s_ms, 1)
            act.activation(R1, R1, ACT.Sqrt, bias=eps[:, 0:1], scale=1.0 / DK).then_inc(s_rms, 1)

        def gate_pool(pool):
            pool.wait_ge(act_job, JA.done("dh", B - 1))
            pool.memset(ST, 0.0).then_inc(s_bst, 1)
            pool.wait_ge(s_p, 1)
            for b in range(B):
                gs = slice(b * GB, b * GB + GB)
                if b:
                    pool.wait_ge(s_o2, b)
                pool.tensor_tensor(O2[:, gs, :], XS[1][:, gs, :], PR[:, gs, 1:2].to_broadcast([P, GB, DK]), ALU.mult).then_inc(s_pl, 1)
                pool.tensor_tensor(O3, XS[3][:, gs, :], PR[:, gs, 3:4].to_broadcast([P, GB, DK]), ALU.mult).then_inc(s_pl, 1)
                pool.wait_ge(s_pl, 2 * b + 2)
                pool.tensor_tensor(O2[:, gs, :], O2[:, gs, :], O3, ALU.add).then_inc(s_o2, 1)

        @block.tensor
        def _(pe):
            def bank_a(*name):
                i = JA.next(*name)
                if i >= RING:
                    pe.wait_ge(act_job, i - RING + 1)
                return banks_a[i % RING]

            def bank_v(*name):
                i = JV.next(*name)
                if i >= RING:
                    pe.wait_ge(dve_job, i - RING + 1)
                return banks_v[i % RING]

            pe.wait_ge(s_w, 16 * NW)
            for b in range(B):
                bank = bank_a("xnT", b)
                for j in range(TB):
                    pe.wait_ge(s_ln, b * TB + j + 1)
                    mm = pe.transpose(bank[:, j * P:(j + 1) * P], xn[:, b * TB + j, :], ident[:, :])
                mm.then_inc(pe_a, 1)
            pe.wait_ge(s_wc, 2)
            pe.wait_ge(s_pad, 3)
            for b in range(B):
                bank = bank_a("v", b)
                pe.wait_ge(act_job, JA.done("xnT", b))
                for j in range(TAPS):
                    mm = pe.matmul(bank[:, :], WC[:, 2, j, :], xnT[:, b, j:j + L], start=j == 0, stop=j == TAPS - 1)
                mm.then_inc(pe_a, 1)
            pe.wait_ge(s_bw, 1)
            for b in range(B):
                bank = bank_v("beta", b)
                pe.matmul(bank[:, :], bw, xnT[:, b, TAPS - 1:], start=True, stop=True).then_inc(pe_v, 1)
            for b in range(B):
                bank = bank_a("vE", b)
                pe.wait_ge(act_job, JA.done("v", b))
                for j in range(TB):
                    t = b * TB + j
                    mm = pe.transpose(bank[:, j * P:(j + 1) * P], VT[:, t * P:(t + 1) * P], ident[:, :])
                mm.then_inc(pe_a, 1)
            pe.wait_ge(s_voz, 1)
            pe.wait_ge(s_vo, 32)
            for s in range(NSLAB):
                bank = bank_a("fir", s)
                pe.wait_ge(s_t[s % 2], 16 * (s // 2 + 1))
                for c in range(8):
                    for f in range(2):
                        for par in range(2):
                            mm = pe.matmul(bank[64 * par:64 * par + 64, (2 * c + f) * NT:(2 * c + f + 1) * NT],
                                           TR[:, s % 2, c, f, :], (vO, vE)[par][:, :, 8 * s + c],
                                           start=True, stop=True)
                mm.then_inc(pe_a, 1)
            pe.wait_ge(act_job, JA.done("fir", NSLAB - 1))
            for f in range(2):
                for b in range(B):
                    bank = bank_v("firT", f, b)
                    for j in range(TB):
                        mm = pe.transpose(bank[:, j * P:(j + 1) * P], FT[:, f, b * TB + j, :], flip)
                    mm.then_inc(pe_v, 1)
            for b in range(B):
                for s in range(2):
                    bank = bank_a("kq", s, b)
                    for j in range(TAPS):
                        mm = pe.matmul(bank[:, :], WC[:, 1 - s, j, :], xnT[:, b, j:j + L], start=j == 0, stop=j == TAPS - 1)
                    mm.then_inc(pe_a, 1)
            for b in range(B):
                for s in range(2):
                    bank = bank_a("ss", s, b)
                    pe.wait_ge(s_sq, 2 * b + s + 1)
                    pe.matmul(bank[:, :], ones_h, SQ[(2 * b + s) % 4], start=True, stop=True).then_inc(pe_a, 1)
            for q in range(G // 8):
                bank = bank_v("kk", q)
                pe.wait_ge(s_nrm, 2 * (q // 2 + 1))
                for g in range(8 * q, 8 * q + 8):
                    for h in range(H):
                        e = slice(DK * h, DK * h + DK)
                        mm = pe.matmul(bank[e, (g % 8) * 64:(g % 8) * 64 + 64], KQ[e, g, 0, :],
                                       KQ[e, g, :, :].rearrange("p s c -> p (s c)"), start=True, stop=True)
                mm.then_inc(pe_v, 1)
            pe.wait_ge(s_msb, B)
            for q in range(C // 4):
                bank = bank_a("me", q)
                for j in range(4):
                    mm = pe.transpose(bank[:, j * P:(j + 1) * P], MS[:, :, 4 * q + j], ident[:, :])
                mm.then_inc(pe_a, 1)
            pe.wait_ge(s_el, 1)
            pe.wait_ge(s_elp, 1)
            for q in range(C // 4):
                bank = bank_a("tt", q)
                for j in range(4):
                    mm = pe.transpose(bank[:, j * P:(j + 1) * P], TIr[:, 4 * q + j, :], ident[:, :])
                mm.then_inc(pe_a, 1)
            pe.wait_ge(act_job, JA.done("tt", C // 4 - 1))
            for q in range(G // 8):
                bank = bank_a("uw", q)
                pe.wait_ge(s_vk, q // 2 + 1)
                for g in range(8 * q, 8 * q + 8):
                    for h in range(H):
                        e = slice(DK * h, DK * h + DK)
                        mm = pe.matmul(bank[e, (g % 8) * 64:(g % 8) * 64 + 64], TT[e, g, :],
                                       VK[e, g, :, :].rearrange("p s c -> p (s c)"), start=True, stop=True)
                mm.then_inc(pe_a, 1)
            for q in range(G // 8):
                pe.wait_ge(act_job, JA.done("uw", q))
                bank = bank_v("qa", q)
                for g in range(8 * q, 8 * q + 8):
                    for h in range(H):
                        e = slice(DK * h, DK * h + DK)
                        mm = pe.matmul(bank[e, (g % 8) * 64:(g % 8) * 64 + 64], VK[e, g, 1, :],
                                       AK[e, g, :, :].rearrange("p s c -> p (s c)"), start=True, stop=True)
                mm.then_inc(pe_v, 1)
                if q % 2 == 1:
                    bank = bank_a("ku", q // 2)
                    for g in range(8 * q - 8, 8 * q + 8):
                        for h in range(H):
                            e = slice(DK * h, DK * h + DK)
                            mm = pe.matmul(bank[e, (g % 16) * C:(g % 16 + 1) * C], AK[e, g, 1, :], VK[e, g, 0, :],
                                           start=True, stop=True)
                    mm.then_inc(pe_a, 1)
            pe.wait_ge(dve_job, JV.done("qa", G // 8 - 1))
            for i in range(1, GB - 1):
                bank = bank_v("scan", i)
                if i == 1:
                    pe.wait_ge(s_scan, 1)
                else:
                    pe.wait_ge(dve_job, JV.done("scan", i - 1))
                for b in range(B):
                    for h in range(H):
                        e = slice(DK * h, DK * h + DK)
                        mm = pe.matmul(bank[e, b * C:(b + 1) * C], AT[e, b * GB + i, :], SS[e, b * GB + i, :],
                                       start=True, stop=True)
                mm.then_inc(pe_v, 1)
            pe.wait_ge(dve_job, JV.done("scan", GB - 2))
            for b in range(B):
                bank = bank_a("dh", b)
                for i in range(GB):
                    g = b * GB + i
                    for h in range(H):
                        e = slice(DK * h, DK * h + DK)
                        o = bank[e, i * C:(i + 1) * C]
                        if i:
                            pe.matmul(o, KQ[e, g, 1, :], SS[e, g, :], start=True, stop=False)
                        mm = pe.matmul(o, AK[e, g, 0, :], VK[e, g, 0, :], start=i == 0, stop=True)
                mm.then_inc(pe_a, 1)
            gate_pe(pe, bank_a, bank_v)

        @block.sync
        def _(sp):
            xr = rows(x_in, D)
            for i in range(B):
                sp.dma_start(X[:, i * TB:(i + 1) * TB, :], xr[:, i * TB:(i + 1) * TB, :]).then_inc(s_x[i], 16)
            sp.dma_start(ident[:, :], cst["ident"]).then_inc(s_w, 16)
            sp.dma_start(ones_h, cst["ones_h"]).then_inc(s_w, 16)
            sp.dma_start(flip, cst["flip"]).then_inc(s_w, 16)
            sp.dma_start(masks[:, :, :], cst["masks"]).then_inc(s_w, 16)
            sp.dma_start(WQKV, w["qkvT"]).then_inc(s_w, 16)
            sp.dma_start(CWB.rearrange("p s j c -> p (s j c)"),
                         bass.AP(tensor=w["cw"].tensor, offset=0, ap=[[0, P], [1, 12 * P]])).then_inc(s_w, 16)
            sp.dma_start(bwT, w["bT"]).then_inc(s_w, 16)
            sp.dma_start(w1x, w["w1xT"]).then_inc(s_w, 16)
            sp.dma_start(wo[:, :], w["oT"]).then_inc(s_w, 16)
            sp.dma_start(w2p[:, 0:4], w["w2T"]).then_inc(s_w, 16)
            sp.dma_start(hdr[:, 0:4], bass.AP(tensor=w["b2"].tensor, offset=0, ap=[[0, P], [1, 4]])).then_inc(s_w, 16)
            sp.dma_start(hdr[:, 4:5], bass.AP(tensor=w["temp"].tensor, offset=0, ap=[[0, P], [1, 1]])).then_inc(s_w, 16)
            for h in range(H):
                e = slice(DK * h, DK * h + DK)
                sp.dma_start(hdr[e, 5:6], bass.AP(tensor=w["res"].tensor, offset=h, ap=[[0, DK], [1, 1]])).then_inc(s_w, 16)
                sp.dma_start(hdr[e, 6:7], w["norm"]).then_inc(s_w, 16)
            sp.dma_start(hdr[:, 7:8], w["b1"]).then_inc(s_w, 16)
            sp.wait_ge(s_w1s, 1)
            for h in range(H):
                sp.dma_start(w1s[DK * h:DK * h + 16, h, :], w["w1sT"]).then_inc(s_w, 16)
            for s in range(NSLAB):
                if s >= 2:
                    sp.wait_ge(pe_a, JA.done("fir", s - 2))
                src = bass.AP(tensor=w["fir"].tensor, offset=8 * s * 2 * 192,
                              ap=[[1, P], [192, 16], [1, 64]])
                sp.dma_start(TR[:, s % 2, :, :, :].rearrange("p c f m -> p (c f) m"), src).then_inc(s_t[s % 2], 16)
            sp.wait_ge(pe_v, JV.done("lg", B - 1))
            for b in range(B):
                sp.dma_start(XR[:, b * TB:(b + 1) * TB, :], xr[:, b * TB:(b + 1) * TB, :]).then_inc(s_x[b], 16)
            xo = rows(x_out, D)
            for b in range(B):
                sp.wait_ge(dve_job, JV.done("o", b))
                sp.dma_start(xo[:, b * TB:(b + 1) * TB, :], XR[:, b * TB:(b + 1) * TB, :]).then_inc(s_out, 16)
            sp.wait_ge(s_out, 16 * B)

        @block.gpsimd
        def _(pool):
            pool.memset(eps[:, 0:1], LN_EPS)
            pool.memset(eps[:, 1:2], 1e-6)
            pool.memset(eps[:, 2:3], 1.0)
            pool.memset(w2p[:, 4:], 0.0).then_inc(s_pad, 1)
            pool.memset(w1s[:, :, :], 0.0).then_inc(s_w1s, 1)
            pool.memset(xnT[:, :, 0:TAPS - 1], 0.0).then_inc(s_pad, 2)
            pool.wait_ge(s_w, 16 * NW)
            for s in range(3):
                for j in range(TAPS):
                    ins = pool.tensor_tensor(WC[:, s, j, :], WQKV[:, s, :], CWB[:, s, j, :], ALU.mult)
            ins.then_inc(s_wc, 2)
            pool.wait_ge(s_sd, 1)
            pool.memset(vO[0:64, :, :].rearrange("p (b j) c -> p b j c", j=TB)[:, :, 0, :], 0.0).then_inc(s_voz, 1)
            pool.wait_ge(act_job, JA.done("vE", B - 1))
            pool.dma_start(vO[64:128, :, :], vE[0:64, :, :]).then_inc(s_vo, 16)
            pool.dma_start(vO[0:64, :, :].rearrange("p (b j) c -> p b j c", j=TB)[:, :, 1:, :],
                           vE[64:128, :, :].rearrange("p (b j) c -> p b j c", j=TB)[:, :, 0:TB - 1, :]).then_inc(s_vo, 16)
            pool.wait_ge(s_beta, 1)
            for b in range(B):
                gs = slice(b * GB, b * GB + GB)
                pool.wait_ge(dve_job, JV.done("kk", 2 * b + 1))
                pool.tensor_tensor(MS[:, gs, :], MS[:, gs, :], beta[:, gs].to_broadcast([P, GB, C]),
                                   ALU.mult).then_inc(s_msb, 1)
            eliminate(pool, slice(3, 4), s_pool, s_elp)
            pool.wait_ge(s_el, 1)
            pool.wait_ge(s_elp, 1)
            for b in range(B):
                gs = slice(b * GB, b * GB + GB)
                pool.wait_ge(s_kh, b + 1)
                pool.tensor_tensor(VK[:, gs, 0, :], VH[:, gs, :], beta[:, gs].to_broadcast([P, GB, C]), ALU.mult)
                pool.tensor_tensor(VK[:, gs, 1, :], AK[:, gs, 1, :], beta[:, gs].to_broadcast([P, GB, C]),
                                   ALU.mult).then_inc(s_vk, 1)
            gate_pool(pool)

        @block.scalar
        def _(act):
            jobs = Jobs()

            def bank(name, *rest):
                i = jobs.next()
                assert JA.named[(name, *rest)] == i, (name, rest)
                act.wait_ge(pe_a, i + 1)
                return banks_a[i % RING]

            def copy(out, in_):
                return act.activation(out, in_, ACT.Copy)

            act.wait_ge(s_pad, 3)
            act.wait_ge(s_sd, 1)
            act.activation(rstd[:, :], mv[:, :, 1], ACT.Sqrt, bias=eps[:, 0:1]).then_inc(s_rs, 1)
            for b in range(B):
                copy(xnT[:, b, TAPS - 1:], bank("xnT", b)[:, :]).then_inc(act_job, 1)
            for b in range(B):
                act.activation(VT[:, b * L:(b + 1) * L], bank("v", b)[:, :], ACT.Silu).then_inc(act_job, 1)
            for b in range(B):
                copy(vE[:, b * TB:(b + 1) * TB, :].rearrange("p t c -> p (t c)"), bank("vE", b)[:, :]).then_inc(act_job, 1)
            for s in range(NSLAB):
                src = bank("fir", s)[:, :].rearrange("p (c f t) -> p c f t", c=8, f=2)
                for f in range(2):
                    ins = copy(FT[:, f, :, 8 * s:8 * s + 8].rearrange("p t c -> p c t"), src[:, :, f, :])
                ins.then_inc(act_job, 1)
            act.wait_ge(s_beta0, 1)
            act.activation(beta[:, :], beta[:, :], ACT.Sigmoid).then_inc(s_beta1, 1)
            act.wait_ge(pe_v, JV.done("firT", 1, B - 1))
            for b in range(B):
                for s in range(2):
                    act.activation(KQ[:, b * GB:(b + 1) * GB, s, :],
                                   bank("kq", s, b)[:, :].rearrange("p (g c) -> p g c", c=C), ACT.Silu).then_inc(act_job, 1)

            def square(n):
                b, s = n // 2, n % 2
                if n == 0:
                    act.wait_ge(pe_a, JA.done("fir", NSLAB - 1))
                if n >= 4:
                    act.wait_ge(pe_a, JA.done("ss", (n - 4) % 2, (n - 4) // 2))
                act.wait_ge(act_job, JA.done("kq", s, b))
                act.activation(SQ[n % 4].rearrange("p (g c) -> p g c", c=C), KQ[:, b * GB:(b + 1) * GB, s, :],
                               ACT.Square).then_inc(s_sq, 1)

            square(0)
            square(1)
            for n in range(2 * B):
                if n + 2 < 2 * B:
                    square(n + 2)
                if n >= 4:
                    act.wait_ge(s_nrm, n - 3)
                act.activation(RN[n % 4], bank("ss", n % 2, n // 2)[:, :], ACT.Sqrt, bias=eps[:, 1:2]).then_inc(act_job, 1)
            for q in range(C // 4):
                copy(ME.rearrange("p h r c -> p (h r) c")[:, :, 4 * q:4 * q + 4].rearrange("p n c -> p c n"),
                     bank("me", q)[:, :].rearrange("p (c n) -> p c n", c=4)).then_inc(act_job, 1)
            for q in range(C // 4):
                copy(TT[:, :, 4 * q:4 * q + 4].rearrange("p g r -> p r g"),
                     bank("tt", q)[:, :].rearrange("p (r g) -> p r g", r=4)).then_inc(act_job, 1)
            def ku(b):
                copy(KQ[:, b * GB:(b + 1) * GB, 0, :], bank("ku", b)[:, :].rearrange("p (g c) -> p g c", c=C)).then_inc(act_job, 1)
            for q in range(G // 8):
                copy(VK[:, 8 * q:8 * q + 8, :, :].rearrange("p g s c -> p (g s c)"), bank("uw", q)[:, :]).then_inc(act_job, 1)
            for b in range(B):
                ku(b)
            act.wait_ge(pe_v, JV.done("scan", GB - 2))
            for b in range(B):
                copy(DH[:, b * GB:(b + 1) * GB, :].rearrange("p g c -> p (g c)"), bank("dh", b)[:, :]).then_inc(act_job, 1)
            gate_act(act, bank, copy)

        @block.vector
        def _(dve):
            jobs = Jobs()
            link_n = [0]

            def link(ins):
                link_n[0] += 1
                ins.then_inc(s_dve, 1)
                dve.wait_ge(s_dve, link_n[0])

            def bank(name, *rest):
                i = jobs.next()
                assert JV.named[(name, *rest)] == i, (name, rest)
                dve.wait_ge(pe_v, i + 1)
                return banks_v[i % RING]

            bc = lambda ap, n=GB: ap.to_broadcast([P, n, C])
            for b in range(B):
                dve.wait_ge(s_x[b], 16)
                for t in range(b * TB, b * TB + TB):
                    ins = dve.bn_stats(stats6[:, t, :], X[:, t, :])
                link(ins)
                for t in range(b * TB, b * TB + TB):
                    ins = dve.bn_aggr(mv[:, t, :], stats6[:, t, :])
            ins.then_inc(s_sd, 1)
            dve.wait_ge(s_rs, 1)
            link(dve.reciprocal(rstd[:, :], rstd[:, :]))
            for t in range(NT):
                dve.tensor_scalar(xn[:, t, :], X[:, t, :], mv[:, t, 0:1], rstd[:, t:t + 1], ALU.subtract, ALU.mult).then_inc(s_ln, 1)
            dve.wait_ge(s_w, 16 * NW)
            dve.tensor_copy(bw.rearrange("p (h r) -> p h r", h=H), bwT.to_broadcast([P, H, DK])).then_inc(s_bw, 1)
            for b in range(B):
                if b:
                    dve.wait_ge(dve_job, JV.done("beta", b - 1))
                link(dve.transpose(OSCR, bank("beta", b)[:, :]))
                dve.tensor_copy(beta[:, b * GB:(b + 1) * GB], OSCR.rearrange("p (g c) -> p g c", c=C)[:, :, 0]).then_inc(dve_job, 1)
            dve.wait_ge(dve_job, JV.done("beta", B - 1))
            dve.tensor_copy(beta[:, :], beta[:, :]).then_inc(s_beta0, 1)
            for b in range(B):
                dve.wait_ge(act_job, JA.done("v", b))
                dve.transpose(VH[:, b * GB:(b + 1) * GB, :].rearrange("p g d -> p (g d)"), VT[:, b * L:(b + 1) * L])
            dve.wait_ge(s_beta1, 1)
            dve.tensor_scalar(beta[:, :], beta[:, :], 1e-6, None, ALU.max).then_inc(s_beta, 1)
            for f in range(2):
                for b in range(B):
                    dve.transpose((LLG, LS)[f][:, b * GB:(b + 1) * GB, :].rearrange("p g d -> p (g d)"),
                                  bank("firT", f, b)[:, :]).then_inc(dve_job, 1)
            for n in range(2 * B):
                b, s = n // 2, n % 2
                gs = slice(b * GB, b * GB + GB)
                dve.wait_ge(act_job, JA.done("ss", s, b))
                link(dve.reciprocal(RN[n % 4], RN[n % 4]))
                dve.tensor_tensor(KQ[:, gs, s, :], KQ[:, gs, s, :], RN[n % 4].rearrange("p (g c) -> p g c", c=C),
                                  ALU.mult).then_inc(s_nrm, 1)
                if s == 0:
                    dve.wait_ge(s_nrm, n + 1)
                    dve.transpose(AK[:, gs, 1, :], KQ[:, gs, 0, :]).then_inc(s_kh, 1)
            for q in range(G // 8):
                gs = slice(8 * q, 8 * q + 8)
                kk = bank("kk", q)[:, :].rearrange("p (g s c) -> p g s c", g=8, s=2)
                dve.tensor_tensor(MS[:, gs, :], kk[:, :, 0, :], masks[:, 0:1, :].to_broadcast([P, 8, C]), ALU.mult)
                dve.tensor_tensor(AK[:, gs, 0, :], kk[:, :, 1, :], masks[:, 1:2, :].to_broadcast([P, 8, C]), ALU.mult).then_inc(dve_job, 1)
            dve.wait_ge(pe_a, JA.done("me", C // 4 - 1))
            link(dve.memset(reg(3), 0.0))
            for h in range(H):
                ins = dve.memset(reg(3)[:, h * C:h * C + (C - 1) * (P + 1) + 1:P + 1], 1.0)
            ins.then_inc(s_tz, 1)
            eliminate(dve, slice(0, 3), s_elim, s_el)
            for q in range(G // 8):
                gs = slice(8 * q, 8 * q + 8)
                qa = bank("qa", q)[:, :].rearrange("p (g s c) -> p g s c", g=8, s=2)
                dve.tensor_tensor(KQ[:, gs, 1, :], KQ[:, gs, 1, :], qa[:, :, 0, :], ALU.subtract)
                dve.tensor_tensor(AT[:, gs, :], masks[:, 2:3, :].to_broadcast([P, 8, C]), qa[:, :, 1, :], ALU.subtract).then_inc(dve_job, 1)
            S4 = SS.rearrange("p (b i) c -> p i b c", b=B)
            B4 = KQ[:, :, 0, :].rearrange("p (b i) c -> p i b c", b=B)
            dve.wait_ge(act_job, JA.done("ku", B - 1))
            dve.tensor_copy(S4[:, 1], B4[:, 0]).then_inc(s_scan, 1)
            for i in range(1, GB - 1):
                ps = bank("scan", i)[:, 0:B * C].rearrange("p (b c) -> p b c", c=C)
                dve.tensor_tensor(S4[:, i + 1], ps, B4[:, i], ALU.add).then_inc(dve_job, 1)
            STk = ST[:, :, 0:16].rearrange("p g (k s) -> p s k g", s=4)
            dve.wait_ge(s_bst, 1)
            dve.wait_ge(act_job, JA.done("dh", B - 1))
            for k in range(4):
                dve.tensor_reduce(S1[:, k, :], XS[k], AX.X, ALU.add)
                dve.tensor_reduce(MM[:, k, :], XS[k], AX.X, ALU.add, apply_absolute_value=True)
                dve.wait_ge(s_sqx, k + 1)
                ins = dve.tensor_reduce(S2[:, k, :], SQX[k], AX.X, ALU.add)
            ins.then_inc(s_st, 1)
            dve.wait_ge(s_st, 1)
            dve.tensor_scalar(STk[:, 0], S1, 1.0 / DK, None, ALU.mult)
            link(dve.tensor_scalar(STk[:, 2], MM, 1.0 / DK, None, ALU.mult))
            link(dve.tensor_tensor(MM, STk[:, 0], STk[:, 0], ALU.mult))
            dve.wait_ge(s_l2, 4)
            link(dve.scalar_tensor_tensor(STk[:, 1], S2, 1.0 / DK, MM, ALU.mult, ALU.subtract))
            for b in range(B):
                dve.transpose(STT[:, b * L:(b + 1) * L], ST[:, b * GB:(b + 1) * GB, :].rearrange("p g s -> p (g s)")).then_inc(s_stt, 1)
            dve.wait_ge(s_hdr2, 4)
            link(dve.tensor_scalar(hdr[:, 10:11], hdr[:, 4:5], 0.0, hdr[:, 8:9], ALU.max, ALU.add))
            dve.reciprocal(hdr[:, 10:11], hdr[:, 10:11])
            dve.tensor_scalar(wo[:, :], wo[:, :], hdr[:, 6:7], None, ALU.mult)
            for b in range(B):
                gs = slice(b * GB, b * GB + GB)
                dve.transpose(LG[:, gs, :].rearrange("p g s -> p (g s)"), bank("lg", b)[:, :]).then_inc(dve_job, 1)
                dve.wait_ge(dve_job, JV.done("lg", b))
                link(dve.tensor_tensor(PR[:, gs, :], LG[:, gs, 0:4], hdr[:, None, 0:4].to_broadcast([P, GB, 4]), ALU.add))
            link(dve.tensor_reduce(R1, PR, AX.X, ALU.max))
            dve.tensor_tensor(PR, PR, R1.to_broadcast([P, G, 4]), ALU.subtract).then_inc(s_e, 1)
            dve.wait_ge(s_ex, 1)
            for again in range(2):
                link(dve.tensor_reduce(R1, PR, AX.X, ALU.add))
                link(dve.reciprocal(R2, R1))
                link(dve.tensor_tensor(PR, PR, R2.to_broadcast([P, G, 4]), ALU.mult))
                if not again:
                    link(dve.tensor_scalar(PR, PR, PROB_FLOOR, None, ALU.max))
            dve.tensor_scalar(PR[:, :, 0], PR[:, :, 0], hdr[:, 9:10], None, ALU.add).then_inc(s_p, 1)
            dve.wait_ge(s_p, 1)
            for b in range(B):
                gs = slice(b * GB, b * GB + GB)
                dve.tensor_tensor(OH[:, gs, :], XS[0][:, gs, :], bc(PR[:, gs, 0:1]), ALU.mult)
                link(dve.tensor_tensor(LG[:, gs, :], XS[2][:, gs, :], bc(PR[:, gs, 2:3]), ALU.mult))
                link(dve.tensor_tensor(OH[:, gs, :], OH[:, gs, :], LG[:, gs, :], ALU.add))
                dve.wait_ge(s_o2, b + 1)
                dve.tensor_tensor(OH[:, gs, :], OH[:, gs, :], O2[:, gs, :], ALU.add).then_inc(s_mix, 1)
            for b in range(B):
                gs = slice(b * GB, b * GB + GB)
                dve.wait_ge(s_o, b + 1)
                ins = dve.tensor_reduce(R1[:, gs], OSQ[:, gs, :], AX.X, ALU.add)
            ins.then_inc(s_ms, 1)
            dve.wait_ge(s_rms, 1)
            link(dve.reciprocal(R2, R1))
            for b in range(B):
                gs = slice(b * GB, b * GB + GB)
                link(dve.tensor_tensor(OH[:, gs, :], OH[:, gs, :], bc(R2[:, gs]), ALU.mult))
                dve.transpose(OT[:, b * L:(b + 1) * L], OH[:, gs, :].rearrange("p g d -> p (g d)")).then_inc(s_oT, 1)
            for b in range(B):
                dve.wait_ge(s_x[b], 32)
                xb = XR[:, b * TB:(b + 1) * TB, :].rearrange("p t d -> p (t d)")
                dve.tensor_tensor(xb, xb, bank("o", b)[:, :], ALU.add).then_inc(dve_job, 1)


E_ = 32
F = 128
CAP = -(-T * 5 // (4 * E_))
SLOTS = E_ * CAP
CH = 4
CT = CH * CAP // P


def moe(nc, sems, s_x, x0, x_in, x_out, w, cst, xbuf, ybuf, tag, first):
    ctx = ExitStack()
    with ctx:
        sb = lambda name, shape, dt=F32: ctx.enter_context(nc.sbuf_tensor(f"{tag}_{name}", shape, dt))
        sem = lambda name: sems.enter_context(nc.semaphore(f"{tag}_{name}"))
        X, XT = sb("X", [P, NT, D]), sb("XT", [P, NT, D])
        tr = sb("tr", [P, SLOTS])
        wg, wu, wd = (sb(n, [P, E_, F]) for n in ("wg", "wu", "wd"))
        BR = sb("BR", [P, SLOTS // P, D])
        YA, YB = sb("YA", [P, E_, D]), sb("YB", [CAP - P, E_, D])
        GY = BR[:, 0:NT, :]
        wr, ident, eps = sb("wr", [P, E_]), sb("ident", [P, P]), sb("eps", [P, 1])
        tri, ones = sb("tri", [P, P], BF16), sb("ones", [P, P], BF16)
        trif = sb("trif", [P, P])
        mv, stats6, rstd = sb("mv", [P, NT, 2]), sb("stats6", [P, NT, 6]), sb("rstd", [P, NT])
        rank, dump = sb("rank", [P, E_]), sb("dump", [P, NT])
        LG, EX = sb("LG", [P, NT, E_]), sb("EX", [P, NT, E_])
        OH, PO = sb("OH", [P, NT, E_], BF16), sb("PO", [P, NT, E_], BF16)
        row = sb("row", [P, 8, NT])
        mx, best, pos, slot, acc, gate, sidx, gidx = (row[:, i, :] for i in range(8))
        si, gi = sb("si", [P, NT], I32), sb("gi", [P, NT], I32)
        SG, hT = sb("SG", [P, 2, CAP]), sb("hT", [P, 4, CAP])
        zero = sb("zero", [P, 1280])
        banks_a = [ctx.enter_context(nc.psum_tensor(f"{tag}_pa{i}", [P, 512], F32)) for i in range(RING)]
        banks_v = [ctx.enter_context(nc.psum_tensor(f"{tag}_pv{i}", [P, 512], F32)) for i in range(RING)]
        pe_a, pe_v, act_job, dve_job = (sem(n) for n in ("pe_a", "pe_v", "act_job", "dve_job"))
        s_gy = [sem(f"gy{b}") for b in range(B)]
        s_c, s_w, s_z, s_zf, s_sd, s_rs, s_ln, s_dve, s_bf, s_lg, s_ex, s_oh, s_idx, s_sc, s_sg, s_y, s_xs, s_out = (
            sem(n) for n in ("c", "w", "z", "zf", "sd", "rs", "ln", "dve", "bf", "lg", "ex", "oh", "idx", "sc", "sg", "y", "xs", "out"))
        JA, JV = Jobs(), Jobs()
        block = ctx.enter_context(nc.Block())

        @block.tensor
        def _(pe):
            def bank_a(*name):
                i = JA.next(*name)
                if i >= RING:
                    pe.wait_ge(act_job, i - RING + 1)
                return banks_a[i % RING]

            def bank_v(*name):
                i = JV.next(*name)
                if i >= RING:
                    pe.wait_ge(dve_job, i - RING + 1)
                return banks_v[i % RING]

            pe.wait_ge(s_c, 16 * 5)
            for b in range(B):
                bank = bank_a("xT", b)
                for j in range(TB):
                    pe.wait_ge(s_ln, b * TB + j + 1)
                    mm = pe.transpose(bank[:, j * P:(j + 1) * P], XT[:, b * TB + j, :], ident[:, :])
                mm.then_inc(pe_a, 1)
            for k in range(2):
                bank = bank_v("lg", k)
                for t in range(16 * k, 16 * k + 16):
                    if t % TB == 0:
                        pe.wait_ge(act_job, JA.done("xT", t // TB))
                    mm = pe.matmul(bank[:, (t % 16) * E_:(t % 16 + 1) * E_], tr[:, t * P:(t + 1) * P], wr[:, :], start=True, stop=True)
                mm.then_inc(pe_v, 1)
            pe.wait_ge(s_oh, 1)
            pe.wait_ge(s_bf, 2)
            for k in range(2):
                bank = bank_v("pos", k)
                ts = slice(16 * k, 16 * k + 16)
                pe.matmul(bank[:, :], tri[:, :], OH[:, ts, :].rearrange("p t e -> p (t e)"), start=True, stop=False)
                pe.matmul(bank[:, :], ones[:, :], PO[:, ts, :].rearrange("p t e -> p (t e)"), start=False, stop=True).then_inc(pe_v, 1)
            pe.wait_ge(s_w, 16 * 3)

            def down(e):
                if e % 2 == 0:
                    down.bank = bank_a("y", e // 2)
                o = (e % 2) * 2 * D
                pe.wait_ge(dve_job, JV.done("gu", e))
                pe.matmul(down.bank[:, o:o + D], hT[:, e % 4, 0:P], wd[:, e, :], start=True, stop=True)
                mm = pe.matmul(down.bank[0:CAP - P, o + D:o + 2 * D], hT[:, e % 4, P:CAP], wd[:, e, :], start=True, stop=True)
                if e % 2:
                    mm.then_inc(pe_a, 1)

            def turn(c):
                pe.wait_ge(s_x[c], x0 + 32)
                for k in range(0, CT, 4):
                    bank = bank_a("bt", c, k)
                    for j in range(k, min(k + 4, CT)):
                        mm = pe.transpose(bank[:, (j - k) * P:(j - k + 1) * P], BR[:, CT * c + j, :], ident[:, :])
                    mm.then_inc(pe_a, 1)

            turn(0)
            for e in range(E_):
                if e % CH == 1 and e + CH < E_:
                    turn(e // CH + 1)
                if e % CH == 0:
                    pe.wait_ge(act_job, JA.done("bt", e // CH, CT - CT % 4 if CT % 4 else CT - 4))
                bank = bank_v("gu", e)
                pe.matmul(bank[:, 0:CAP], wg[:, e, :], tr[:, e * CAP:(e + 1) * CAP], start=True, stop=True)
                pe.matmul(bank[:, CAP:2 * CAP], wu[:, e, :], tr[:, e * CAP:(e + 1) * CAP], start=True, stop=True).then_inc(pe_v, 1)
                if e:
                    down(e - 1)
            down(E_ - 1)

        @block.sync
        def _(sp):
            xr = rows(x_in, D)
            for b in range(B):
                sp.dma_start(X[:, b * TB:(b + 1) * TB, :], xr[:, b * TB:(b + 1) * TB, :]).then_inc(s_x[b], 16)
            for dst, src in ((ident, "ident"), (trif, "tri"), (rank, "rank"), (dump, "dump")):
                sp.dma_start(dst[:, :], cst[src]).then_inc(s_c, 16)
            sp.dma_start(wr[:, :], w["router"]).then_inc(s_c, 16)
            if first:
                sp.wait_ge(s_z, 2)
                sp.dma_start(xbuf[0:SLOTS, :].rearrange("(p r) d -> p (r d)", p=P)[:, 0:2560],
                             zero[:, None, :].to_broadcast([P, 2, 1280])).then_inc(s_zf, 16)
                sp.dma_start(xbuf[0:SLOTS, :].rearrange("(p r) d -> p (r d)", p=P)[:, 2560:5120],
                             zero[:, None, :].to_broadcast([P, 2, 1280])).then_inc(s_zf, 16)
                sp.dma_start(ybuf[SLOTS:SLOTS + 1, :], zero[0:1, 0:D]).then_inc(s_zf, 16)
            for dst, src in ((wg, "gate"), (wu, "up"), (wd, "down")):
                sp.dma_start(dst[:, :, :], w[src].rearrange("e h f -> h e f")).then_inc(s_w, 16)
            sp.wait_ge(s_sc, 16 * NT)
            for c in range(E_ // CH):
                sp.dma_start(BR[:, CT * c:CT * c + CT, :],
                             xbuf[c * CT * P:(c + 1) * CT * P, :].rearrange("(t p) d -> p t d", p=P)).then_inc(s_x[c], 16)
            yr = ybuf[0:SLOTS, :].rearrange("(e s) d -> s e d", s=CAP)
            for c in range(E_ // CH):
                es = slice(CH * c, CH * c + CH)
                sp.wait_ge(act_job, JA.done("y", (CH * c + CH) // 2 - 1))
                sp.dma_start(yr[0:P, es, :], YA[:, es, :]).then_inc(s_y, 16)
                sp.dma_start(yr[P:CAP, es, :], YB[:, es, :]).then_inc(s_y, 16)
            xo = rows(x_out, D)
            for b in range(B):
                sp.wait_ge(s_xs, b + 1)
                sp.dma_start(xo[:, b * TB:(b + 1) * TB, :], X[:, b * TB:(b + 1) * TB, :]).then_inc(s_out, 16)
            sp.wait_ge(s_out, 16 * B)

        @block.gpsimd
        def _(pool):
            pool.memset(eps[:, :], LN_EPS).then_inc(s_z, 1)
            if first:
                pool.memset(zero[:, :], 0.0).then_inc(s_z, 1)
            pool.memset(ones[:, :], 1.0).then_inc(s_bf, 1)
            pool.wait_ge(s_c, 16 * 5)
            pool.tensor_copy(tri[:, :], trif[:, :]).then_inc(s_bf, 1)
            if first:
                pool.wait_ge(s_zf, 16 * 3)
            pool.wait_ge(s_idx, 1)
            for t in range(NT):
                pool.indirect_dma_start(xbuf, bass.IndirectOffsetOnAxis(ap=si[:, t:t + 1], axis=0), XT[:, t, :], None).then_inc(s_sc, 16)
            pool.wait_ge(s_y, 16 * 2 * E_ // CH)
            for t in range(NT):
                pool.indirect_dma_start(GY[:, t, :], None, ybuf, bass.IndirectOffsetOnAxis(ap=gi[:, t:t + 1], axis=0)).then_inc(s_gy[t // TB], 16)

        @block.scalar
        def _(act):
            jobs = Jobs()

            def bank(name, *rest):
                i = jobs.next()
                assert JA.named[(name, *rest)] == i, (name, rest)
                act.wait_ge(pe_a, i + 1)
                return banks_a[i % RING]

            def copy(out, in_):
                return act.activation(out, in_, ACT.Copy)

            act.wait_ge(s_z, 1)
            act.wait_ge(s_sd, 1)
            act.activation(rstd[:, :], mv[:, :, 1], ACT.Sqrt, bias=eps[:, 0:1]).then_inc(s_rs, 1)
            for b in range(B):
                copy(tr[:, b * L:(b + 1) * L], bank("xT", b)[:, :]).then_inc(act_job, 1)
            act.wait_ge(s_lg, 1)
            act.activation(EX[:, :, :], LG[:, :, :], ACT.Exp).then_inc(s_ex, 1)

            def turn(c):
                for k in range(0, CT, 4):
                    n = min(4, CT - k) * P
                    if c == 0 and k == 0:
                        act.wait_ge(pe_v, JV.done("lg", 1))
                    copy(tr[:, (c * CT + k) * P:(c * CT + k) * P + n], bank("bt", c, k)[:, 0:n]).then_inc(act_job, 1)

            def y(q):
                src = bank("y", q)[:, :].rearrange("p (e s d) -> p e s d", e=2, s=2)
                copy(YA[:, 2 * q:2 * q + 2, :], src[:, :, 0, :])
                copy(YB[:, 2 * q:2 * q + 2, :], src[0:CAP - P, :, 1, :]).then_inc(act_job, 1)

            turn(0)
            for e in range(E_):
                if e >= 2 and e % 2 == 0:
                    y(e // 2 - 1)
                if e % CH == 1 and e + CH < E_:
                    turn(e // CH + 1)
                act.wait_ge(pe_v, JV.done("gu", e))
                if e >= 2:
                    act.wait_ge(dve_job, JV.done("gu", e - 2))
                act.activation(SG[:, e % 2, :], banks_v[JV.named[("gu", e)] % RING][:, 0:CAP], ACT.Silu).then_inc(s_sg, 1)
            y(E_ // 2 - 1)

        @block.vector
        def _(dve):
            jobs = Jobs()
            link_n = [0]

            def link(ins):
                link_n[0] += 1
                ins.then_inc(s_dve, 1)
                dve.wait_ge(s_dve, link_n[0])

            def bank(name, *rest):
                i = jobs.next()
                assert JV.named[(name, *rest)] == i, (name, rest)
                dve.wait_ge(pe_v, i + 1)
                return banks_v[i % RING]

            for b in range(B):
                dve.wait_ge(s_x[b], x0 + 16)
                for t in range(b * TB, b * TB + TB):
                    ins = dve.bn_stats(stats6[:, t, :], X[:, t, :])
                link(ins)
                for t in range(b * TB, b * TB + TB):
                    ins = dve.bn_aggr(mv[:, t, :], stats6[:, t, :])
            ins.then_inc(s_sd, 1)
            dve.wait_ge(s_rs, 1)
            link(dve.reciprocal(rstd[:, :], rstd[:, :]))
            for t in range(NT):
                dve.tensor_scalar(XT[:, t, :], X[:, t, :], mv[:, t, 0:1], rstd[:, t:t + 1], ALU.subtract, ALU.mult).then_inc(s_ln, 1)
            dve.wait_ge(s_c, 16 * 5)
            for k in range(2):
                ts = slice(16 * k, 16 * k + 16)
                src = bank("lg", k)[:, :].rearrange("p (t e) -> p t e", e=E_)
                link(dve.tensor_reduce(mx[:, ts], src, AX.X, ALU.max))
                dve.tensor_tensor(LG[:, ts, :], src, mx[:, ts].to_broadcast([P, 16, E_]), ALU.subtract).then_inc(dve_job, 1)
            dve.wait_ge(dve_job, JV.done("lg", 1))
            dve.tensor_scalar(LG[:, 0:1, 0:1], LG[:, 0:1, 0:1], 0.0, None, ALU.add).then_inc(s_lg, 1)
            dve.wait_ge(s_lg, 1)
            dve.wait_ge(s_ex, 1)
            link(dve.tensor_reduce(gate, EX[:, :, :], AX.X, ALU.add))
            dve.reciprocal(gate, gate)
            link(dve.tensor_scalar(LG[:, :, :], LG[:, :, :], 0.0, None, ALU.is_equal))
            link(dve.tensor_tensor(LG[:, :, :], LG[:, :, :], rank[:, None, :].to_broadcast([P, NT, E_]), ALU.mult))
            link(dve.tensor_reduce(best, LG[:, :, :], AX.X, ALU.max))
            dve.memset(PO[:, 0, :], 0.0)
            link(dve.tensor_tensor(OH[:, :, :], LG[:, :, :], best.to_broadcast([P, NT, E_]), ALU.is_equal))
            for t in range(1, NT):
                ins = dve.tensor_tensor(PO[:, t, :], PO[:, t - 1, :], OH[:, t - 1, :], ALU.add)
                if t < NT - 1:
                    link(ins)
            ins.then_inc(s_oh, 1)
            for k in range(2):
                ts = slice(16 * k, 16 * k + 16)
                dve.tensor_tensor(EX[:, ts, :], bank("pos", k)[:, :].rearrange("p (t e) -> p t e", e=E_), OH[:, ts, :], ALU.mult).then_inc(dve_job, 1)
            dve.wait_ge(dve_job, JV.done("pos", 1))
            link(dve.tensor_reduce(pos, EX[:, :, :], AX.X, ALU.add))
            dve.tensor_scalar(acc, pos, float(CAP), None, ALU.is_le)
            link(dve.scalar_tensor_tensor(slot, best, -float(CAP), pos, ALU.mult, ALU.add))
            link(dve.tensor_scalar(slot, slot, float(SLOTS - 1), None, ALU.add))
            dve.tensor_tensor(sidx, slot, dump[:, :], ALU.subtract)
            link(dve.tensor_scalar(gidx, slot, -float(SLOTS), None, ALU.add))
            dve.tensor_tensor(sidx, sidx, acc, ALU.mult)
            dve.tensor_tensor(gate, gate, acc, ALU.mult)
            link(dve.tensor_tensor(gidx, gidx, acc, ALU.mult))
            link(dve.tensor_tensor(sidx, sidx, dump[:, :], ALU.add))
            dve.tensor_scalar(gi[:, :], gidx, float(SLOTS), None, ALU.add)
            dve.tensor_copy(si[:, :], sidx).then_inc(s_idx, 1)
            for b in range(B):
                ts = slice(b * TB, b * TB + TB)
                ins = dve.tensor_tensor(X[:, ts, :], X[:, ts, :], XT[:, ts, :], ALU.add)
            link(ins)
            for e in range(E_):
                src = bank("gu", e)
                dve.wait_ge(s_sg, e + 1)
                if e >= 4:
                    dve.wait_ge(pe_a, JA.done("y", (e - 4) // 2))
                dve.tensor_tensor(hT[:, e % 4, :], src[:, CAP:2 * CAP], SG[:, e % 2, :], ALU.mult).then_inc(dve_job, 1)
            for b in range(B):
                dve.wait_ge(s_gy[b], 16 * TB)
                for t in range(b * TB, b * TB + TB):
                    ins = dve.scalar_tensor_tensor(X[:, t, :], GY[:, t, :], gate[:, t:t + 1], X[:, t, :], ALU.mult, ALU.add)
                ins.then_inc(s_xs, 1)


HB, DB = 16, D // 16
CLAMP = 1e5
Q_PART = (0, 0, 1, 1, 0, 2)
K_PART = (0, 1, 0, 1, 2, 0)
NTERM = len(Q_PART)
MAXROW = NTERM * DB
SEC = (0, 512, 896, 1152)
PW = 1280


def attn_b(nc, sems, s_x, x0, x_in, x_out, w, cst, stack):
    ctx = ExitStack()
    with ctx:
        sb = lambda name, shape, dt=F32: ctx.enter_context(nc.sbuf_tensor(f"b_{name}", shape, dt))
        sem = lambda name: sems.enter_context(nc.semaphore(f"b_{name}"))
        X = sb("X", [P, NT, D])
        xn, xnT = sb("xn", [P, 2 * TB, D]), sb("xnT", [P, 2, L])
        wp = sb("wp", [P, 5, D])
        rope = sb("rope", [P, 4, L])
        WO = sb("WO", [P, D])
        ident, eps = sb("ident", [P, P]), sb("eps", [P, 1])
        identb, mqf, mq, mk = sb("identb", [P, P], BF16), sb("mqf", [P, 2, P]), sb("mq", [P, P], BF16), sb("mk", [P, P], BF16)
        mv, stats6, rstd = sb("mv", [P, NT, 2]), sb("stats6", [P, NT, 6]), sb("rstd", [P, NT])
        RT = sb("RT", [P, 2, 2, L])
        PS = sb("PS", [P, 2, 2, 3, L], BF16)
        QS, KS = sb("QS", [P, 2, HB, L], BF16), sb("KS", [P, 2, HB, L], BF16)
        zr = sb("zr", [3, L], BF16)
        VX = sb("VX", [P, 3, TB, HB, 32])
        PB = sb("PB", [P, 8, PW])
        MX, MR = sb("MX", [P, TB, HB]), sb("MR", [P, TB, HB])
        N3 = sb("N3", [P, TB, 3, HB], BF16)
        NMT = sb("NMT", [3 * HB, L], BF16)
        OT, RC, OTK, OTT = sb("OT", [P, 2, L]), sb("RC", [P, TB, 4]), sb("OTK", [P, TB, D]), sb("OTT", [P, L])
        banks_a = [ctx.enter_context(nc.psum_tensor(f"b_pa{i}", [P, 512], F32)) for i in range(RING)]
        banks_v = [ctx.enter_context(nc.psum_tensor(f"b_pv{i}", [P, 512], F32)) for i in range(RING)]
        pe_a, pe_v, act_job, dve_job = (sem(n) for n in ("pe_a", "pe_v", "act_job", "dve_job"))
        (s_c, s_set, s_cb, s_sd, s_rs, s_ln, s_dve, s_pool, s_ps, s_nm, s_cp, s_cd, s_qz, s_vx, s_out) = (
            sem(n) for n in ("c", "set", "cb", "sd", "rs", "ln", "dve", "pool", "ps", "nm", "cp", "cd", "qz", "vx", "out"))
        s_st = [sem(f"st{i}") for i in range(2)]
        s_ld = [sem(f"ld{i}") for i in range(2)]
        s_mr = [sem(f"mr{i}") for i in range(2)]
        JA, JV = Jobs(), Jobs()
        NC = 5
        LOADS = 16 * (2 * NTERM + 1)

        amax = [(q, h, n) for q, n in ((0, 4), (1, 2), (2, 1), (3, 1)) for h in range(0, HB, n)]

        def steps():
            yield "project", 0, 0
            yield "project", 1, 0
            for i in range(len(amax)):
                yield "max", 0, i
            yield "take", 0, 0
            for b in range(B):
                for h in range(HB):
                    yield "probs", b, h
                    if b + 1 < B and 3 <= h < 13:
                        for i in range(len(amax) * (h - 3) // 10, len(amax) * (h - 2) // 10):
                            yield "max", b + 1, i
                    if h == 12 and b + 1 < B:
                        yield "take", b + 1, 0
                    if h == 8 and b + 2 < B:
                        yield "project", b + 2, 0
                    if h % 4 == 1 and h > 4:
                        yield "values", b, h // 4 - 1
                    if h % 4 == 3 and h > 4:
                        yield "norm", b, h // 4 - 1
                yield "values", b, 3
                yield "norm", b, 3
                yield "out", b, 0

        def load(sp, b):
            s = b % 2
            sp.wait_ge(s_st[s], 32 * (b // 2 + 1))
            sp.wait_ge(s_set, 3)
            sp.wait_ge(s_qz, 1)
            if b >= 2:
                sp.wait_ge(pe_a, JA.done("sc", b - 2, HB - 1, 2))
            for t in range(NTERM):
                e = slice(DB * t, DB * t + DB)
                for k, (S, part) in enumerate(((QS, Q_PART), (KS, K_PART))):
                    sp.dma_start(S[e, s, :, :], stack[s, k, part[t]].rearrange("(h d) t -> d h t", d=DB)).then_inc(s_ld[s], 16)
            sp.dma_start(QS[MAXROW:MAXROW + 3, s, :, :], zr[:, None, :].to_broadcast([3, HB, L])).then_inc(s_ld[s], 16)

        block = ctx.enter_context(nc.Block())

        @block.tensor
        def _(pe):
            def bank_a(*name):
                i = JA.next(*name)
                if i >= RING:
                    pe.wait_ge(act_job, i - RING + 1)
                return banks_a[i % RING]

            def bank_v(*name):
                i = JV.next(*name)
                if i >= RING:
                    pe.wait_ge(dve_job, i - RING + 1)
                return banks_v[i % RING]

            pe.wait_ge(s_c, 16 * NC)
            pe.wait_ge(s_cb, 3)
            for step, b, i in steps():
                s = b % 2
                if step == "project":
                    bank = bank_a("xT", b)
                    for j in range(TB):
                        pe.wait_ge(s_ln, b * TB + j + 1)
                        mm = pe.transpose(bank[:, j * P:(j + 1) * P], xn[:, s * TB + j, :], ident[:, :])
                    mm.then_inc(pe_a, 1)
                    pe.wait_ge(act_job, JA.done("xT", b))
                    for k in range(4):
                        bank = bank_v("qk", b, k)
                        pe.matmul(bank[:, :], wp[:, k, :], xnT[:, s, :], start=True, stop=True).then_inc(pe_v, 1)
                    bank = bank_a("v", b)
                    for j in range(TB):
                        mm = pe.matmul(bank[:, j * P:(j + 1) * P], xnT[:, s, j * P:(j + 1) * P], wp[:, 4, :], start=True, stop=True)
                    mm.then_inc(pe_a, 1)
                elif step == "max":
                    q, h0, n = amax[i]
                    if i == 0:
                        pe.wait_ge(s_ld[s], LOADS * (b // 2 + 1))
                    bank = bank_v("max", b, i)
                    wd = (q + 1) * P
                    for h in range(h0, h0 + n):
                        o = (h - h0) * wd
                        pe.matmul(bank[:, o:o + wd], QS[:, s, h, q * P:wd], KS[:, s, h, 0:wd], start=True, stop=False)
                        mm = pe.matmul(bank[:, o + q * P:o + wd], identb[:, :], mq[:, :], start=False, stop=True)
                    mm.then_inc(pe_v, 1)
                elif step == "take":
                    bank = bank_a("nm", b)
                    pe.wait_ge(s_nm, b + 1)
                    for j in range(TB):
                        mm = pe.transpose(bank[:, 0:256].bitcast(BF16)[0:3 * HB, j * P:(j + 1) * P],
                                          N3[:, j, :, :].rearrange("p a h -> p (a h)"), identb[:, :])
                    mm.then_inc(pe_a, 1)
                elif step == "probs":
                    h = i
                    if h == 0:
                        pe.wait_ge(s_mr[s], 48 * (b // 2 + 1))
                    for part in ((0,), (1,), (2, 3)):
                        bank = bank_a("sc", b, h, part[0])
                        o = 0
                        for kt in part:
                            n = L - kt * P
                            pe.matmul(bank[:, o:o + n], KS[:, s, h, kt * P:(kt + 1) * P], QS[:, s, h, kt * P:L], start=True, stop=False)
                            mm = pe.matmul(bank[:, o:o + P], identb[:, :], mk[:, :], start=False, stop=True)
                            o += n
                        mm.then_inc(pe_a, 1)
                elif step == "values":
                    bank = bank_a("pv", b, i)
                    n = b * HB + 4 * i + 4
                    pe.wait_ge(s_cd, n)
                    pe.wait_ge(s_cp, n)
                    for kt in range(TB):
                        for j in range(4):
                            h = 4 * i + j
                            mm = pe.matmul(bank[32 * j:32 * j + 32, kt * P:L], VX[:, b % 3, kt, h, :],
                                           PB[:, h % 8, SEC[kt]:SEC[kt] + L - kt * P], start=kt == 0, stop=kt == TB - 1)
                    mm.then_inc(pe_a, 1)
                elif step == "norm":
                    bank = bank_v("den", b, i)
                    pe.wait_ge(act_job, JA.done("pv", b, i))
                    for j in range(TB):
                        mm = pe.transpose(bank[:, j * P:(j + 1) * P], OT[:, i % 2, j * P:(j + 1) * P], ident[:, :])
                    mm.then_inc(pe_v, 1)
                else:
                    bank = bank_a("oT", b)
                    pe.wait_ge(dve_job, JV.done("den", b, 3))
                    for j in range(TB):
                        mm = pe.transpose(bank[:, j * P:(j + 1) * P], OTK[:, j, :], ident[:, :])
                    mm.then_inc(pe_a, 1)
                    bank = bank_v("out", b)
                    pe.wait_ge(act_job, JA.done("oT", b))
                    for j in range(TB):
                        mm = pe.matmul(bank[:, j * P:(j + 1) * P], OTT[:, j * P:(j + 1) * P], WO[:, :], start=True, stop=True)
                    mm.then_inc(pe_v, 1)

        @block.sync
        def _(sp):
            xr, xo = rows(x_in, D), rows(x_out, D)
            for b in range(B):
                sp.dma_start(X[:, b * TB:(b + 1) * TB, :], xr[:, b * TB:(b + 1) * TB, :]).then_inc(s_x[b], 16)
            sp.dma_start(ident[:, :], cst["ident"]).then_inc(s_c, 16)
            sp.dma_start(mqf[:, :, :], cst["causal"]).then_inc(s_c, 16)
            sp.dma_start(rope[:, :, :], cst["rope"]).then_inc(s_c, 16)
            sp.dma_start(wp[:, :, :], w["qkv"]).then_inc(s_c, 16)
            sp.dma_start(WO[:, :], w["o"]).then_inc(s_c, 16)
            for step, b, i in steps():
                s = b % 2
                if step == "project":
                    sp.wait_ge(s_ps, 2 * b + 2)
                    if b >= 2:
                        sp.wait_ge(s_ld[s], LOADS * (b // 2))
                    for k in range(2):
                        sp.dma_start(stack[s, k].rearrange("a p t -> p a t"), PS[:, s, k, :, :]).then_inc(s_st[s], 16)
                elif step == "max" and i == 0 and b == 0:
                    load(sp, 0)
                    load(sp, 1)
                elif step == "take":
                    sp.wait_ge(act_job, JA.done("nm", b))
                    for a in range(3):
                        sp.dma_start(QS[MAXROW + a:MAXROW + a + 1, s, :, :], NMT[a * HB:(a + 1) * HB, :]).then_inc(s_mr[s], 16)
                elif step == "out":
                    if b + 2 < B:
                        load(sp, b + 2)
                    sp.wait_ge(dve_job, JV.done("out", b))
                    sp.dma_start(xo[:, b * TB:(b + 1) * TB, :], X[:, b * TB:(b + 1) * TB, :]).then_inc(s_out, 16)
            sp.wait_ge(s_out, 16 * B)


        @block.gpsimd
        def _(pool):
            pool.memset(eps[:, :], LN_EPS).then_inc(s_set, 1)
            pool.memset(KS[:, :, :, :], 1.0).then_inc(s_set, 1)
            pool.memset(zr[:, :], 0.0).then_inc(s_set, 1)
            pool.memset(VX[:, :, :, :, :], 0.0).then_inc(s_vx, 1)
            pool.wait_ge(s_vx, 1)
            pool.memset(VX[:, :, :, :, DB], 1.0).then_inc(s_vx, 1)
            pool.wait_ge(s_c, 16 * NC)
            pool.tensor_copy(identb[:, :], ident[:, :]).then_inc(s_cb, 1)
            pool.tensor_copy(mq[:, :], mqf[:, 0, :]).then_inc(s_cb, 1)
            pool.tensor_copy(mk[:, :], mqf[:, 1, :]).then_inc(s_cb, 1)
            link_n = [0]

            def link(ins):
                link_n[0] += 1
                ins.then_inc(s_pool, 1)
                pool.wait_ge(s_pool, link_n[0])

            def clamp(n):
                b, h = n // HB, n % HB
                pool.wait_ge(act_job, JA.done("sc", b, h, 0))
                e = PB[:, h % 8, 0:512]
                pool.tensor_scalar(e, e, 1.0, None, ALU.min).then_inc(s_cp, 1)

            for step, b, i in steps():
                s = b % 2
                if step == "project":
                    if b >= 2:
                        pool.wait_ge(s_st[s], 32 * (b // 2))
                    for k in range(2):
                        pool.wait_ge(dve_job, JV.done("qk", b, 2 * k + 1))
                        a, r, part = RT[:, k, 0, :], RT[:, k, 1, :], PS[:, s, k, :, :]
                        link(pool.tensor_tensor(a, a, r, ALU.add))
                        link(pool.tensor_copy(part[:, 0, :], a))
                        link(pool.tensor_tensor(r, a, part[:, 0, :], ALU.subtract))
                        link(pool.tensor_copy(part[:, 1, :], r))
                        pool.tensor_tensor(part[:, 2, :], r, part[:, 1, :], ALU.subtract).then_inc(s_ps, 1)
                elif step == "probs" and i:
                    clamp(b * HB + i - 1)
                elif step == "values" and i == 3:
                    clamp(b * HB + HB - 1)

        @block.scalar
        def _(act):
            jobs = Jobs()

            def bank(name, *rest):
                i = jobs.next()
                assert JA.named[(name, *rest)] == i, (name, rest)
                act.wait_ge(pe_a, i + 1)
                return banks_a[i % RING]

            def copy(out, in_):
                return act.activation(out, in_, ACT.Copy)

            act.wait_ge(s_set, 1)
            act.wait_ge(s_sd, 1)
            act.activation(rstd[:, :], mv[:, :, 1], ACT.Sqrt, bias=eps[:, 0:1]).then_inc(s_rs, 1)
            act.wait_ge(s_vx, 2)
            for step, b, i in steps():
                s = b % 2
                if step == "project":
                    if b >= 2:
                        act.wait_ge(pe_a, JA.done("v", b - 2))
                    copy(xnT[:, s, :], bank("xT", b)[:, :]).then_inc(act_job, 1)
                    if b >= 3:
                        act.wait_ge(pe_a, JA.done("pv", b - 3, 3))
                    copy(VX[:, b % 3, :, :, 0:DB].rearrange("p k h d -> p (k h) d"),
                         bank("v", b)[:, :].rearrange("p (n d) -> p n d", d=DB)).then_inc(act_job, 1)
                elif step == "take":
                    if b:
                        act.wait_ge(s_mr[1 - s], 48 * ((b - 1) // 2 + 1))
                    copy(NMT[:, :], bank("nm", b)[:, 0:256].bitcast(BF16)[0:3 * HB, :]).then_inc(act_job, 1)
                elif step == "probs":
                    n = b * HB + i
                    if n >= 8:
                        act.wait_ge(pe_a, JA.done("pv", (n - 8) // HB, (n - 8) % HB // 4))
                    for o, e, part in ((0, 512, 0), (512, 896, 1), (896, PW, 2)):
                        act.activation(PB[:, i % 8, o:e], bank("sc", b, i, part)[:, 0:e - o], ACT.Exp).then_inc(act_job, 1)
                elif step == "values":
                    n = 4 * b + i
                    if n >= 2:
                        act.wait_ge(pe_v, JV.done("den", (n - 2) // 4, (n - 2) % 4))
                    copy(OT[:, i % 2, :], bank("pv", b, i)[:, :]).then_inc(act_job, 1)
                elif step == "out":
                    if b:
                        act.wait_ge(pe_v, JV.done("out", b - 1))
                    copy(OTT[:, :], bank("oT", b)[:, :]).then_inc(act_job, 1)

        @block.vector
        def _(dve):
            jobs = Jobs()
            link_n = [0]

            def link(ins):
                link_n[0] += 1
                ins.then_inc(s_dve, 1)
                dve.wait_ge(s_dve, link_n[0])

            def bank(name, *rest):
                i = jobs.next()
                assert JV.named[(name, *rest)] == i, (name, rest)
                dve.wait_ge(pe_v, i + 1)
                return banks_v[i % RING]

            def clamp(n):
                b, h = n // HB, n % HB
                dve.wait_ge(act_job, JA.done("sc", b, h, 2))
                e = PB[:, h % 8, 512:PW]
                dve.tensor_scalar(e, e, 1.0, None, ALU.min).then_inc(s_cd, 1)

            dve.memset(QS[:, :, :, :].rearrange("p s h t -> p (s h t)").bitcast(F32), 0.0).then_inc(s_qz, 1)
            for b in range(B):
                dve.wait_ge(s_x[b], x0 + 16)
                for t in range(b * TB, b * TB + TB):
                    ins = dve.bn_stats(stats6[:, t, :], X[:, t, :])
                link(ins)
                for t in range(b * TB, b * TB + TB):
                    ins = dve.bn_aggr(mv[:, t, :], stats6[:, t, :])
            ins.then_inc(s_sd, 1)
            dve.wait_ge(s_rs, 1)
            link(dve.reciprocal(rstd[:, :], rstd[:, :]))
            dve.wait_ge(s_c, 16 * NC)
            for step, b, i in steps():
                s = b % 2
                if step == "project":
                    if b >= 2:
                        dve.wait_ge(pe_a, JA.done("xT", b - 2))
                    for t in range(b * TB, b * TB + TB):
                        dve.tensor_scalar(xn[:, t % (2 * TB), :], X[:, t, :], mv[:, t, 0:1], rstd[:, t:t + 1],
                                          ALU.subtract, ALU.mult).then_inc(s_ln, 1)
                    if b:
                        dve.wait_ge(s_ps, 2 * b)
                    for k in range(4):
                        dve.tensor_tensor(RT[:, k // 2, k % 2, :], bank("qk", b, k)[:, :], rope[:, k, :], ALU.mult).then_inc(dve_job, 1)
                elif step == "max":
                    q, h0, n = amax[i]
                    dve.tensor_reduce(MX[:, q, h0:h0 + n],
                                      bank("max", b, i)[:, 0:n * (q + 1) * P].rearrange("p (h k) -> p h k", h=n),
                                      AX.X, ALU.max).then_inc(dve_job, 1)
                elif step == "take":
                    dve.wait_ge(dve_job, JV.done("max", b, len(amax) - 1))
                    if b:
                        dve.wait_ge(pe_a, JA.done("nm", b - 1))
                    link(dve.tensor_scalar(MR[:, :, :], MX[:, :, :], -CLAMP, CLAMP, ALU.max, ALU.min))
                    link(dve.tensor_scalar(MX[:, :, :], MR[:, :, :], -1.0, None, ALU.mult))
                    link(dve.tensor_copy(N3[:, :, 0, :], MX[:, :, :]))
                    link(dve.tensor_tensor(MR[:, :, :], MX[:, :, :], N3[:, :, 0, :], ALU.subtract))
                    link(dve.tensor_copy(N3[:, :, 1, :], MR[:, :, :]))
                    dve.tensor_tensor(N3[:, :, 2, :], MR[:, :, :], N3[:, :, 1, :], ALU.subtract).then_inc(s_nm, 1)
                elif step == "probs" and i:
                    clamp(b * HB + i - 1)
                elif step == "values" and i == 3:
                    clamp(b * HB + HB - 1)
                elif step == "norm":
                    src = bank("den", b, i)[:, :].rearrange("p (t j r) -> p t j r", t=TB, j=4)
                    if i or b:
                        dve.wait_ge(dve_job, JV.done("den", b, i) - 1)
                    link(dve.reciprocal(RC[:, :, :], src[:, :, :, DB]))
                    if i == 0 and b:
                        dve.wait_ge(pe_a, JA.done("oT", b - 1))
                    dve.tensor_tensor(OTK[:, :, 4 * DB * i:4 * DB * (i + 1)].rearrange("p t (j d) -> p t j d", j=4),
                                      src[:, :, :, 0:DB], RC[:, :, :].to_broadcast([P, TB, 4, DB]), ALU.mult).then_inc(dve_job, 1)
                elif step == "out":
                    xb = X[:, b * TB:(b + 1) * TB, :].rearrange("p t d -> p (t d)")
                    dve.tensor_tensor(xb, xb, bank("out", b)[:, :], ALU.add).then_inc(dve_job, 1)


def layers(nc, x_in, x_out, wa, wb, wf, ca, cb, cf):
    x1, x2, x3 = (nc.dram_tensor(f"x{i}", [T, D], F32).ap() for i in (1, 2, 3))
    xbuf = nc.dram_tensor("xbuf", [SLOTS + T, D], F32).ap()
    ybuf = nc.dram_tensor("ybuf", [SLOTS + 1, D], F32).ap()
    stack = nc.dram_tensor("stack", [2, 2, 3, P, L], BF16).ap()
    with ExitStack() as sems:
        s_x = [sems.enter_context(nc.semaphore(f"batch{b}")) for b in range(B)]
        attn_a(nc, sems, s_x, x_in, x1, wa, ca)
        moe(nc, sems, s_x, 32, x1, x2, wf, cf, xbuf, ybuf, "f1", True)
        attn_b(nc, sems, s_x, 64, x2, x3, wb, cb, stack)
        moe(nc, sems, s_x, 80, x3, x_out, wf, cf, xbuf, ybuf, "f2", False)


def kernel(**inputs):
    import concourse.bacc as _bacc
    from concourse.bass_utils import run_bass_kernel_spmd as _run

    x = np.ascontiguousarray(inputs["L0_attn_a_hidden_states"]).reshape(T, D)
    a = {n[len("L0_attn_a_"):]: np.asarray(v) for n, v in inputs.items() if n.startswith("L0_attn_a_")}
    b = {n[len("L0_attn_b_"):]: np.asarray(v) for n, v in inputs.items() if n.startswith("L0_attn_b_")}
    f = {n[len("L0_ffn_w_"):]: np.asarray(v) for n, v in inputs.items() if n.startswith("L0_ffn_w_")}

    fir = np.zeros((P, 2, 3 * KL), np.float32)
    fir[:, 0, KL:2 * KL] = a["fir_long_w"].reshape(P, KL)
    fir[:, 1, 2 * KL - 5:2 * KL] = a["fir_short_w"].reshape(P, 5)
    swap = np.arange(D) ^ 1
    weights = {
        "a": {"qkvT": np.stack([a["q_w"].T, a["k_w"].T, a["v_w"].T], axis=1),
              "cw": np.stack([a["q_cw"].T, a["k_cw"].T, a["v_cw"].T]),
              "bT": a["b_w"].T, "w1xT": a["mlp1_w"][:, :D].T, "w1sT": a["mlp1_w"][:, D:].T,
              "oT": a["o_w"].T, "fir": fir, "w2T": a["mlp2_w"].T, "b2": a["mlp2_b"],
              "temp": a["logit_temp"], "res": a["conv_res_logit"],
              "norm": a["norm_w"].reshape(DK, 1), "b1": a["mlp1_b"].reshape(P, 1)},
        "b": {"qkv": np.stack([b["WQ"].T, b["WQ"][swap].T, b["WK"].T, b["WK"][swap].T, b["WV"].T], axis=1),
              "o": b["WO"].T},
        "f": f,
    }

    p, q = np.arange(P)[:, None], np.arange(P)[None]
    r, c = p % C, np.arange(C)[None]
    turns = np.float32(10000.0) ** -(((p % DB) // 2).astype(np.float32) / np.float32(DB // 2))
    angle = np.arange(L, dtype=np.float32)[None] * turns
    cos, sin = np.cos(angle), np.sin(angle) * np.where(p % 2 == 0, -1.0, 1.0)
    later = np.where(q > p, -1e30, 0.0)
    ident = p == q
    constants = {
        "a": {"ident": ident, "ones_h": p // DK == q // DK, "flip": q == 64 * (p // 64) + 63 - p % 64,
              "masks": np.stack([-1.0 * (r > c), 1.0 * (c >= r), 1.0 * (c == r)], axis=1)},
        "b": {"ident": ident, "causal": np.stack([later, later.T], axis=1),
              "rope": np.stack([cos / np.sqrt(DB), sin / np.sqrt(DB), cos, sin], axis=1)},
        "f": {"ident": ident, "tri": p <= q, "rank": np.tile(np.arange(E_, 0, -1), (P, 1)),
              "dump": SLOTS + p + P * np.arange(NT)[None]},
    }

    nc = _bacc.Bacc("TRN2", target_bir_lowering=False, num_devices=1)
    arrays = {}

    def given(name, array):
        arrays[name] = np.ascontiguousarray(array)
        return nc.dram_tensor(name, array.shape, mybir.dt.from_np(array.dtype), kind="ExternalInput").ap()

    x_ap = given("in_x_dram", x)
    w = {k: {n: given(f"in_{k}_{n}_dram", v) for n, v in d.items()} for k, d in weights.items()}
    cst = {k: {n: given(f"const_{k}_{n}_dram", v.astype(np.float32)) for n, v in d.items()} for k, d in constants.items()}
    out = nc.dram_tensor("out_0_dram", (T, D), F32, kind="ExternalOutput").ap()
    layers(nc, x_ap, out, w["a"], w["b"], w["f"], cst["a"], cst["b"], cst["f"])
    got = _run(nc, [arrays], core_ids=[0])
    return got.results[0]["out_0_dram"].reshape(B, L, D)
```

```python
from contextlib import ExitStack

import numpy as np

import concourse.bass as bass
from concourse import mybir

F32 = mybir.dt.float32
BF16 = mybir.dt.bfloat16
I32 = mybir.dt.int32
ALU = mybir.AluOpType
ACT = mybir.ActivationFunctionType
AX = mybir.AxisListType

P = 128
B, L, D = 8, 512, 128
T = B * L
NT = T // P
TB = L // P
H, DK = 4, 32
C = 32
G = T // C
GB = L // C
TAPS = 4
PROB_FLOOR = 0.02
KL = 64
LN_EPS = 1e-5

RING = 4


class Jobs:

    def __init__(self):
        self.n = 0
        self.named = {}

    def next(self, *name):
        i = self.n
        self.n += 1
        if name:
            self.named[name] = i
        return i

    def done(self, *name):
        return self.named[name] + 1


def rows(dram, cols):
    return dram.rearrange("(t p) d -> p t d", p=P)


def attn_a(nc, sems, s_x, x_in, x_out, w, cst):
    NTR = 4
    ctx = ExitStack()
    with ctx:
        R = ctx.enter_context(nc.sbuf_tensor("a_regions", [P, 11, 4096], F32))
        xnT = ctx.enter_context(nc.sbuf_tensor("a_xnT", [P, B, L + TAPS - 1], F32))

        def reg(i, n=1):
            return R[:, i:i + n, :].rearrange("p a b -> p (a b)")

        small = lambda name, shape, dt=F32: ctx.enter_context(nc.sbuf_tensor("a_" + name, shape, dt))
        ident = small("ident", [P, P])
        eps = small("eps", [P, 4])
        mv = small("mv", [P, NT, 2])
        rstd = small("rstd", [P, NT])
        beta = small("beta", [P, G])
        rn = small("rn", [P, 2, G])
        bk = small("bk", [P, 2, G])
        wo = small("wo", [P, P])
        masks = small("masks", [P, 3, C])
        wbig = small("wbig", [P, 3, P])
        hdr = small("hdr", [P, 16])

        X = reg(9).rearrange("p (t d) -> p t d", t=NT)
        xn = reg(10).rearrange("p (t d) -> p t d", t=NT)
        stats6 = reg(6)[:, 0:NT * 6].rearrange("p (t s) -> p t s", s=6)
        WC = reg(8)[:, 0:12 * P].rearrange("p (s j c) -> p s j c", s=3, j=TAPS)
        CWB = reg(7)[:, 12 * P:24 * P].rearrange("p (s j c) -> p s j c", s=3, j=TAPS)
        WQKV = reg(7)[:, 24 * P:27 * P].rearrange("p (s c) -> p s c", s=3)
        bwT = reg(7)[:, 27 * P:27 * P + H]
        VT = reg(3)
        VH = reg(4).rearrange("p (g d) -> p g d", d=DK)
        v0 = reg(9).rearrange("p (t c) -> p t c", c=P)
        vE = reg(5).rearrange("p (t c) -> p t c", c=P)
        vO = reg(6).rearrange("p (t c) -> p t c", c=P)
        TR = reg(1, 2).rearrange("p (r h d n) -> p r h d n", r=NTR, h=H, d=4)
        LS = reg(9).rearrange("p (g d) -> p g d", d=DK)
        LLG = reg(10).rearrange("p (g d) -> p g d", d=DK)
        KQ = reg(1, 2).rearrange("p (g s c) -> p g s c", s=2, c=C)
        VK = reg(5, 2).rearrange("p (g s c) -> p g s c", s=2, c=C)
        AK = reg(7, 2).rearrange("p (g s c) -> p g s c", s=2, c=C)
        MS = reg(3).rearrange("p (g c) -> p g c", c=C)
        ME = reg(0).rearrange("p (h r c) -> p h r c", h=H, r=C)
        TI = reg(3).rearrange("p (r h c) -> p h r c", h=H, r=C)
        TIr = reg(3).rearrange("p (r n) -> p r n", r=C)
        TMP = reg(5).rearrange("p (h n) -> p h n", h=H)
        TT = reg(0).rearrange("p (g c) -> p g c", c=C)
        AT = reg(3).rearrange("p (g c) -> p g c", c=C)
        SS = reg(0).rearrange("p (g c) -> p g c", c=C)
        DH = reg(3).rearrange("p (g c) -> p g c", c=C)
        QKH = reg(6).rearrange("p (i s g c) -> p i s g c", i=4, s=2, c=C)

        w1s = small("w1s", [P, H, P])
        w2p = small("w2p", [P, DK])
        NW = 8 + 3 + 2 * H + 1 + H
        XS = [LS, LLG, DH, VH]
        SQX = [AK[:, :, 1, :], VK[:, :, 1, :], AK[:, :, 1, :], AK[:, :, 1, :]]
        ST = KQ[:, :, 0, :]
        STT = VK[:, :, 1, :]
        H1 = [reg(0)[:, i * L:(i + 1) * L] for i in range(8)]
        LG = reg(2).rearrange("p (g s) -> p g s", s=DK)
        OH = reg(1).rearrange("p (g d) -> p g d", d=DK)
        O2 = reg(7).rearrange("p (g d) -> p g d", d=DK)
        OSQ = LLG
        OT = reg(9)
        OSCR = reg(7)[:, 3584:4096]
        groups = ((0, 4), (4, 6), (6, 8))
        XR = xnT[:, :, :].rearrange("p b l -> p (b l)")[:, 0:T].rearrange("p (t d) -> p t d", d=D)
        sm = reg(8)
        stat = small("stat", [P, 3, 4, G])
        S1, S2, MM = (stat[:, i] for i in range(3))
        PR = sm[:, 0:512].rearrange("p (g k) -> p g k", k=4)
        R1, R2 = sm[:, 512:512 + G], sm[:, 640:640 + G]
        O3 = sm[:, 1024:1536].rearrange("p (g d) -> p g d", d=DK)
        w1x, bw, flip = (wbig[:, i, :] for i in range(3))

        banks_a = [ctx.enter_context(nc.psum_tensor(f"a_pa{i}", [P, 512], F32)) for i in range(RING)]
        banks_v = [ctx.enter_context(nc.psum_tensor(f"a_pv{i}", [P, 512], F32)) for i in range(RING)]
        sem = lambda name: sems.enter_context(nc.semaphore("a_" + name))
        pe_a, pe_v = sem("pe_a"), sem("pe_v")
        act_job, dve_job = sem("act_job"), sem("dve_job")
        s_w, s_out = sem("s_w"), sem("s_out")
        s_t = [sem(f"s_t{i}") for i in range(NTR)]
        s_pad, s_bw, s_wc, s_ln, s_sd, s_rs = (sem(n) for n in ("pad", "bw", "wc", "ln", "sd", "rs"))
        s_vo, s_voz, s_sq, s_nrm, s_kh, s_dve, s_pool, s_beta, s_vk, s_msb, s_el, s_elp, s_tz = (
            sem(n) for n in ("vo", "voz", "sq", "nrm", "kh", "dve", "pool", "beta", "vk", "msb", "el", "elp", "tz"))
        s_beta0, s_beta1, s_scan, s_kt, s_ss, s_rd, s_bk, s_r2 = (sem(n) for n in ("beta0", "beta1", "scan", "kt", "ss", "rd", "bk", "r2"))
        s_st, s_sqx, s_l2, s_stt, s_hdr2, s_e, s_ex, s_mix, s_ms, s_rms, s_o, s_oT, s_w1s, s_elim, s_bst, s_p, s_pl, s_o2 = (
            sem(n) for n in ("st", "sqx", "l2", "stt", "hdr2", "e", "ex", "mix", "ms", "rms", "o", "oT", "w1s", "elim", "bst", "p", "pl", "o2"))
        JA, JV = Jobs(), Jobs()
        NSLAB = DK // 4

        block = ctx.enter_context(nc.Block())

        def eliminate(eng, hs, chain, last):
            n = hs.stop - hs.start
            eng.wait_ge(act_job, JA.done("me", C // 4 - 1))
            eng.wait_ge(s_tz, 1)
            for j in range(C - 1):
                r, c = C - 1 - j, j + 1
                tmp = TMP[:, hs, 0:r * c].rearrange("p h (r c) -> p h r c", c=c)
                if j:
                    eng.wait_ge(chain, 2 * j)
                eng.tensor_tensor(tmp, ME[:, hs, j + 1:C, j:j + 1].to_broadcast([P, n, r, c]),
                                  TI[:, hs, j:j + 1, 0:c].to_broadcast([P, n, r, c]), ALU.mult).then_inc(chain, 1)
                eng.wait_ge(chain, 2 * j + 1)
                ins = eng.tensor_tensor(TI[:, hs, j + 1:C, 0:c], TI[:, hs, j + 1:C, 0:c], tmp, ALU.add)
                if j < C - 2:
                    ins.then_inc(chain, 1)
            ins.then_inc(last, 1)

        def gate_pe(pe, bank_a, bank_v):
            def logits(b):
                bank = bank_v("lg", b)
                pe.wait_ge(act_job, JA.done("h1", b, H - 1))
                for h in range(H):
                    mm = pe.matmul(bank[DK * h:DK * h + DK, :], w2p[:, :], H1[(b * H + h) % 8], start=True, stop=True)
                mm.then_inc(pe_v, 1)

            for b in range(B):
                for h in range(H):
                    bank = bank_a("h1", b, h)
                    if h == 0:
                        pe.wait_ge(s_stt, b + 1)
                    pe.matmul(bank[:, :], w1x, xnT[:, b, TAPS - 1:], start=True, stop=False)
                    pe.matmul(bank[:, :], w1s[:, h, :], STT[:, b * GB:(b + 1) * GB, :], start=False, stop=True).then_inc(pe_a, 1)
                if b:
                    logits(b - 1)
            logits(B - 1)
            for b in range(B):
                bank = bank_v("o", b)
                pe.wait_ge(s_oT, b + 1)
                for j in range(TB):
                    t = b * TB + j
                    mm = pe.matmul(bank[:, j * P:(j + 1) * P], OT[:, t * P:(t + 1) * P], wo[:, :], start=True, stop=True)
                mm.then_inc(pe_v, 1)

        def gate_act(act, bank, copy):
            act.wait_ge(act_job, JA.done("ku", B - 1))
            act.wait_ge(pe_a, JA.done("ku", B - 1))
            act.activation(SQX[0], XS[0], ACT.Square).then_inc(s_sqx, 1)
            act.wait_ge(pe_v, JV.done("qa", G // 8 - 1))
            act.activation(SQX[1], XS[1], ACT.Square).then_inc(s_sqx, 1)
            act.wait_ge(s_r2, 1)
            act.activation(SQX[3], XS[3], ACT.Square).then_inc(s_sqx, 1)
            act.wait_ge(s_r2, 2)
            for b in range(B + 1):
                if b < B:
                    gs = slice(b * GB, b * GB + GB)
                    act.wait_ge(dve_job, JV.done("dh", b))
                    act.activation(SQX[2][:, gs, :], DH[:, gs, :], ACT.Square).then_inc(s_sqx, 1)
                if b:
                    gs = slice((b - 1) * GB, b * GB)
                    act.wait_ge(s_st, b)
                    act.activation(ST[:, gs, 3:16:4].rearrange("p g k -> p k g"), S2[:, :, gs], ACT.Sqrt).then_inc(s_l2, 1)
            act.activation(hdr[:, 8:9], hdr[:, 4:5], ACT.Abs).then_inc(s_hdr2, 1)
            act.wait_ge(s_hdr2, 1)
            act.activation(hdr[:, 8:9], hdr[:, 8:9], ACT.Exp, scale=-1.0).then_inc(s_hdr2, 1)
            act.wait_ge(s_hdr2, 2)
            act.activation(hdr[:, 8:9], hdr[:, 8:9], ACT.Ln, bias=eps[:, 2:3]).then_inc(s_hdr2, 1)
            act.activation(hdr[:, 9:10], hdr[:, 5:6], ACT.Sigmoid).then_inc(s_hdr2, 1)
            def exps(n):
                b0, b1 = groups[n]
                gs = slice(b0 * GB, b1 * GB)
                act.wait_ge(s_e, n + 1)
                act.activation(PR[:, gs, :], PR[:, gs, :], ACT.Exp, scale=hdr[:, 10:11]).then_inc(s_ex, 1)

            def squares(n):
                b0, b1 = groups[n]
                for b in range(b0, b1):
                    gs = slice(b * GB, b * GB + GB)
                    act.wait_ge(s_mix, b + 1)
                    act.activation(OSQ[:, gs, :], OH[:, gs, :], ACT.Square).then_inc(s_o, 1)
                act.wait_ge(s_ms, n + 1)
                act.activation(R1[:, b0 * GB:b1 * GB], R1[:, b0 * GB:b1 * GB], ACT.Sqrt, bias=eps[:, 0:1], scale=1.0 / DK).then_inc(s_rms, 1)

            for b in range(B):
                for h in range(H):
                    if b >= 2 and h == 0:
                        act.wait_ge(pe_v, JV.done("lg", b - 2))
                    act.activation(H1[(b * H + h) % 8], bank("h1", b, h)[:, :], ACT.Gelu_apprx_tanh,
                                   bias=hdr[:, 7:8]).then_inc(act_job, 1)
                for n, (b0, b1) in enumerate(groups):
                    if b == b1:
                        exps(n)
                    if b == b1 + 1 and n < len(groups) - 1:
                        squares(n)
            exps(len(groups) - 1)
            squares(len(groups) - 1)

        def gate_pool(pool):
            pool.wait_ge(dve_job, JV.done("scan", GB - 2))
            pool.memset(ST[:, :, 16:], 0.0).then_inc(s_bst, 1)
            for b in range(B):
                for n, group in enumerate(groups):
                    if b == group[0]:
                        pool.wait_ge(s_p, n + 1)
                gs = slice(b * GB, b * GB + GB)
                if b:
                    pool.wait_ge(s_o2, b)
                pool.tensor_tensor(O2[:, gs, :], XS[1][:, gs, :], PR[:, gs, 1:2].to_broadcast([P, GB, DK]), ALU.mult).then_inc(s_pl, 1)
                pool.tensor_tensor(O3, XS[3][:, gs, :], PR[:, gs, 3:4].to_broadcast([P, GB, DK]), ALU.mult).then_inc(s_pl, 1)
                pool.wait_ge(s_pl, 2 * b + 2)
                pool.tensor_tensor(O2[:, gs, :], O2[:, gs, :], O3, ALU.add).then_inc(s_o2, 1)

        @block.tensor
        def _(pe):
            def bank_a(*name):
                i = JA.next(*name)
                if i >= RING:
                    pe.wait_ge(act_job, i - RING + 1)
                return banks_a[i % RING]

            def bank_v(*name):
                i = JV.next(*name)
                if i >= RING:
                    pe.wait_ge(dve_job, i - RING + 1)
                return banks_v[i % RING]

            pe.wait_ge(s_w, 16 * NW)
            for b in range(B):
                bank = bank_a("xnT", b)
                for j in range(TB):
                    pe.wait_ge(s_ln, b * TB + j + 1)
                    mm = pe.transpose(bank[:, j * P:(j + 1) * P], xn[:, b * TB + j, :], ident[:, :])
                mm.then_inc(pe_a, 1)
            pe.wait_ge(s_wc, 2)
            pe.wait_ge(s_pad, 3)
            for b in range(B):
                bank = bank_a("v", b)
                pe.wait_ge(act_job, JA.done("xnT", b))
                for j in range(TAPS):
                    mm = pe.matmul(bank[:, :], WC[:, 2, j, :], xnT[:, b, j:j + L], start=j == 0, stop=j == TAPS - 1)
                mm.then_inc(pe_a, 1)
            pe.wait_ge(s_bw, 1)
            for b in range(B):
                bank = bank_v("beta", b)
                pe.matmul(bank[:, :], bw, xnT[:, b, TAPS - 1:], start=True, stop=True).then_inc(pe_v, 1)
            for b in range(B):
                bank = bank_a("vE", b)
                pe.wait_ge(act_job, JA.done("v", b))
                for j in range(TB):
                    t = b * TB + j
                    mm = pe.transpose(bank[:, j * P:(j + 1) * P], VT[:, t * P:(t + 1) * P], ident[:, :])
                mm.then_inc(pe_a, 1)
            for b in range(B):
                bank = bank_a("vR", b)
                pe.wait_ge(act_job, JA.done("vE", b))
                pe.matmul(bank[:, :], flip, v0[:, b * TB:(b + 1) * TB, :].rearrange("p t c -> p (t c)"),
                          start=True, stop=True).then_inc(pe_a, 1)
            pe.wait_ge(s_voz, 1)
            pe.wait_ge(s_vo, 32)
            for s in range(NSLAB):
                pe.wait_ge(s_t[s % NTR], 16 * (s // NTR + 1))
                for half in range(2):
                    bank = bank_v("fir", s, half)
                    for d in range(4):
                        for h in range(H):
                            mm = pe.matmul(bank[DK * h:DK * h + DK, d * P:(d + 1) * P],
                                           (vO, vE)[half][:, :, DK * h + 4 * s + d], TR[:, s % NTR, h, d, :],
                                           start=True, stop=True)
                    mm.then_inc(pe_v, 1)
            for b in range(B):
                for s in range(2):
                    bank = bank_a("kq", s, b)
                    for j in range(TAPS):
                        mm = pe.matmul(bank[:, :], WC[:, 1 - s, j, :], xnT[:, b, j:j + L], start=j == 0, stop=j == TAPS - 1)
                    mm.then_inc(pe_a, 1)
            for q in range(G // 8):
                bank = bank_v("kk", q)
                pe.wait_ge(act_job, JA.done("kq", 1, q // 2))
                for g in range(8 * q, 8 * q + 8):
                    for h in range(H):
                        e = slice(DK * h, DK * h + DK)
                        mm = pe.matmul(bank[e, (g % 8) * 64:(g % 8) * 64 + 64], KQ[e, g, 0, :],
                                       KQ[e, g, :, :].rearrange("p s c -> p (s c)"), start=True, stop=True)
                mm.then_inc(pe_v, 1)
            pe.wait_ge(s_msb, B)
            for q in range(C // 4):
                bank = bank_a("me", q)
                for j in range(4):
                    mm = pe.transpose(bank[:, j * P:(j + 1) * P], MS[:, :, 4 * q + j], ident[:, :])
                mm.then_inc(pe_a, 1)
            pe.wait_ge(s_el, 1)
            pe.wait_ge(s_elp, 1)
            for q in range(C // 4):
                bank = bank_a("tt", q)
                for j in range(4):
                    mm = pe.transpose(bank[:, j * P:(j + 1) * P], TIr[:, 4 * q + j, :], ident[:, :])
                mm.then_inc(pe_a, 1)
            pe.wait_ge(act_job, JA.done("tt", C // 4 - 1))
            for q in range(G // 8):
                bank = bank_a("uw", q)
                pe.wait_ge(s_vk, q // 2 + 1)
                for g in range(8 * q, 8 * q + 8):
                    for h in range(H):
                        e = slice(DK * h, DK * h + DK)
                        mm = pe.matmul(bank[e, (g % 8) * 64:(g % 8) * 64 + 64], TT[e, g, :],
                                       VK[e, g, :, :].rearrange("p s c -> p (s c)"), start=True, stop=True)
                mm.then_inc(pe_a, 1)
            for q in range(G // 8):
                pe.wait_ge(act_job, JA.done("uw", q))
                bank = bank_v("qa", q)
                for g in range(8 * q, 8 * q + 8):
                    for h in range(H):
                        e = slice(DK * h, DK * h + DK)
                        mm = pe.matmul(bank[e, (g % 8) * 64:(g % 8) * 64 + 64], VK[e, g, 1, :],
                                       AK[e, g, :, :].rearrange("p s c -> p (s c)"), start=True, stop=True)
                mm.then_inc(pe_v, 1)
                if q % 2 == 1:
                    bank = bank_a("ku", q // 2)
                    for g in range(8 * q - 8, 8 * q + 8):
                        for h in range(H):
                            e = slice(DK * h, DK * h + DK)
                            mm = pe.matmul(bank[e, (g % 16) * C:(g % 16 + 1) * C], AK[e, g, 1, :], VK[e, g, 0, :],
                                           start=True, stop=True)
                    mm.then_inc(pe_a, 1)
            pe.wait_ge(dve_job, JV.done("qa", G // 8 - 1))
            for i in range(1, GB - 1):
                bank = bank_v("scan", i)
                if i == 1:
                    pe.wait_ge(s_scan, 1)
                else:
                    pe.wait_ge(dve_job, JV.done("scan", i - 1))
                for b in range(B):
                    for h in range(H):
                        e = slice(DK * h, DK * h + DK)
                        mm = pe.matmul(bank[e, b * C:(b + 1) * C], AT[e, b * GB + i, :], SS[e, b * GB + i, :],
                                       start=True, stop=True)
                mm.then_inc(pe_v, 1)
            pe.wait_ge(dve_job, JV.done("scan", GB - 2))
            for b in range(B):
                bank = bank_v("dh", b)
                for i in range(GB):
                    g = b * GB + i
                    for h in range(H):
                        e = slice(DK * h, DK * h + DK)
                        o = bank[e, i * C:(i + 1) * C]
                        if i:
                            pe.matmul(o, KQ[e, g, 1, :], SS[e, g, :], start=True, stop=False)
                        mm = pe.matmul(o, AK[e, g, 0, :], VK[e, g, 0, :], start=i == 0, stop=True)
                mm.then_inc(pe_v, 1)
            gate_pe(pe, bank_a, bank_v)

        @block.sync
        def _(sp):
            xr = rows(x_in, D)
            for i in range(B):
                sp.dma_start(X[:, i * TB:(i + 1) * TB, :], xr[:, i * TB:(i + 1) * TB, :]).then_inc(s_x[i], 16)
            sp.dma_start(ident[:, :], cst["ident"]).then_inc(s_w, 16)
            sp.dma_start(flip, cst["flip"]).then_inc(s_w, 16)
            sp.dma_start(masks[:, :, :], cst["masks"]).then_inc(s_w, 16)
            sp.dma_start(WQKV, w["qkvT"]).then_inc(s_w, 16)
            sp.dma_start(CWB.rearrange("p s j c -> p (s j c)"),
                         bass.AP(tensor=w["cw"].tensor, offset=0, ap=[[0, P], [1, 12 * P]])).then_inc(s_w, 16)
            sp.dma_start(bwT, w["bT"]).then_inc(s_w, 16)
            sp.dma_start(w1x, w["w1xT"]).then_inc(s_w, 16)
            sp.dma_start(wo[:, :], w["oT"]).then_inc(s_w, 16)
            sp.dma_start(w2p[:, 0:4], w["w2T"]).then_inc(s_w, 16)
            sp.dma_start(hdr[:, 0:4], bass.AP(tensor=w["b2"].tensor, offset=0, ap=[[0, P], [1, 4]])).then_inc(s_w, 16)
            sp.dma_start(hdr[:, 4:5], bass.AP(tensor=w["temp"].tensor, offset=0, ap=[[0, P], [1, 1]])).then_inc(s_w, 16)
            for h in range(H):
                e = slice(DK * h, DK * h + DK)
                sp.dma_start(hdr[e, 5:6], bass.AP(tensor=w["res"].tensor, offset=h, ap=[[0, DK], [1, 1]])).then_inc(s_w, 16)
                sp.dma_start(hdr[e, 6:7], w["norm"]).then_inc(s_w, 16)
            sp.dma_start(hdr[:, 7:8], w["b1"]).then_inc(s_w, 16)
            sp.wait_ge(s_w1s, 1)
            for h in range(H):
                sp.dma_start(w1s[DK * h:DK * h + 16, h, :], w["w1sT"]).then_inc(s_w, 16)
            for s in range(NSLAB):
                if s >= NTR:
                    sp.wait_ge(pe_v, JV.done("fir", s - NTR, 1))
                src = bass.AP(tensor=w["fir"].tensor, offset=16 * s * 2 * 3 * KL,
                              ap=[[1, P], [3 * KL, 2 * 4 * H], [1, KL]])
                sp.dma_start(TR[:, s % NTR].rearrange("p h d (f m) -> p (h d f) m", f=2), src).then_inc(s_t[s % NTR], 16)
            sp.wait_ge(pe_v, JV.done("lg", B - 1))
            for b in range(B):
                sp.dma_start(XR[:, b * TB:(b + 1) * TB, :], xr[:, b * TB:(b + 1) * TB, :]).then_inc(s_x[b], 16)
            xo = rows(x_out, D)
            for b in range(B):
                sp.wait_ge(dve_job, JV.done("o", b))
                sp.dma_start(xo[:, b * TB:(b + 1) * TB, :], XR[:, b * TB:(b + 1) * TB, :]).then_inc(s_out, 16)
            sp.wait_ge(s_out, 16 * B)

        @block.gpsimd
        def _(pool):
            pool.memset(eps[:, 0:1], LN_EPS)
            pool.memset(eps[:, 1:2], 1e-6)
            pool.memset(eps[:, 2:3], 1.0)
            pool.memset(w2p[:, 4:], 0.0).then_inc(s_pad, 1)
            pool.memset(w1s[:, :, :], 0.0).then_inc(s_w1s, 1)
            pool.memset(xnT[:, :, 0:TAPS - 1], 0.0).then_inc(s_pad, 2)
            pool.wait_ge(s_w, 16 * NW)
            for s in range(3):
                for j in range(TAPS):
                    ins = pool.tensor_tensor(WC[:, s, j, :], WQKV[:, s, :], CWB[:, s, j, :], ALU.mult)
            ins.then_inc(s_wc, 2)
            pool.wait_ge(s_sd, 1)
            pool.wait_ge(s_wc, 2)
            pool.memset(vO[64:128, :, :].rearrange("p (b j) c -> p b j c", j=TB)[:, :, 0, :], 0.0).then_inc(s_voz, 1)
            pool.wait_ge(act_job, JA.done("vR", B - 1))
            pool.dma_start(vO[0:64, :, :], vE[64:128, :, :]).then_inc(s_vo, 16)
            pool.dma_start(vO[64:128, :, :].rearrange("p (b j) c -> p b j c", j=TB)[:, :, 1:, :],
                           vE[0:64, :, :].rearrange("p (b j) c -> p b j c", j=TB)[:, :, 0:TB - 1, :]).then_inc(s_vo, 16)
            pool.wait_ge(s_bk, 1)
            for b in range(B):
                gs = slice(b * GB, b * GB + GB)
                pool.wait_ge(dve_job, JV.done("kk", 2 * b + 1))
                pool.tensor_tensor(MS[:, gs, :], MS[:, gs, :], bk[:, 1, gs].to_broadcast([P, GB, C]),
                                   ALU.mult).then_inc(s_msb, 1)
            eliminate(pool, slice(3, 4), s_pool, s_elp)
            pool.wait_ge(s_el, 1)
            pool.wait_ge(s_elp, 1)
            pool.wait_ge(s_kh, 1)
            for b in range(B):
                gs = slice(b * GB, b * GB + GB)
                pool.tensor_tensor(VK[:, gs, 0, :], VH[:, gs, :], bk[:, 0, gs].to_broadcast([P, GB, C]), ALU.mult)
                pool.tensor_tensor(VK[:, gs, 1, :], AK[:, gs, 1, :], bk[:, 1, gs].to_broadcast([P, GB, C]),
                                   ALU.mult).then_inc(s_vk, 1)
            gate_pool(pool)

        @block.scalar
        def _(act):
            jobs = Jobs()

            def bank(name, *rest):
                i = jobs.next()
                assert JA.named[(name, *rest)] == i, (name, rest)
                act.wait_ge(pe_a, i + 1)
                return banks_a[i % RING]

            def copy(out, in_):
                return act.activation(out, in_, ACT.Copy)

            act.wait_ge(s_pad, 3)
            act.wait_ge(s_sd, 1)
            act.activation(rstd[:, :], mv[:, :, 1], ACT.Sqrt, bias=eps[:, 0:1]).then_inc(s_rs, 1)
            for b in range(B):
                copy(xnT[:, b, TAPS - 1:], bank("xnT", b)[:, :]).then_inc(act_job, 1)
            for b in range(B):
                act.activation(VT[:, b * L:(b + 1) * L], bank("v", b)[:, :], ACT.Silu).then_inc(act_job, 1)
            act.wait_ge(s_ln, NT)
            for name, dst in (("vE", v0), ("vR", vE)):
                for b in range(B):
                    copy(dst[:, b * TB:(b + 1) * TB, :].rearrange("p t c -> p (t c)"), bank(name, b)[:, :]).then_inc(act_job, 1)
            act.wait_ge(s_beta0, 1)
            act.activation(beta[:, :], beta[:, :], ACT.Sigmoid).then_inc(s_beta1, 1)
            act.wait_ge(pe_v, JV.done("fir", NSLAB - 1, 1))
            for b in range(B + 1):
                if b < B:
                    for s in range(2):
                        act.activation(KQ[:, b * GB:(b + 1) * GB, s, :],
                                       bank("kq", s, b)[:, :].rearrange("p (g c) -> p g c", c=C), ACT.Silu).then_inc(act_job, 1)
                if b:
                    act.wait_ge(s_kt, b)
                    act.activation(QKH[:, (b - 1) % 4], QKH[:, (b - 1) % 4], ACT.Square).then_inc(s_sq, 1)
            act.wait_ge(s_ss, 1)
            act.activation(rn[:, :, :], rn[:, :, :], ACT.Sqrt, bias=eps[:, 1:2]).then_inc(s_nrm, 1)

            for q in range(C // 4):
                copy(ME.rearrange("p h r c -> p (h r) c")[:, :, 4 * q:4 * q + 4].rearrange("p n c -> p c n"),
                     bank("me", q)[:, :].rearrange("p (c n) -> p c n", c=4)).then_inc(act_job, 1)
            for q in range(C // 4):
                copy(TT[:, :, 4 * q:4 * q + 4].rearrange("p g r -> p r g"),
                     bank("tt", q)[:, :].rearrange("p (r g) -> p r g", r=4)).then_inc(act_job, 1)
            def ku(b):
                copy(KQ[:, b * GB:(b + 1) * GB, 0, :], bank("ku", b)[:, :].rearrange("p (g c) -> p g c", c=C)).then_inc(act_job, 1)
            for q in range(G // 8):
                copy(VK[:, 8 * q:8 * q + 8, :, :].rearrange("p g s c -> p (g s c)"), bank("uw", q)[:, :]).then_inc(act_job, 1)
            for b in range(B):
                ku(b)
            gate_act(act, bank, copy)

        @block.vector
        def _(dve):
            jobs = Jobs()
            link_n = [0]

            def link(ins):
                link_n[0] += 1
                ins.then_inc(s_dve, 1)
                dve.wait_ge(s_dve, link_n[0])

            def bank(name, *rest):
                i = jobs.next()
                assert JV.named[(name, *rest)] == i, (name, rest)
                dve.wait_ge(pe_v, i + 1)
                return banks_v[i % RING]

            bc = lambda ap, n=GB: ap.to_broadcast([P, n, C])
            for b in range(B):
                dve.wait_ge(s_x[b], 16)
                for t in range(b * TB, b * TB + TB):
                    ins = dve.bn_stats(stats6[:, t, :], X[:, t, :])
                link(ins)
                for t in range(b * TB, b * TB + TB):
                    ins = dve.bn_aggr(mv[:, t, :], stats6[:, t, :])
            ins.then_inc(s_sd, 1)
            dve.wait_ge(s_rs, 1)
            link(dve.reciprocal(rstd[:, :], rstd[:, :]))
            for t in range(NT):
                dve.tensor_scalar(xn[:, t, :], X[:, t, :], mv[:, t, 0:1], rstd[:, t:t + 1], ALU.subtract, ALU.mult).then_inc(s_ln, 1)
            dve.wait_ge(s_w, 16 * NW)
            dve.tensor_copy(bw.rearrange("p (h r) -> p h r", h=H), bwT.to_broadcast([P, H, DK])).then_inc(s_bw, 1)
            for b in range(B):
                if b:
                    dve.wait_ge(dve_job, JV.done("beta", b - 1))
                link(dve.transpose(OSCR, bank("beta", b)[:, :]))
                dve.tensor_copy(beta[:, b * GB:(b + 1) * GB], OSCR.rearrange("p (g c) -> p g c", c=C)[:, :, 0]).then_inc(dve_job, 1)
            dve.wait_ge(dve_job, JV.done("beta", B - 1))
            dve.tensor_copy(beta[:, :], beta[:, :]).then_inc(s_beta0, 1)
            for b in range(B):
                dve.wait_ge(act_job, JA.done("v", b))
                dve.transpose(VH[:, b * GB:(b + 1) * GB, :].rearrange("p g d -> p (g d)"), VT[:, b * L:(b + 1) * L])
            dve.wait_ge(s_beta1, 1)
            dve.tensor_scalar(beta[:, :], beta[:, :], 1e-6, None, ALU.max).then_inc(s_beta, 1)
            dve.wait_ge(pe_a, JA.done("vR", B - 1))
            for s in range(NSLAB):
                for half in range(2):
                    src = bank("fir", s, half)[:, :].rearrange("p (d f m) -> p d f m", d=4, f=2)
                    for f in range(2):
                        dst = (LLG, LS)[f].rearrange("p (t r i) d -> p r d i t", r=2, i=2)
                        ins = dve.transpose(dst[:, half, 4 * s:4 * s + 4], src[:, :, f, :])
                    ins.then_inc(dve_job, 1)
            for b in range(B + 1):
                gs = slice(b * GB, b * GB + GB)
                if b < B:
                    dve.wait_ge(act_job, JA.done("kq", 1, b))
                    if b >= 4:
                        dve.wait_ge(s_rd, b - 3)
                    dve.transpose(QKH[:, b % 4, 0], KQ[:, gs, 0, :])
                    dve.transpose(QKH[:, b % 4, 1], KQ[:, gs, 1, :]).then_inc(s_kt, 1)
                if b:
                    dve.wait_ge(s_sq, b)
                    dve.tensor_reduce(rn[:, :, (b - 1) * GB:b * GB], QKH[:, (b - 1) % 4], AX.X, ALU.add).then_inc(s_rd, 1)
            dve.wait_ge(s_rd, B)
            dve.wait_ge(pe_a, JA.done("kq", 1, B - 1))
            for b in range(B):
                gs = slice(b * GB, b * GB + GB)
                ins = dve.transpose(AK[:, gs, 1, :], KQ[:, gs, 0, :])
                if b == 0:
                    ins.then_inc(s_ss, 1)
            ins.then_inc(s_kh, 1)
            dve.wait_ge(s_nrm, 1)
            link(dve.reciprocal(rn[:, :, :], rn[:, :, :]))
            link(dve.tensor_tensor(bk[:, 0, :], beta[:, :], rn[:, 0, :], ALU.mult))
            dve.tensor_tensor(bk[:, 1, :], bk[:, 0, :], rn[:, 0, :], ALU.mult).then_inc(s_bk, 1)
            for q in range(G // 8):
                gs = slice(8 * q, 8 * q + 8)
                kk = bank("kk", q)[:, :].rearrange("p (g s c) -> p g s c", g=8, s=2)
                dve.tensor_tensor(MS[:, gs, :], kk[:, :, 0, :], masks[:, 0:1, :].to_broadcast([P, 8, C]), ALU.mult)
                dve.tensor_tensor(AK[:, gs, 0, :], kk[:, :, 1, :], masks[:, 1:2, :].to_broadcast([P, 8, C]), ALU.mult).then_inc(dve_job, 1)
            dve.wait_ge(pe_a, JA.done("me", C // 4 - 1))
            link(dve.memset(reg(3), 0.0))
            for h in range(H):
                ins = dve.memset(reg(3)[:, h * C:h * C + (C - 1) * (P + 1) + 1:P + 1], 1.0)
            ins.then_inc(s_tz, 1)
            eliminate(dve, slice(0, 3), s_elim, s_el)
            for q in range(G // 8):
                gs = slice(8 * q, 8 * q + 8)
                qa = bank("qa", q)[:, :].rearrange("p (g s c) -> p g s c", g=8, s=2)
                dve.tensor_tensor(KQ[:, gs, 1, :], KQ[:, gs, 1, :], qa[:, :, 0, :], ALU.subtract)
                dve.tensor_tensor(AT[:, gs, :], masks[:, 2:3, :].to_broadcast([P, 8, C]), qa[:, :, 1, :], ALU.subtract).then_inc(dve_job, 1)
                if q == 0:
                    dve.wait_ge(dve_job, JV.done("kk", G // 8 - 1))
                for n in range(3 * q, 3 * q + 3):
                    k, b = (0, 1, 3)[n // 16], n % 8
                    gs = slice(b * GB, b * GB + GB)
                    if n % 16 < 8:
                        dve.tensor_reduce(S1[:, k, gs], XS[k][:, gs, :], AX.X, ALU.add)
                    else:
                        dve.tensor_reduce(MM[:, k, gs], XS[k][:, gs, :], AX.X, ALU.add, apply_absolute_value=True)
            S4 = SS.rearrange("p (b i) c -> p i b c", b=B)
            B4 = KQ[:, :, 0, :].rearrange("p (b i) c -> p i b c", b=B)
            dve.wait_ge(act_job, JA.done("ku", B - 1))
            dve.tensor_copy(S4[:, 1], B4[:, 0]).then_inc(s_scan, 1)
            for i in range(1, GB - 1):
                ps = bank("scan", i)[:, 0:B * C].rearrange("p (b c) -> p b c", c=C)
                dve.tensor_tensor(S4[:, i + 1], ps, B4[:, i], ALU.add).then_inc(dve_job, 1)
                for n in range(2 * (i - 1), min(2 * i, 3 * B)):
                    k, b = (0, 1, 3)[n // B], n % B
                    gs = slice(b * GB, b * GB + GB)
                    dve.wait_ge(s_sqx, n // B + 1)
                    ins = dve.tensor_reduce(S2[:, k, gs], SQX[k][:, gs, :], AX.X, ALU.add)
                    if k != 1 and b == B - 1:
                        ins.then_inc(s_r2, 1)
            STk = ST[:, :, 0:16].rearrange("p g (k s) -> p s k g", s=4)
            dve.wait_ge(dve_job, JV.done("scan", GB - 2))
            for b in range(B + 2):
                if b < B:
                    gs = slice(b * GB, b * GB + GB)
                    dve.tensor_tensor(DH[:, gs, :], bank("dh", b)[:, :].rearrange("p (g c) -> p g c", c=C), bc(rn[:, 1, gs]),
                                      ALU.mult).then_inc(dve_job, 1)
                    dve.wait_ge(dve_job, JV.done("dh", b))
                    dve.tensor_reduce(S1[:, 2, gs], DH[:, gs, :], AX.X, ALU.add)
                    link(dve.tensor_reduce(MM[:, 2, gs], DH[:, gs, :], AX.X, ALU.add, apply_absolute_value=True))
                if 1 <= b <= B:
                    gs = slice((b - 1) * GB, b * GB)
                    dve.wait_ge(s_sqx, 3 + b)
                    dve.tensor_reduce(S2[:, 2, gs], SQX[2][:, gs, :], AX.X, ALU.add).then_inc(s_st, 1)
                    dve.tensor_scalar(STk[:, 0, :, gs], S1[:, :, gs], 1.0 / DK, None, ALU.mult)
                    link(dve.tensor_scalar(STk[:, 2, :, gs], MM[:, :, gs], 1.0 / DK, None, ALU.mult))
                    link(dve.tensor_tensor(MM[:, :, gs], STk[:, 0, :, gs], STk[:, 0, :, gs], ALU.mult))
                    link(dve.scalar_tensor_tensor(STk[:, 1, :, gs], S2[:, :, gs], 1.0 / DK, MM[:, :, gs], ALU.mult, ALU.subtract))
                if b >= 2:
                    gs = slice((b - 2) * GB, (b - 1) * GB)
                    if b == 2:
                        dve.wait_ge(s_bst, 1)
                    dve.wait_ge(s_l2, b - 1)
                    dve.transpose(STT[:, gs, :], ST[:, gs, :]).then_inc(s_stt, 1)
            dve.wait_ge(s_hdr2, 4)
            link(dve.tensor_scalar(hdr[:, 10:11], hdr[:, 4:5], 0.0, hdr[:, 8:9], ALU.max, ALU.add))
            dve.reciprocal(hdr[:, 10:11], hdr[:, 10:11])
            dve.tensor_scalar(wo[:, :], wo[:, :], hdr[:, 6:7], None, ALU.mult)
            dve.wait_ge(s_stt, B)

            def shares(n):
                b0, b1 = groups[n]
                for b in range(b0, b1):
                    gs = slice(b * GB, b * GB + GB)
                    dve.transpose(LG[:, gs, :].rearrange("p g s -> p (g s)"), bank("lg", b)[:, :]).then_inc(dve_job, 1)
                    dve.wait_ge(dve_job, JV.done("lg", b))
                    ins = dve.tensor_tensor(PR[:, gs, :], LG[:, gs, 0:4], hdr[:, None, 0:4].to_broadcast([P, GB, 4]), ALU.add)
                link(ins)
                gs = slice(b0 * GB, b1 * GB)
                pr, r1, r2 = PR[:, gs, :], R1[:, gs], R2[:, gs]
                shape = [P, (b1 - b0) * GB, 4]
                link(dve.tensor_reduce(r1, pr, AX.X, ALU.max))
                dve.tensor_tensor(pr, pr, r1.to_broadcast(shape), ALU.subtract).then_inc(s_e, 1)
                dve.wait_ge(s_ex, n + 1)
                for again in range(2):
                    link(dve.tensor_reduce(r1, pr, AX.X, ALU.add))
                    link(dve.reciprocal(r2, r1))
                    link(dve.tensor_tensor(pr, pr, r2.to_broadcast(shape), ALU.mult))
                    if not again:
                        link(dve.tensor_scalar(pr, pr, PROB_FLOOR, None, ALU.max))
                dve.tensor_scalar(pr[:, :, 0], pr[:, :, 0], hdr[:, 9:10], None, ALU.add).then_inc(s_p, 1)
                dve.wait_ge(s_p, n + 1)

            def mix(n):
                b0, b1 = groups[n]
                for b in range(b0, b1):
                    gs = slice(b * GB, b * GB + GB)
                    dve.tensor_tensor(OH[:, gs, :], XS[0][:, gs, :], bc(PR[:, gs, 0:1]), ALU.mult)
                    link(dve.tensor_tensor(LG[:, gs, :], XS[2][:, gs, :], bc(PR[:, gs, 2:3]), ALU.mult))
                    link(dve.tensor_tensor(OH[:, gs, :], OH[:, gs, :], LG[:, gs, :], ALU.add))
                    dve.wait_ge(s_o2, b + 1)
                    dve.tensor_tensor(OH[:, gs, :], OH[:, gs, :], O2[:, gs, :], ALU.add).then_inc(s_mix, 1)
                for b in range(b0, b1):
                    gs = slice(b * GB, b * GB + GB)
                    dve.wait_ge(s_o, b + 1)
                    ins = dve.tensor_reduce(R1[:, gs], OSQ[:, gs, :], AX.X, ALU.add)
                ins.then_inc(s_ms, 1)
                dve.wait_ge(s_rms, n + 1)
                link(dve.reciprocal(R2[:, b0 * GB:b1 * GB], R1[:, b0 * GB:b1 * GB]))
                for b in range(b0, b1):
                    gs = slice(b * GB, b * GB + GB)
                    link(dve.tensor_tensor(OH[:, gs, :], OH[:, gs, :], bc(R2[:, gs]), ALU.mult))
                    dve.transpose(OT[:, b * L:(b + 1) * L], OH[:, gs, :].rearrange("p g d -> p (g d)")).then_inc(s_oT, 1)

            for n in range(len(groups)):
                shares(n)
                mix(n)
            for b in range(B):
                dve.wait_ge(s_x[b], 32)
                xb = XR[:, b * TB:(b + 1) * TB, :].rearrange("p t d -> p (t d)")
                dve.tensor_tensor(xb, xb, bank("o", b)[:, :], ALU.add).then_inc(dve_job, 1)


E_ = 32
F = 128
CAP = -(-T * 5 // (4 * E_))
SLOTS = E_ * CAP
CH = 4
CT = CH * CAP // P


def moe(nc, sems, s_x, x0, x_in, x_out, w, cst, xbuf, ybuf, tag, first):
    ctx = ExitStack()
    with ctx:
        sb = lambda name, shape, dt=F32: ctx.enter_context(nc.sbuf_tensor(f"{tag}_{name}", shape, dt))
        sem = lambda name: sems.enter_context(nc.semaphore(f"{tag}_{name}"))
        X, XT = sb("X", [P, NT, D]), sb("XT", [P, NT, D])
        tr = sb("tr", [P, SLOTS])
        wg, wu, wd = (sb(n, [P, E_, F]) for n in ("wg", "wu", "wd"))
        BR = sb("BR", [P, SLOTS // P, D])
        YA, YB = sb("YA", [P, E_, D]), sb("YB", [CAP - P, E_, D])
        GY = BR[:, 0:NT, :]
        wr, ident, eps = sb("wr", [P, E_]), sb("ident", [P, P]), sb("eps", [P, 1])
        tri, ones = sb("tri", [P, P], BF16), sb("ones", [P, P], BF16)
        trif = sb("trif", [P, P])
        mv, stats6, rstd = sb("mv", [P, NT, 2]), sb("stats6", [P, NT, 6]), sb("rstd", [P, NT])
        rank, dump = sb("rank", [P, E_]), sb("dump", [P, NT])
        LG, EX = sb("LG", [P, NT, E_]), sb("EX", [P, NT, E_])
        OH, PO = sb("OH", [P, NT, E_], BF16), sb("PO", [P, NT, E_], BF16)
        row = sb("row", [P, 8, NT])
        mx, best, pos, slot, acc, gate, sidx, gidx = (row[:, i, :] for i in range(8))
        si, gi = sb("si", [P, NT], I32), sb("gi", [P, NT], I32)
        SG, hT = sb("SG", [P, 2, CAP]), sb("hT", [P, 4, CAP])
        zero = sb("zero", [P, 1280])
        banks_a = [ctx.enter_context(nc.psum_tensor(f"{tag}_pa{i}", [P, 512], F32)) for i in range(RING)]
        banks_v = [ctx.enter_context(nc.psum_tensor(f"{tag}_pv{i}", [P, 512], F32)) for i in range(RING)]
        pe_a, pe_v, act_job, dve_job = (sem(n) for n in ("pe_a", "pe_v", "act_job", "dve_job"))
        s_gy = [sem(f"gy{b}") for b in range(B)]
        s_c, s_w, s_z, s_zf, s_sd, s_rs, s_ln, s_dve, s_bf, s_lg, s_ex, s_oh, s_idx, s_sc, s_sg, s_y, s_xs, s_out = (
            sem(n) for n in ("c", "w", "z", "zf", "sd", "rs", "ln", "dve", "bf", "lg", "ex", "oh", "idx", "sc", "sg", "y", "xs", "out"))
        JA, JV = Jobs(), Jobs()
        block = ctx.enter_context(nc.Block())

        @block.tensor
        def _(pe):
            def bank_a(*name):
                i = JA.next(*name)
                if i >= RING:
                    pe.wait_ge(act_job, i - RING + 1)
                return banks_a[i % RING]

            def bank_v(*name):
                i = JV.next(*name)
                if i >= RING:
                    pe.wait_ge(dve_job, i - RING + 1)
                return banks_v[i % RING]

            pe.wait_ge(s_c, 16 * 5)
            for b in range(B):
                bank = bank_a("xT", b)
                for j in range(TB):
                    pe.wait_ge(s_ln, b * TB + j + 1)
                    mm = pe.transpose(bank[:, j * P:(j + 1) * P], XT[:, b * TB + j, :], ident[:, :])
                mm.then_inc(pe_a, 1)
            for k in range(2):
                bank = bank_v("lg", k)
                for t in range(16 * k, 16 * k + 16):
                    if t % TB == 0:
                        pe.wait_ge(act_job, JA.done("xT", t // TB))
                    mm = pe.matmul(bank[:, (t % 16) * E_:(t % 16 + 1) * E_], tr[:, t * P:(t + 1) * P], wr[:, :], start=True, stop=True)
                mm.then_inc(pe_v, 1)
            pe.wait_ge(s_oh, 1)
            pe.wait_ge(s_bf, 2)
            for k in range(2):
                bank = bank_v("pos", k)
                ts = slice(16 * k, 16 * k + 16)
                pe.matmul(bank[:, :], tri[:, :], OH[:, ts, :].rearrange("p t e -> p (t e)"), start=True, stop=False)
                pe.matmul(bank[:, :], ones[:, :], PO[:, ts, :].rearrange("p t e -> p (t e)"), start=False, stop=True).then_inc(pe_v, 1)
            pe.wait_ge(s_w, 16 * 3)

            def down(e):
                if e % 2 == 0:
                    down.bank = bank_a("y", e // 2)
                o = (e % 2) * 2 * D
                pe.wait_ge(dve_job, JV.done("gu", e))
                pe.matmul(down.bank[:, o:o + D], hT[:, e % 4, 0:P], wd[:, e, :], start=True, stop=True)
                mm = pe.matmul(down.bank[0:CAP - P, o + D:o + 2 * D], hT[:, e % 4, P:CAP], wd[:, e, :], start=True, stop=True)
                if e % 2:
                    mm.then_inc(pe_a, 1)

            def turn(c):
                pe.wait_ge(s_x[c], x0 + 32)
                for k in range(0, CT, 4):
                    bank = bank_a("bt", c, k)
                    for j in range(k, min(k + 4, CT)):
                        mm = pe.transpose(bank[:, (j - k) * P:(j - k + 1) * P], BR[:, CT * c + j, :], ident[:, :])
                    mm.then_inc(pe_a, 1)

            turn(0)
            for e in range(E_):
                if e % CH == 1 and e + CH < E_:
                    turn(e // CH + 1)
                if e % CH == 0:
                    pe.wait_ge(act_job, JA.done("bt", e // CH, CT - CT % 4 if CT % 4 else CT - 4))
                bank = bank_v("gu", e)
                pe.matmul(bank[:, 0:CAP], wg[:, e, :], tr[:, e * CAP:(e + 1) * CAP], start=True, stop=True)
                pe.matmul(bank[:, CAP:2 * CAP], wu[:, e, :], tr[:, e * CAP:(e + 1) * CAP], start=True, stop=True).then_inc(pe_v, 1)
                if e:
                    down(e - 1)
            down(E_ - 1)

        @block.sync
        def _(sp):
            xr = rows(x_in, D)
            for b in range(B):
                sp.dma_start(X[:, b * TB:(b + 1) * TB, :], xr[:, b * TB:(b + 1) * TB, :]).then_inc(s_x[b], 16)
            for dst, src in ((ident, "ident"), (trif, "tri"), (rank, "rank"), (dump, "dump")):
                sp.dma_start(dst[:, :], cst[src]).then_inc(s_c, 16)
            sp.dma_start(wr[:, :], w["router"]).then_inc(s_c, 16)
            if first:
                sp.wait_ge(s_z, 2)
                sp.dma_start(xbuf[0:SLOTS, :].rearrange("(p r) d -> p (r d)", p=P)[:, 0:2560],
                             zero[:, None, :].to_broadcast([P, 2, 1280])).then_inc(s_zf, 16)
                sp.dma_start(xbuf[0:SLOTS, :].rearrange("(p r) d -> p (r d)", p=P)[:, 2560:5120],
                             zero[:, None, :].to_broadcast([P, 2, 1280])).then_inc(s_zf, 16)
                sp.dma_start(ybuf[SLOTS:SLOTS + 1, :], zero[0:1, 0:D]).then_inc(s_zf, 16)
            for dst, src in ((wg, "gate"), (wu, "up"), (wd, "down")):
                sp.dma_start(dst[:, :, :], w[src].rearrange("e h f -> h e f")).then_inc(s_w, 16)
            sp.wait_ge(s_sc, 16 * NT)
            for c in range(E_ // CH):
                sp.dma_start(BR[:, CT * c:CT * c + CT, :],
                             xbuf[c * CT * P:(c + 1) * CT * P, :].rearrange("(t p) d -> p t d", p=P)).then_inc(s_x[c], 16)
            yr = ybuf[0:SLOTS, :].rearrange("(e s) d -> s e d", s=CAP)
            for c in range(E_ // CH):
                es = slice(CH * c, CH * c + CH)
                sp.wait_ge(act_job, JA.done("y", (CH * c + CH) // 2 - 1))
                sp.dma_start(yr[0:P, es, :], YA[:, es, :]).then_inc(s_y, 16)
                sp.dma_start(yr[P:CAP, es, :], YB[:, es, :]).then_inc(s_y, 16)
            xo = rows(x_out, D)
            for b in range(B):
                sp.wait_ge(s_xs, b + 1)
                sp.dma_start(xo[:, b * TB:(b + 1) * TB, :], X[:, b * TB:(b + 1) * TB, :]).then_inc(s_out, 16)
            sp.wait_ge(s_out, 16 * B)

        @block.gpsimd
        def _(pool):
            pool.memset(eps[:, :], LN_EPS).then_inc(s_z, 1)
            if first:
                pool.memset(zero[:, :], 0.0).then_inc(s_z, 1)
            pool.memset(ones[:, :], 1.0).then_inc(s_bf, 1)
            pool.wait_ge(s_c, 16 * 5)
            pool.tensor_copy(tri[:, :], trif[:, :]).then_inc(s_bf, 1)
            if first:
                pool.wait_ge(s_zf, 16 * 3)
            pool.wait_ge(s_idx, 1)
            for t in range(NT):
                pool.indirect_dma_start(xbuf, bass.IndirectOffsetOnAxis(ap=si[:, t:t + 1], axis=0), XT[:, t, :], None).then_inc(s_sc, 16)
            pool.wait_ge(s_y, 16 * 2 * E_ // CH)
            for t in range(NT):
                pool.indirect_dma_start(GY[:, t, :], None, ybuf, bass.IndirectOffsetOnAxis(ap=gi[:, t:t + 1], axis=0)).then_inc(s_gy[t // TB], 16)

        @block.scalar
        def _(act):
            jobs = Jobs()

            def bank(name, *rest):
                i = jobs.next()
                assert JA.named[(name, *rest)] == i, (name, rest)
                act.wait_ge(pe_a, i + 1)
                return banks_a[i % RING]

            def copy(out, in_):
                return act.activation(out, in_, ACT.Copy)

            act.wait_ge(s_z, 1)
            act.wait_ge(s_sd, 1)
            act.activation(rstd[:, :], mv[:, :, 1], ACT.Sqrt, bias=eps[:, 0:1]).then_inc(s_rs, 1)
            for b in range(B):
                copy(tr[:, b * L:(b + 1) * L], bank("xT", b)[:, :]).then_inc(act_job, 1)
            act.wait_ge(s_lg, 1)
            act.activation(EX[:, :, :], LG[:, :, :], ACT.Exp).then_inc(s_ex, 1)

            def turn(c):
                for k in range(0, CT, 4):
                    n = min(4, CT - k) * P
                    if c == 0 and k == 0:
                        act.wait_ge(pe_v, JV.done("lg", 1))
                    copy(tr[:, (c * CT + k) * P:(c * CT + k) * P + n], bank("bt", c, k)[:, 0:n]).then_inc(act_job, 1)

            def y(q):
                src = bank("y", q)[:, :].rearrange("p (e s d) -> p e s d", e=2, s=2)
                copy(YA[:, 2 * q:2 * q + 2, :], src[:, :, 0, :])
                copy(YB[:, 2 * q:2 * q + 2, :], src[0:CAP - P, :, 1, :]).then_inc(act_job, 1)

            turn(0)
            for e in range(E_):
                if e >= 2 and e % 2 == 0:
                    y(e // 2 - 1)
                if e % CH == 1 and e + CH < E_:
                    turn(e // CH + 1)
                act.wait_ge(pe_v, JV.done("gu", e))
                if e >= 2:
                    act.wait_ge(dve_job, JV.done("gu", e - 2))
                act.activation(SG[:, e % 2, :], banks_v[JV.named[("gu", e)] % RING][:, 0:CAP], ACT.Silu).then_inc(s_sg, 1)
            y(E_ // 2 - 1)

        @block.vector
        def _(dve):
            jobs = Jobs()
            link_n = [0]

            def link(ins):
                link_n[0] += 1
                ins.then_inc(s_dve, 1)
                dve.wait_ge(s_dve, link_n[0])

            def bank(name, *rest):
                i = jobs.next()
                assert JV.named[(name, *rest)] == i, (name, rest)
                dve.wait_ge(pe_v, i + 1)
                return banks_v[i % RING]

            for b in range(B):
                dve.wait_ge(s_x[b], x0 + 16)
                for t in range(b * TB, b * TB + TB):
                    ins = dve.bn_stats(stats6[:, t, :], X[:, t, :])
                link(ins)
                for t in range(b * TB, b * TB + TB):
                    ins = dve.bn_aggr(mv[:, t, :], stats6[:, t, :])
            ins.then_inc(s_sd, 1)
            dve.wait_ge(s_rs, 1)
            link(dve.reciprocal(rstd[:, :], rstd[:, :]))
            for t in range(NT):
                dve.tensor_scalar(XT[:, t, :], X[:, t, :], mv[:, t, 0:1], rstd[:, t:t + 1], ALU.subtract, ALU.mult).then_inc(s_ln, 1)
            dve.wait_ge(s_c, 16 * 5)
            for k in range(2):
                ts = slice(16 * k, 16 * k + 16)
                src = bank("lg", k)[:, :].rearrange("p (t e) -> p t e", e=E_)
                link(dve.tensor_reduce(mx[:, ts], src, AX.X, ALU.max))
                dve.tensor_tensor(LG[:, ts, :], src, mx[:, ts].to_broadcast([P, 16, E_]), ALU.subtract).then_inc(dve_job, 1)
            dve.wait_ge(dve_job, JV.done("lg", 1))
            dve.tensor_scalar(LG[:, 0:1, 0:1], LG[:, 0:1, 0:1], 0.0, None, ALU.add).then_inc(s_lg, 1)
            dve.wait_ge(s_lg, 1)
            dve.wait_ge(s_ex, 1)
            link(dve.tensor_reduce(gate, EX[:, :, :], AX.X, ALU.add))
            dve.reciprocal(gate, gate)
            link(dve.tensor_scalar(LG[:, :, :], LG[:, :, :], 0.0, None, ALU.is_equal))
            link(dve.tensor_tensor(LG[:, :, :], LG[:, :, :], rank[:, None, :].to_broadcast([P, NT, E_]), ALU.mult))
            link(dve.tensor_reduce(best, LG[:, :, :], AX.X, ALU.max))
            dve.memset(PO[:, 0, :], 0.0)
            link(dve.tensor_tensor(OH[:, :, :], LG[:, :, :], best.to_broadcast([P, NT, E_]), ALU.is_equal))
            for t in range(1, NT):
                ins = dve.tensor_tensor(PO[:, t, :], PO[:, t - 1, :], OH[:, t - 1, :], ALU.add)
                if t < NT - 1:
                    link(ins)
            ins.then_inc(s_oh, 1)
            for k in range(2):
                ts = slice(16 * k, 16 * k + 16)
                dve.tensor_tensor(EX[:, ts, :], bank("pos", k)[:, :].rearrange("p (t e) -> p t e", e=E_), OH[:, ts, :], ALU.mult).then_inc(dve_job, 1)
            dve.wait_ge(dve_job, JV.done("pos", 1))
            link(dve.tensor_reduce(pos, EX[:, :, :], AX.X, ALU.add))
            dve.tensor_scalar(acc, pos, float(CAP), None, ALU.is_le)
            link(dve.scalar_tensor_tensor(slot, best, -float(CAP), pos, ALU.mult, ALU.add))
            link(dve.tensor_scalar(slot, slot, float(SLOTS - 1), None, ALU.add))
            dve.tensor_tensor(sidx, slot, dump[:, :], ALU.subtract)
            link(dve.tensor_scalar(gidx, slot, -float(SLOTS), None, ALU.add))
            dve.tensor_tensor(sidx, sidx, acc, ALU.mult)
            dve.tensor_tensor(gate, gate, acc, ALU.mult)
            link(dve.tensor_tensor(gidx, gidx, acc, ALU.mult))
            link(dve.tensor_tensor(sidx, sidx, dump[:, :], ALU.add))
            dve.tensor_scalar(gi[:, :], gidx, float(SLOTS), None, ALU.add)
            dve.tensor_copy(si[:, :], sidx).then_inc(s_idx, 1)
            for b in range(B):
                ts = slice(b * TB, b * TB + TB)
                ins = dve.tensor_tensor(X[:, ts, :], X[:, ts, :], XT[:, ts, :], ALU.add)
            link(ins)
            for e in range(E_):
                src = bank("gu", e)
                dve.wait_ge(s_sg, e + 1)
                if e >= 4:
                    dve.wait_ge(pe_a, JA.done("y", (e - 4) // 2))
                dve.tensor_tensor(hT[:, e % 4, :], src[:, CAP:2 * CAP], SG[:, e % 2, :], ALU.mult).then_inc(dve_job, 1)
            for b in range(B):
                dve.wait_ge(s_gy[b], 16 * TB)
                for t in range(b * TB, b * TB + TB):
                    ins = dve.scalar_tensor_tensor(X[:, t, :], GY[:, t, :], gate[:, t:t + 1], X[:, t, :], ALU.mult, ALU.add)
                ins.then_inc(s_xs, 1)


HB, DB = 16, D // 16
CLAMP = 1e5
Q_PART = (0, 0, 1, 1, 0, 2)
K_PART = (0, 1, 0, 1, 2, 0)
NTERM = len(Q_PART)
MAXROW = NTERM * DB
SEC = (0, 512, 896, 1152)
PW = 1280


def attn_b(nc, sems, s_x, x0, x_in, x_out, w, cst, stack):
    ctx = ExitStack()
    with ctx:
        sb = lambda name, shape, dt=F32: ctx.enter_context(nc.sbuf_tensor(f"b_{name}", shape, dt))
        sem = lambda name: sems.enter_context(nc.semaphore(f"b_{name}"))
        X = sb("X", [P, NT, D])
        xn, xnT = sb("xn", [P, 2 * TB, D]), sb("xnT", [P, 2, L])
        wp = sb("wp", [P, 5, D])
        rope = sb("rope", [P, 4, L])
        WO = sb("WO", [P, D])
        ident, eps = sb("ident", [P, P]), sb("eps", [P, 1])
        identb, mqf, mq, mk = sb("identb", [P, P], BF16), sb("mqf", [P, 2, P]), sb("mq", [P, P], BF16), sb("mk", [P, P], BF16)
        mv, stats6, rstd = sb("mv", [P, NT, 2]), sb("stats6", [P, NT, 6]), sb("rstd", [P, NT])
        RT = sb("RT", [P, 2, 2, L])
        PS = sb("PS", [P, 2, 2, 3, L], BF16)
        QS, KS = sb("QS", [P, 2, HB, L], BF16), sb("KS", [P, 2, HB, L], BF16)
        zr = sb("zr", [3, L], BF16)
        VX = sb("VX", [P, 3, TB, HB, 32])
        PB = sb("PB", [P, 8, PW])
        MX, MR = sb("MX", [P, TB, HB]), sb("MR", [P, TB, HB])
        N3 = sb("N3", [P, TB, 3, HB], BF16)
        NMT = sb("NMT", [3 * HB, L], BF16)
        OT, RC, OTK, OTT = sb("OT", [P, 2, L]), sb("RC", [P, TB, 4]), sb("OTK", [P, TB, D]), sb("OTT", [P, L])
        banks_a = [ctx.enter_context(nc.psum_tensor(f"b_pa{i}", [P, 512], F32)) for i in range(RING)]
        banks_v = [ctx.enter_context(nc.psum_tensor(f"b_pv{i}", [P, 512], F32)) for i in range(RING)]
        pe_a, pe_v, act_job, dve_job = (sem(n) for n in ("pe_a", "pe_v", "act_job", "dve_job"))
        (s_c, s_set, s_cb, s_sd, s_rs, s_ln, s_dve, s_pool, s_ps, s_nm, s_cp, s_cd, s_qz, s_vx, s_out) = (
            sem(n) for n in ("c", "set", "cb", "sd", "rs", "ln", "dve", "pool", "ps", "nm", "cp", "cd", "qz", "vx", "out"))
        s_st = [sem(f"st{i}") for i in range(2)]
        s_ld = [sem(f"ld{i}") for i in range(2)]
        s_mr = [sem(f"mr{i}") for i in range(2)]
        JA, JV = Jobs(), Jobs()
        NC = 5
        LOADS = 16 * (2 * NTERM + 1)

        amax = [(q, h, n) for q, n in ((0, 4), (1, 2), (2, 1), (3, 1)) for h in range(0, HB, n)]

        def steps():
            yield "project", 0, 0
            yield "project", 1, 0
            for i in range(len(amax)):
                yield "max", 0, i
            yield "take", 0, 0
            for b in range(B):
                for h in range(HB):
                    yield "probs", b, h
                    if b + 1 < B and 3 <= h < 13:
                        for i in range(len(amax) * (h - 3) // 10, len(amax) * (h - 2) // 10):
                            yield "max", b + 1, i
                    if h == 12 and b + 1 < B:
                        yield "take", b + 1, 0
                    if h == 8 and b + 2 < B:
                        yield "project", b + 2, 0
                    if h % 4 == 1 and h > 4:
                        yield "values", b, h // 4 - 1
                    if h % 4 == 3 and h > 4:
                        yield "norm", b, h // 4 - 1
                yield "values", b, 3
                yield "norm", b, 3
                yield "out", b, 0

        def load(sp, b):
            s = b % 2
            sp.wait_ge(s_st[s], 32 * (b // 2 + 1))
            sp.wait_ge(s_set, 3)
            sp.wait_ge(s_qz, 1)
            if b >= 2:
                sp.wait_ge(pe_a, JA.done("sc", b - 2, HB - 1, 2))
            for t in range(NTERM):
                e = slice(DB * t, DB * t + DB)
                for k, (S, part) in enumerate(((QS, Q_PART), (KS, K_PART))):
                    sp.dma_start(S[e, s, :, :], stack[s, k, part[t]].rearrange("(h d) t -> d h t", d=DB)).then_inc(s_ld[s], 16)
            sp.dma_start(QS[MAXROW:MAXROW + 3, s, :, :], zr[:, None, :].to_broadcast([3, HB, L])).then_inc(s_ld[s], 16)

        block = ctx.enter_context(nc.Block())

        @block.tensor
        def _(pe):
            def bank_a(*name):
                i = JA.next(*name)
                if i >= RING:
                    pe.wait_ge(act_job, i - RING + 1)
                return banks_a[i % RING]

            def bank_v(*name):
                i = JV.next(*name)
                if i >= RING:
                    pe.wait_ge(dve_job, i - RING + 1)
                return banks_v[i % RING]

            pe.wait_ge(s_c, 16 * NC)
            pe.wait_ge(s_cb, 3)
            for step, b, i in steps():
                s = b % 2
                if step == "project":
                    bank = bank_a("xT", b)
                    for j in range(TB):
                        pe.wait_ge(s_ln, b * TB + j + 1)
                        mm = pe.transpose(bank[:, j * P:(j + 1) * P], xn[:, s * TB + j, :], ident[:, :])
                    mm.then_inc(pe_a, 1)
                    pe.wait_ge(act_job, JA.done("xT", b))
                    for k in range(4):
                        bank = bank_v("qk", b, k)
                        pe.matmul(bank[:, :], wp[:, k, :], xnT[:, s, :], start=True, stop=True).then_inc(pe_v, 1)
                    bank = bank_a("v", b)
                    for j in range(TB):
                        mm = pe.matmul(bank[:, j * P:(j + 1) * P], xnT[:, s, j * P:(j + 1) * P], wp[:, 4, :], start=True, stop=True)
                    mm.then_inc(pe_a, 1)
                elif step == "max":
                    q, h0, n = amax[i]
                    if i == 0:
                        pe.wait_ge(s_ld[s], LOADS * (b // 2 + 1))
                    bank = bank_v("max", b, i)
                    wd = (q + 1) * P
                    for h in range(h0, h0 + n):
                        o = (h - h0) * wd
                        pe.matmul(bank[:, o:o + wd], QS[:, s, h, q * P:wd], KS[:, s, h, 0:wd], start=True, stop=False)
                        mm = pe.matmul(bank[:, o + q * P:o + wd], identb[:, :], mq[:, :], start=False, stop=True)
                    mm.then_inc(pe_v, 1)
                elif step == "take":
                    bank = bank_a("nm", b)
                    pe.wait_ge(s_nm, b + 1)
                    for j in range(TB):
                        mm = pe.transpose(bank[:, 0:256].bitcast(BF16)[0:3 * HB, j * P:(j + 1) * P],
                                          N3[:, j, :, :].rearrange("p a h -> p (a h)"), identb[:, :])
                    mm.then_inc(pe_a, 1)
                elif step == "probs":
                    h = i
                    if h == 0:
                        pe.wait_ge(s_mr[s], 48 * (b // 2 + 1))
                    for part in ((0,), (1,), (2, 3)):
                        bank = bank_a("sc", b, h, part[0])
                        o = 0
                        for kt in part:
                            n = L - kt * P
                            pe.matmul(bank[:, o:o + n], KS[:, s, h, kt * P:(kt + 1) * P], QS[:, s, h, kt * P:L], start=True, stop=False)
                            mm = pe.matmul(bank[:, o:o + P], identb[:, :], mk[:, :], start=False, stop=True)
                            o += n
                        mm.then_inc(pe_a, 1)
                elif step == "values":
                    bank = bank_a("pv", b, i)
                    n = b * HB + 4 * i + 4
                    pe.wait_ge(s_cd, n)
                    pe.wait_ge(s_cp, n)
                    for kt in range(TB):
                        for j in range(4):
                            h = 4 * i + j
                            mm = pe.matmul(bank[32 * j:32 * j + 32, kt * P:L], VX[:, b % 3, kt, h, :],
                                           PB[:, h % 8, SEC[kt]:SEC[kt] + L - kt * P], start=kt == 0, stop=kt == TB - 1)
                    mm.then_inc(pe_a, 1)
                elif step == "norm":
                    bank = bank_v("den", b, i)
                    pe.wait_ge(act_job, JA.done("pv", b, i))
                    for j in range(TB):
                        mm = pe.transpose(bank[:, j * P:(j + 1) * P], OT[:, i % 2, j * P:(j + 1) * P], ident[:, :])
                    mm.then_inc(pe_v, 1)
                else:
                    bank = bank_a("oT", b)
                    pe.wait_ge(dve_job, JV.done("den", b, 3))
                    for j in range(TB):
                        mm = pe.transpose(bank[:, j * P:(j + 1) * P], OTK[:, j, :], ident[:, :])
                    mm.then_inc(pe_a, 1)
                    bank = bank_v("out", b)
                    pe.wait_ge(act_job, JA.done("oT", b))
                    for j in range(TB):
                        mm = pe.matmul(bank[:, j * P:(j + 1) * P], OTT[:, j * P:(j + 1) * P], WO[:, :], start=True, stop=True)
                    mm.then_inc(pe_v, 1)

        @block.sync
        def _(sp):
            xr, xo = rows(x_in, D), rows(x_out, D)
            for b in range(B):
                sp.dma_start(X[:, b * TB:(b + 1) * TB, :], xr[:, b * TB:(b + 1) * TB, :]).then_inc(s_x[b], 16)
            sp.dma_start(ident[:, :], cst["ident"]).then_inc(s_c, 16)
            sp.dma_start(mqf[:, :, :], cst["causal"]).then_inc(s_c, 16)
            sp.dma_start(rope[:, :, :], cst["rope"]).then_inc(s_c, 16)
            sp.dma_start(wp[:, :, :], w["qkv"]).then_inc(s_c, 16)
            sp.dma_start(WO[:, :], w["o"]).then_inc(s_c, 16)
            for step, b, i in steps():
                s = b % 2
                if step == "project":
                    sp.wait_ge(s_ps, 2 * b + 2)
                    if b >= 2:
                        sp.wait_ge(s_ld[s], LOADS * (b // 2))
                    for k in range(2):
                        sp.dma_start(stack[s, k].rearrange("a p t -> p a t"), PS[:, s, k, :, :]).then_inc(s_st[s], 16)
                elif step == "max" and i == 0 and b == 0:
                    load(sp, 0)
                    load(sp, 1)
                elif step == "take":
                    sp.wait_ge(act_job, JA.done("nm", b))
                    for a in range(3):
                        sp.dma_start(QS[MAXROW + a:MAXROW + a + 1, s, :, :], NMT[a * HB:(a + 1) * HB, :]).then_inc(s_mr[s], 16)
                elif step == "out":
                    if b + 2 < B:
                        load(sp, b + 2)
                    sp.wait_ge(dve_job, JV.done("out", b))
                    sp.dma_start(xo[:, b * TB:(b + 1) * TB, :], X[:, b * TB:(b + 1) * TB, :]).then_inc(s_out, 16)
            sp.wait_ge(s_out, 16 * B)


        @block.gpsimd
        def _(pool):
            pool.memset(eps[:, :], LN_EPS).then_inc(s_set, 1)
            pool.memset(KS[:, :, :, :], 1.0).then_inc(s_set, 1)
            pool.memset(zr[:, :], 0.0).then_inc(s_set, 1)
            pool.memset(VX[:, :, :, :, :], 0.0).then_inc(s_vx, 1)
            pool.wait_ge(s_vx, 1)
            pool.memset(VX[:, :, :, :, DB], 1.0).then_inc(s_vx, 1)
            pool.wait_ge(s_c, 16 * NC)
            pool.tensor_copy(identb[:, :], ident[:, :]).then_inc(s_cb, 1)
            pool.tensor_copy(mq[:, :], mqf[:, 0, :]).then_inc(s_cb, 1)
            pool.tensor_copy(mk[:, :], mqf[:, 1, :]).then_inc(s_cb, 1)
            link_n = [0]

            def link(ins):
                link_n[0] += 1
                ins.then_inc(s_pool, 1)
                pool.wait_ge(s_pool, link_n[0])

            def clamp(n):
                b, h = n // HB, n % HB
                pool.wait_ge(act_job, JA.done("sc", b, h, 0))
                e = PB[:, h % 8, 0:512]
                pool.tensor_scalar(e, e, 1.0, None, ALU.min).then_inc(s_cp, 1)

            for step, b, i in steps():
                s = b % 2
                if step == "project":
                    if b >= 2:
                        pool.wait_ge(s_st[s], 32 * (b // 2))
                    for k in range(2):
                        pool.wait_ge(dve_job, JV.done("qk", b, 2 * k + 1))
                        a, r, part = RT[:, k, 0, :], RT[:, k, 1, :], PS[:, s, k, :, :]
                        link(pool.tensor_tensor(a, a, r, ALU.add))
                        link(pool.tensor_copy(part[:, 0, :], a))
                        link(pool.tensor_tensor(r, a, part[:, 0, :], ALU.subtract))
                        link(pool.tensor_copy(part[:, 1, :], r))
                        pool.tensor_tensor(part[:, 2, :], r, part[:, 1, :], ALU.subtract).then_inc(s_ps, 1)
                elif step == "probs" and i:
                    clamp(b * HB + i - 1)
                elif step == "values" and i == 3:
                    clamp(b * HB + HB - 1)

        @block.scalar
        def _(act):
            jobs = Jobs()

            def bank(name, *rest):
                i = jobs.next()
                assert JA.named[(name, *rest)] == i, (name, rest)
                act.wait_ge(pe_a, i + 1)
                return banks_a[i % RING]

            def copy(out, in_):
                return act.activation(out, in_, ACT.Copy)

            act.wait_ge(s_set, 1)
            act.wait_ge(s_sd, 1)
            act.activation(rstd[:, :], mv[:, :, 1], ACT.Sqrt, bias=eps[:, 0:1]).then_inc(s_rs, 1)
            act.wait_ge(s_vx, 2)
            for step, b, i in steps():
                s = b % 2
                if step == "project":
                    if b >= 2:
                        act.wait_ge(pe_a, JA.done("v", b - 2))
                    copy(xnT[:, s, :], bank("xT", b)[:, :]).then_inc(act_job, 1)
                    if b >= 3:
                        act.wait_ge(pe_a, JA.done("pv", b - 3, 3))
                    copy(VX[:, b % 3, :, :, 0:DB].rearrange("p k h d -> p (k h) d"),
                         bank("v", b)[:, :].rearrange("p (n d) -> p n d", d=DB)).then_inc(act_job, 1)
                elif step == "take":
                    if b:
                        act.wait_ge(s_mr[1 - s], 48 * ((b - 1) // 2 + 1))
                    copy(NMT[:, :], bank("nm", b)[:, 0:256].bitcast(BF16)[0:3 * HB, :]).then_inc(act_job, 1)
                elif step == "probs":
                    n = b * HB + i
                    if n >= 8:
                        act.wait_ge(pe_a, JA.done("pv", (n - 8) // HB, (n - 8) % HB // 4))
                    for o, e, part in ((0, 512, 0), (512, 896, 1), (896, PW, 2)):
                        act.activation(PB[:, i % 8, o:e], bank("sc", b, i, part)[:, 0:e - o], ACT.Exp).then_inc(act_job, 1)
                elif step == "values":
                    n = 4 * b + i
                    if n >= 2:
                        act.wait_ge(pe_v, JV.done("den", (n - 2) // 4, (n - 2) % 4))
                    copy(OT[:, i % 2, :], bank("pv", b, i)[:, :]).then_inc(act_job, 1)
                elif step == "out":
                    if b:
                        act.wait_ge(pe_v, JV.done("out", b - 1))
                    copy(OTT[:, :], bank("oT", b)[:, :]).then_inc(act_job, 1)

        @block.vector
        def _(dve):
            jobs = Jobs()
            link_n = [0]

            def link(ins):
                link_n[0] += 1
                ins.then_inc(s_dve, 1)
                dve.wait_ge(s_dve, link_n[0])

            def bank(name, *rest):
                i = jobs.next()
                assert JV.named[(name, *rest)] == i, (name, rest)
                dve.wait_ge(pe_v, i + 1)
                return banks_v[i % RING]

            def clamp(n):
                b, h = n // HB, n % HB
                dve.wait_ge(act_job, JA.done("sc", b, h, 2))
                e = PB[:, h % 8, 512:PW]
                dve.tensor_scalar(e, e, 1.0, None, ALU.min).then_inc(s_cd, 1)

            dve.memset(QS[:, :, :, :].rearrange("p s h t -> p (s h t)").bitcast(F32), 0.0).then_inc(s_qz, 1)
            for b in range(B):
                dve.wait_ge(s_x[b], x0 + 16)
                for t in range(b * TB, b * TB + TB):
                    ins = dve.bn_stats(stats6[:, t, :], X[:, t, :])
                link(ins)
                for t in range(b * TB, b * TB + TB):
                    ins = dve.bn_aggr(mv[:, t, :], stats6[:, t, :])
            ins.then_inc(s_sd, 1)
            dve.wait_ge(s_rs, 1)
            link(dve.reciprocal(rstd[:, :], rstd[:, :]))
            dve.wait_ge(s_c, 16 * NC)
            for step, b, i in steps():
                s = b % 2
                if step == "project":
                    if b >= 2:
                        dve.wait_ge(pe_a, JA.done("xT", b - 2))
                    for t in range(b * TB, b * TB + TB):
                        dve.tensor_scalar(xn[:, t % (2 * TB), :], X[:, t, :], mv[:, t, 0:1], rstd[:, t:t + 1],
                                          ALU.subtract, ALU.mult).then_inc(s_ln, 1)
                    if b:
                        dve.wait_ge(s_ps, 2 * b)
                    for k in range(4):
                        dve.tensor_tensor(RT[:, k // 2, k % 2, :], bank("qk", b, k)[:, :], rope[:, k, :], ALU.mult).then_inc(dve_job, 1)
                elif step == "max":
                    q, h0, n = amax[i]
                    dve.tensor_reduce(MX[:, q, h0:h0 + n],
                                      bank("max", b, i)[:, 0:n * (q + 1) * P].rearrange("p (h k) -> p h k", h=n),
                                      AX.X, ALU.max).then_inc(dve_job, 1)
                elif step == "take":
                    dve.wait_ge(dve_job, JV.done("max", b, len(amax) - 1))
                    if b:
                        dve.wait_ge(pe_a, JA.done("nm", b - 1))
                    link(dve.tensor_scalar(MR[:, :, :], MX[:, :, :], -CLAMP, CLAMP, ALU.max, ALU.min))
                    link(dve.tensor_scalar(MX[:, :, :], MR[:, :, :], -1.0, None, ALU.mult))
                    link(dve.tensor_copy(N3[:, :, 0, :], MX[:, :, :]))
                    link(dve.tensor_tensor(MR[:, :, :], MX[:, :, :], N3[:, :, 0, :], ALU.subtract))
                    link(dve.tensor_copy(N3[:, :, 1, :], MR[:, :, :]))
                    dve.tensor_tensor(N3[:, :, 2, :], MR[:, :, :], N3[:, :, 1, :], ALU.subtract).then_inc(s_nm, 1)
                elif step == "probs" and i:
                    clamp(b * HB + i - 1)
                elif step == "values" and i == 3:
                    clamp(b * HB + HB - 1)
                elif step == "norm":
                    src = bank("den", b, i)[:, :].rearrange("p (t j r) -> p t j r", t=TB, j=4)
                    if i or b:
                        dve.wait_ge(dve_job, JV.done("den", b, i) - 1)
                    link(dve.reciprocal(RC[:, :, :], src[:, :, :, DB]))
                    if i == 0 and b:
                        dve.wait_ge(pe_a, JA.done("oT", b - 1))
                    dve.tensor_tensor(OTK[:, :, 4 * DB * i:4 * DB * (i + 1)].rearrange("p t (j d) -> p t j d", j=4),
                                      src[:, :, :, 0:DB], RC[:, :, :].to_broadcast([P, TB, 4, DB]), ALU.mult).then_inc(dve_job, 1)
                elif step == "out":
                    xb = X[:, b * TB:(b + 1) * TB, :].rearrange("p t d -> p (t d)")
                    dve.tensor_tensor(xb, xb, bank("out", b)[:, :], ALU.add).then_inc(dve_job, 1)


def layers(nc, x_in, x_out, wa, wb, wf, ca, cb, cf):
    x1, x2, x3 = (nc.dram_tensor(f"x{i}", [T, D], F32).ap() for i in (1, 2, 3))
    xbuf = nc.dram_tensor("xbuf", [SLOTS + T, D], F32).ap()
    ybuf = nc.dram_tensor("ybuf", [SLOTS + 1, D], F32).ap()
    stack = nc.dram_tensor("stack", [2, 2, 3, P, L], BF16).ap()
    with ExitStack() as sems:
        s_x = [sems.enter_context(nc.semaphore(f"batch{b}")) for b in range(B)]
        attn_a(nc, sems, s_x, x_in, x1, wa, ca)
        moe(nc, sems, s_x, 32, x1, x2, wf, cf, xbuf, ybuf, "f1", True)
        attn_b(nc, sems, s_x, 64, x2, x3, wb, cb, stack)
        moe(nc, sems, s_x, 80, x3, x_out, wf, cf, xbuf, ybuf, "f2", False)


def kernel(**inputs):
    import concourse.bacc as _bacc
    from concourse.bass_utils import run_bass_kernel_spmd as _run

    x = np.ascontiguousarray(inputs["L0_attn_a_hidden_states"]).reshape(T, D)
    a = {n[len("L0_attn_a_"):]: np.asarray(v) for n, v in inputs.items() if n.startswith("L0_attn_a_")}
    b = {n[len("L0_attn_b_"):]: np.asarray(v) for n, v in inputs.items() if n.startswith("L0_attn_b_")}
    f = {n[len("L0_ffn_w_"):]: np.asarray(v) for n, v in inputs.items() if n.startswith("L0_ffn_w_")}

    fir = np.zeros((H, DK // 4, 4, 2, 3 * KL), np.float32)
    fir[..., 0, KL - 1:2 * KL - 1] = a["fir_long_w"].reshape(H, DK // 4, 4, KL)[..., ::-1]
    fir[..., 1, KL - 1:KL + 4] = a["fir_short_w"].reshape(H, DK // 4, 4, 5)[..., ::-1]
    fir = fir.transpose(1, 0, 2, 3, 4).reshape(P, 2, 3 * KL)
    swap = np.arange(D) ^ 1
    weights = {
        "a": {"qkvT": np.stack([a["q_w"].T, a["k_w"].T, a["v_w"].T], axis=1),
              "cw": np.stack([a["q_cw"].T, a["k_cw"].T, a["v_cw"].T]),
              "bT": a["b_w"].T, "w1xT": a["mlp1_w"][:, :D].T, "w1sT": a["mlp1_w"][:, D:].T,
              "oT": a["o_w"].T, "fir": fir, "w2T": a["mlp2_w"].T, "b2": a["mlp2_b"],
              "temp": a["logit_temp"], "res": a["conv_res_logit"],
              "norm": a["norm_w"].reshape(DK, 1), "b1": a["mlp1_b"].reshape(P, 1)},
        "b": {"qkv": np.stack([b["WQ"].T, b["WQ"][swap].T, b["WK"].T, b["WK"][swap].T, b["WV"].T], axis=1),
              "o": b["WO"].T},
        "f": f,
    }

    p, q = np.arange(P)[:, None], np.arange(P)[None]
    r, c = p % C, np.arange(C)[None]
    turns = np.float32(10000.0) ** -(((p % DB) // 2).astype(np.float32) / np.float32(DB // 2))
    angle = np.arange(L, dtype=np.float32)[None] * turns
    cos, sin = np.cos(angle), np.sin(angle) * np.where(p % 2 == 0, -1.0, 1.0)
    later = np.where(q > p, -1e30, 0.0)
    ident = p == q
    constants = {
        "a": {"ident": ident, "flip": p + q == P - 1, "masks": np.stack([-1.0 * (r > c), 1.0 * (c >= r), 1.0 * (c == r)], axis=1)},
        "b": {"ident": ident, "causal": np.stack([later, later.T], axis=1),
              "rope": np.stack([cos / np.sqrt(DB), sin / np.sqrt(DB), cos, sin], axis=1)},
        "f": {"ident": ident, "tri": p <= q, "rank": np.tile(np.arange(E_, 0, -1), (P, 1)),
              "dump": SLOTS + p + P * np.arange(NT)[None]},
    }

    nc = _bacc.Bacc("TRN2", target_bir_lowering=False, num_devices=1)
    arrays = {}

    def given(name, array):
        arrays[name] = np.ascontiguousarray(array)
        return nc.dram_tensor(name, array.shape, mybir.dt.from_np(array.dtype), kind="ExternalInput").ap()

    x_ap = given("in_x_dram", x)
    w = {k: {n: given(f"in_{k}_{n}_dram", v) for n, v in d.items()} for k, d in weights.items()}
    cst = {k: {n: given(f"const_{k}_{n}_dram", v.astype(np.float32)) for n, v in d.items()} for k, d in constants.items()}
    out = nc.dram_tensor("out_0_dram", (T, D), F32, kind="ExternalOutput").ap()
    layers(nc, x_ap, out, w["a"], w["b"], w["f"], cst["a"], cst["b"], cst["f"])
    got = _run(nc, [arrays], core_ids=[0])
    return got.results[0]["out_0_dram"].reshape(B, L, D)
```

```python
from contextlib import ExitStack

import numpy as np

import concourse.bass as bass
from concourse import mybir

F32 = mybir.dt.float32
BF16 = mybir.dt.bfloat16
I32 = mybir.dt.int32
ALU = mybir.AluOpType
ACT = mybir.ActivationFunctionType
AX = mybir.AxisListType

P = 128
B, L, D = 8, 512, 128
T = B * L
NT = T // P
TB = L // P
H, DK = 4, 32
C = 32
G = T // C
GB = L // C
TAPS = 4
PROB_FLOOR = 0.02
KL = 64
LN_EPS = 1e-5

RING = 4


class Jobs:

    def __init__(self):
        self.n = 0
        self.named = {}

    def next(self, *name):
        i = self.n
        self.n += 1
        if name:
            self.named[name] = i
        return i

    def done(self, *name):
        return self.named[name] + 1


def rows(dram, cols):
    return dram.rearrange("(t p) d -> p t d", p=P)


def attn_a(nc, sems, s_x, x_in, x_out, w, cst):
    NTR = 4
    ctx = ExitStack()
    with ctx:
        R = ctx.enter_context(nc.sbuf_tensor("a_regions", [P, 11, 4096], F32))
        xnT = ctx.enter_context(nc.sbuf_tensor("a_xnT", [P, B, L + TAPS - 1], F32))

        def reg(i, n=1):
            return R[:, i:i + n, :].rearrange("p a b -> p (a b)")

        small = lambda name, shape, dt=F32: ctx.enter_context(nc.sbuf_tensor("a_" + name, shape, dt))
        ident = small("ident", [P, P])
        eps = small("eps", [P, 4])
        mv = small("mv", [P, NT, 2])
        rstd = small("rstd", [P, NT])
        beta = small("beta", [P, G])
        rn = small("rn", [P, 2, G])
        bk = small("bk", [P, 2, G])
        wo = small("wo", [P, P])
        masks = small("masks", [P, 3, C])
        wbig = small("wbig", [P, 3, P])
        hdr = small("hdr", [P, 16])

        X = reg(9).rearrange("p (t d) -> p t d", t=NT)
        xn = reg(10).rearrange("p (t d) -> p t d", t=NT)
        stats6 = reg(6)[:, 0:NT * 6].rearrange("p (t s) -> p t s", s=6)
        WC = reg(8)[:, 0:12 * P].rearrange("p (s j c) -> p s j c", s=3, j=TAPS)
        CWB = reg(7)[:, 12 * P:24 * P].rearrange("p (s j c) -> p s j c", s=3, j=TAPS)
        WQKV = reg(7)[:, 24 * P:27 * P].rearrange("p (s c) -> p s c", s=3)
        bwT = reg(7)[:, 27 * P:27 * P + H]
        VT = reg(9)
        VH = reg(4).rearrange("p (g d) -> p g d", d=DK)
        v0 = reg(10).rearrange("p (t c) -> p t c", c=P)
        vE = reg(6).rearrange("p (t c) -> p t c", c=P)
        TR = reg(5).rearrange("p (r h d n) -> p r h d n", r=NTR, h=H, d=2)
        LS = reg(9).rearrange("p (g d) -> p g d", d=DK)
        LLG = reg(10).rearrange("p (g d) -> p g d", d=DK)
        KQ = reg(1, 2).rearrange("p (g s c) -> p g s c", s=2, c=C)
        VK = reg(5, 2).rearrange("p (g s c) -> p g s c", s=2, c=C)
        AK = reg(7, 2).rearrange("p (g s c) -> p g s c", s=2, c=C)
        vO = AK[:, :, 1, :]
        MS = reg(3).rearrange("p (g c) -> p g c", c=C)
        ME = reg(0).rearrange("p (h r c) -> p h r c", h=H, r=C)
        TI = reg(3).rearrange("p (r h c) -> p h r c", h=H, r=C)
        TIr = reg(3).rearrange("p (r n) -> p r n", r=C)
        stat = small("stat", [P, 3, 4, G])
        TMP = stat[:, :, :, :].rearrange("p i k g -> p (i k g)")[:, 0:8 * P].rearrange("p (h n) -> p h n", h=H)
        TT = reg(0).rearrange("p (g c) -> p g c", c=C)
        AT = reg(3).rearrange("p (g c) -> p g c", c=C)
        SS = reg(0).rearrange("p (g c) -> p g c", c=C)
        DH = reg(3).rearrange("p (g c) -> p g c", c=C)
        QKH = reg(6).rearrange("p (i s g c) -> p i s g c", i=4, s=2, c=C)

        w1s = small("w1s", [P, H, P])
        w2p = small("w2p", [P, DK])
        NW = 8 + 3 + 2 * H + 1 + H
        XS = [LS, LLG, DH, VH]
        SQX = [AK[:, :, 1, :], VK[:, :, 1, :], AK[:, :, 1, :], AK[:, :, 1, :]]
        ST = KQ[:, :, 0, :]
        STT = VK[:, :, 1, :]
        H1 = [reg(0)[:, i * L:(i + 1) * L] for i in range(8)]
        LG = reg(2).rearrange("p (g s) -> p g s", s=DK)
        OH = reg(1).rearrange("p (g d) -> p g d", d=DK)
        O2 = reg(7).rearrange("p (g d) -> p g d", d=DK)
        OSQ = LLG
        OT = reg(9)
        OSCR = reg(7)[:, 3584:4096]
        groups = ((0, 1), (1, 3), (3, 5), (5, 8))
        XR = xnT[:, :, :].rearrange("p b l -> p (b l)")[:, 0:T].rearrange("p (t d) -> p t d", d=D)
        sm = reg(8)
        S1, S2, MM = (stat[:, i] for i in range(3))
        PR = sm[:, 0:512].rearrange("p (g k) -> p g k", k=4)
        R1, R2 = sm[:, 512:512 + G], sm[:, 640:640 + G]
        O3 = sm[:, 1024:1536].rearrange("p (g d) -> p g d", d=DK)
        w1x, bw, flip = (wbig[:, i, :] for i in range(3))

        banks_a = [ctx.enter_context(nc.psum_tensor(f"a_pa{i}", [P, 512], F32)) for i in range(RING)]
        banks_v = [ctx.enter_context(nc.psum_tensor(f"a_pv{i}", [P, 512], F32)) for i in range(RING)]
        sem = lambda name: sems.enter_context(nc.semaphore("a_" + name))
        pe_a, pe_v = sem("pe_a"), sem("pe_v")
        act_job, dve_job = sem("act_job"), sem("dve_job")
        s_w, s_out = sem("s_w"), sem("s_out")
        s_t = [sem(f"s_t{i}") for i in range(NTR)]
        s_pad, s_bw, s_wc, s_ln, s_sd, s_rs = (sem(n) for n in ("pad", "bw", "wc", "ln", "sd", "rs"))
        s_vo, s_voz, s_sq, s_nrm, s_kh, s_dve, s_pool, s_beta, s_vk, s_msb, s_el, s_elp, s_tz = (
            sem(n) for n in ("vo", "voz", "sq", "nrm", "kh", "dve", "pool", "beta", "vk", "msb", "el", "elp", "tz"))
        s_beta0, s_beta1, s_scan, s_kt, s_tu, s_sqd, s_rd, s_bk, s_r2 = (sem(n) for n in ("beta0", "beta1", "scan", "kt", "tu", "sqd", "rd", "bk", "r2"))
        s_st, s_sqx, s_l2, s_stt, s_hdr2, s_e, s_ex, s_mix, s_ms, s_rms, s_o, s_oT, s_w1s, s_elim, s_bst, s_p, s_pl, s_o2 = (
            sem(n) for n in ("st", "sqx", "l2", "stt", "hdr2", "e", "ex", "mix", "ms", "rms", "o", "oT", "w1s", "elim", "bst", "p", "pl", "o2"))
        JA, JV = Jobs(), Jobs()
        NSLAB = DK // 2
        FIR0 = C - 1 - NSLAB

        block = ctx.enter_context(nc.Block())

        def eliminate(eng, hs, chain, last, between=lambda j: None):
            n = hs.stop - hs.start
            eng.wait_ge(act_job, JA.done("me", C // 4 - 1))
            eng.wait_ge(s_tz, 1)
            for j in range(C - 1):
                r, c = C - 1 - j, j + 1
                tmp = TMP[:, hs, 0:r * c].rearrange("p h (r c) -> p h r c", c=c)
                if j:
                    eng.wait_ge(chain, 2 * j)
                eng.tensor_tensor(tmp, ME[:, hs, j + 1:C, j:j + 1].to_broadcast([P, n, r, c]),
                                  TI[:, hs, j:j + 1, 0:c].to_broadcast([P, n, r, c]), ALU.mult).then_inc(chain, 1)
                eng.wait_ge(chain, 2 * j + 1)
                ins = eng.tensor_tensor(TI[:, hs, j + 1:C, 0:c], TI[:, hs, j + 1:C, 0:c], tmp, ALU.add)
                ins.then_inc(chain if j < C - 2 else last, 1)
                between(j)

        def gate_pe(pe, bank_a, bank_v):
            def logits(b):
                bank = bank_v("lg", b)
                pe.wait_ge(act_job, JA.done("h1", b, H - 1))
                for h in range(H):
                    mm = pe.matmul(bank[DK * h:DK * h + DK, :], w2p[:, :], H1[(b * H + h) % 8], start=True, stop=True)
                mm.then_inc(pe_v, 1)

            for b in range(B):
                for h in range(H):
                    bank = bank_a("h1", b, h)
                    if h == 0:
                        pe.wait_ge(s_stt, b + 1)
                    pe.matmul(bank[:, :], w1x, xnT[:, b, TAPS - 1:], start=True, stop=False)
                    pe.matmul(bank[:, :], w1s[:, h, :], STT[:, b * GB:(b + 1) * GB, :], start=False, stop=True).then_inc(pe_a, 1)
                if b:
                    logits(b - 1)
            logits(B - 1)
            for b in range(B):
                bank = bank_v("o", b)
                pe.wait_ge(s_oT, b + 1)
                for j in range(TB):
                    t = b * TB + j
                    mm = pe.matmul(bank[:, j * P:(j + 1) * P], OT[:, t * P:(t + 1) * P], wo[:, :], start=True, stop=True)
                mm.then_inc(pe_v, 1)

        def gate_act(act, bank, copy):
            act.activation(hdr[:, 8:9], hdr[:, 4:5], ACT.Abs).then_inc(s_hdr2, 1)
            act.wait_ge(s_hdr2, 1)
            act.activation(hdr[:, 8:9], hdr[:, 8:9], ACT.Exp, scale=-1.0).then_inc(s_hdr2, 1)
            act.wait_ge(s_hdr2, 2)
            act.activation(hdr[:, 8:9], hdr[:, 8:9], ACT.Ln, bias=eps[:, 2:3]).then_inc(s_hdr2, 1)
            act.activation(hdr[:, 9:10], hdr[:, 5:6], ACT.Sigmoid).then_inc(s_hdr2, 1)
            act.wait_ge(act_job, JA.done("ku", B - 1))
            act.wait_ge(pe_a, JA.done("ku", B - 1))
            act.activation(SQX[0], XS[0], ACT.Square).then_inc(s_sqx, 1)
            act.wait_ge(pe_v, JV.done("qa", G // 8 - 1))
            act.activation(SQX[1], XS[1], ACT.Square).then_inc(s_sqx, 1)
            D4 = DH.rearrange("p (b i) c -> p i b c", b=B)
            B4 = KQ[:, :, 0, :].rearrange("p (b i) c -> p i b c", b=B)
            for i in range(GB):
                if i == GB // 2 - 2:
                    act.wait_ge(s_r2, 1)
                    act.activation(SQX[3], XS[3], ACT.Square).then_inc(s_sqx, 1)
                act.wait_ge(dve_job, JV.done("dh", i))
                act.activation(B4[:, i], D4[:, i], ACT.Square).then_inc(s_sqd, 1)
            act.wait_ge(s_st, 1)
            act.activation(ST[:, :, 3:16:4].rearrange("p g k -> p k g"), S2, ACT.Sqrt).then_inc(s_l2, 1)
            def exps(n):
                b0, b1 = groups[n]
                gs = slice(b0 * GB, b1 * GB)
                act.wait_ge(s_e, n + 1)
                act.activation(PR[:, gs, :], PR[:, gs, :], ACT.Exp, scale=hdr[:, 10:11]).then_inc(s_ex, 1)

            def squares(n):
                b0, b1 = groups[n]
                for b in range(b0, b1):
                    gs = slice(b * GB, b * GB + GB)
                    act.wait_ge(s_mix, b + 1)
                    act.activation(OSQ[:, gs, :], OH[:, gs, :], ACT.Square).then_inc(s_o, 1)

            def roots(n):
                b0, b1 = groups[n]
                act.wait_ge(s_ms, n + 1)
                act.activation(R1[:, b0 * GB:b1 * GB], R1[:, b0 * GB:b1 * GB], ACT.Sqrt, bias=eps[:, 0:1], scale=1.0 / DK).then_inc(s_rms, 1)

            for b in range(B + 3):
                for h in range(H if b < B else 0):
                    if b >= 2 and h == 0:
                        act.wait_ge(pe_v, JV.done("lg", b - 2))
                    act.activation(H1[(b * H + h) % 8], bank("h1", b, h)[:, :], ACT.Gelu_apprx_tanh,
                                   bias=hdr[:, 7:8]).then_inc(act_job, 1)
                for n, (b0, b1) in enumerate(groups):
                    if b == b1:
                        exps(n)
                for n, (b0, b1) in enumerate(groups):
                    if b == b1 + 1:
                        squares(n)
                    if b == max(b1 + 2, groups[min(n + 1, len(groups) - 1)][1]):
                        roots(n)

        def gate_pool(pool):
            pool.wait_ge(s_st, 1)
            pool.memset(ST[:, :, 16:], 0.0).then_inc(s_bst, 1)
            for b in range(B):
                for n, group in enumerate(groups):
                    if b == group[0]:
                        pool.wait_ge(s_p, n + 1)
                gs = slice(b * GB, b * GB + GB)
                if b:
                    pool.wait_ge(s_o2, b)
                pool.tensor_tensor(O2[:, gs, :], XS[1][:, gs, :], PR[:, gs, 1:2].to_broadcast([P, GB, DK]), ALU.mult).then_inc(s_pl, 1)
                pool.tensor_tensor(O3, XS[3][:, gs, :], PR[:, gs, 3:4].to_broadcast([P, GB, DK]), ALU.mult).then_inc(s_pl, 1)
                pool.wait_ge(s_pl, 2 * b + 2)
                pool.tensor_tensor(O2[:, gs, :], O2[:, gs, :], O3, ALU.add).then_inc(s_o2, 1)

        @block.tensor
        def _(pe):
            def bank_a(*name):
                i = JA.next(*name)
                if i >= RING:
                    pe.wait_ge(act_job, i - RING + 1)
                return banks_a[i % RING]

            def bank_v(*name):
                i = JV.next(*name)
                if i >= RING:
                    pe.wait_ge(dve_job, i - RING + 1)
                return banks_v[i % RING]

            pe.wait_ge(s_w, 16 * NW)
            for b in range(B):
                bank = bank_a("xnT", b)
                for j in range(TB):
                    pe.wait_ge(s_ln, b * TB + j + 1)
                    mm = pe.transpose(bank[:, j * P:(j + 1) * P], xn[:, b * TB + j, :], ident[:, :])
                mm.then_inc(pe_a, 1)
            pe.wait_ge(s_wc, 2)
            pe.wait_ge(s_pad, 3)
            for b in range(B):
                bank = bank_a("v", b)
                pe.wait_ge(act_job, JA.done("xnT", b))
                for j in range(TAPS):
                    mm = pe.matmul(bank[:, :], WC[:, 2, j, :], xnT[:, b, j:j + L], start=j == 0, stop=j == TAPS - 1)
                mm.then_inc(pe_a, 1)
            pe.wait_ge(s_bw, 1)
            for b in range(B):
                bank = bank_v("beta", b)
                pe.matmul(bank[:, :], bw, xnT[:, b, TAPS - 1:], start=True, stop=True).then_inc(pe_v, 1)
            for b in range(B):
                for s in range(2):
                    bank = bank_a("kq", s, b)
                    for j in range(TAPS):
                        mm = pe.matmul(bank[:, :], WC[:, 1 - s, j, :], xnT[:, b, j:j + L], start=j == 0, stop=j == TAPS - 1)
                    mm.then_inc(pe_a, 1)
            for q in range(G // 8):
                bank = bank_v("kk", q)
                pe.wait_ge(act_job, JA.done("kq", 1, q // 2))
                for g in range(8 * q, 8 * q + 8):
                    for h in range(H):
                        e = slice(DK * h, DK * h + DK)
                        mm = pe.matmul(bank[e, (g % 8) * 64:(g % 8) * 64 + 64], KQ[e, g, 0, :],
                                       KQ[e, g, :, :].rearrange("p s c -> p (s c)"), start=True, stop=True)
                mm.then_inc(pe_v, 1)
            pe.wait_ge(s_msb, B)
            for q in range(C // 4):
                bank = bank_a("me", q)
                for j in range(4):
                    mm = pe.transpose(bank[:, j * P:(j + 1) * P], MS[:, :, 4 * q + j], ident[:, :])
                mm.then_inc(pe_a, 1)
            for b in range(B):
                bank = bank_a("vE", b)
                pe.wait_ge(act_job, JA.done("v", b))
                for j in range(TB):
                    t = b * TB + j
                    mm = pe.transpose(bank[:, j * P:(j + 1) * P], VT[:, t * P:(t + 1) * P], ident[:, :])
                mm.then_inc(pe_a, 1)
            for b in range(B):
                bank = bank_a("vR", b)
                pe.wait_ge(act_job, JA.done("vE", b))
                pe.matmul(bank[:, :], flip, v0[:, b * TB:(b + 1) * TB, :].rearrange("p t c -> p (t c)"),
                          start=True, stop=True).then_inc(pe_a, 1)
            pe.wait_ge(s_voz, 1)
            pe.wait_ge(s_vo, 16 * (B + 1))
            vOt = vO.rearrange("p (t h) c -> p t h c", h=H)
            for q in range(NSLAB // 2):
                banks = [bank_v("fir", q, half) for half in range(2)]
                for i in range(2):
                    s = 2 * q + i
                    pe.wait_ge(s_t[s % NTR], 16 * (s // NTR + 1))
                    for half in range(2):
                        for d in (2 * i, 2 * i + 1):
                            for h in range(H):
                                mm = pe.matmul(banks[half][DK * h:DK * h + DK, d * P:(d + 1) * P],
                                               vE[:, :, DK * h + 4 * q + d] if half else vOt[:, :, h, 4 * q + d],
                                               TR[:, s % NTR, h, d % 2, :], start=True, stop=True)
                        if i:
                            mm.then_inc(pe_v, 1)
                    if i == 0:
                        mm.then_inc(s_tu, 1)
            pe.wait_ge(s_el, 1)
            pe.wait_ge(s_elp, 1)
            for q in range(C // 4):
                bank = bank_a("tt", q)
                for j in range(4):
                    mm = pe.transpose(bank[:, j * P:(j + 1) * P], TIr[:, 4 * q + j, :], ident[:, :])
                mm.then_inc(pe_a, 1)
            pe.wait_ge(act_job, JA.done("tt", C // 4 - 1))
            for q in range(G // 8):
                bank = bank_a("uw", q)
                pe.wait_ge(s_vk, q // 2 + 1)
                for g in range(8 * q, 8 * q + 8):
                    for h in range(H):
                        e = slice(DK * h, DK * h + DK)
                        mm = pe.matmul(bank[e, (g % 8) * 64:(g % 8) * 64 + 64], TT[e, g, :],
                                       VK[e, g, :, :].rearrange("p s c -> p (s c)"), start=True, stop=True)
                mm.then_inc(pe_a, 1)
            for q in range(G // 8):
                pe.wait_ge(act_job, JA.done("uw", q))
                bank = bank_v("qa", q)
                for g in range(8 * q, 8 * q + 8):
                    for h in range(H):
                        e = slice(DK * h, DK * h + DK)
                        mm = pe.matmul(bank[e, (g % 8) * 64:(g % 8) * 64 + 64], VK[e, g, 1, :],
                                       AK[e, g, :, :].rearrange("p s c -> p (s c)"), start=True, stop=True)
                mm.then_inc(pe_v, 1)
                if q % 2 == 1:
                    bank = bank_a("ku", q // 2)
                    for g in range(8 * q - 8, 8 * q + 8):
                        for h in range(H):
                            e = slice(DK * h, DK * h + DK)
                            mm = pe.matmul(bank[e, (g % 16) * C:(g % 16 + 1) * C], AK[e, g, 1, :], VK[e, g, 0, :],
                                           start=True, stop=True)
                    mm.then_inc(pe_a, 1)
            pe.wait_ge(dve_job, JV.done("qa", G // 8 - 1))
            pe.wait_ge(act_job, JA.done("uw", G // 8 - 1))
            for i in range(GB):
                if i == 1:
                    pe.wait_ge(s_scan, 1)
                elif i:
                    pe.wait_ge(dve_job, JV.done("scan", i - 1))
                if 0 < i < GB - 1:
                    bank = bank_v("scan", i)
                    for b in range(B):
                        for h in range(H):
                            e = slice(DK * h, DK * h + DK)
                            mm = pe.matmul(bank[e, b * C:(b + 1) * C], AT[e, b * GB + i, :], SS[e, b * GB + i, :],
                                           start=True, stop=True)
                    mm.then_inc(pe_v, 1)
                bank = bank_v("dh", i)
                for b in range(B):
                    g = b * GB + i
                    for h in range(H):
                        e = slice(DK * h, DK * h + DK)
                        o = bank[e, b * C:(b + 1) * C]
                        if i:
                            pe.matmul(o, KQ[e, g, 1, :], SS[e, g, :], start=True, stop=False)
                        mm = pe.matmul(o, AK[e, g, 0, :], VK[e, g, 0, :], start=i == 0, stop=True)
                mm.then_inc(pe_v, 1)
            gate_pe(pe, bank_a, bank_v)

        @block.sync
        def _(sp):
            xr = rows(x_in, D)
            for i in range(B):
                sp.dma_start(X[:, i * TB:(i + 1) * TB, :], xr[:, i * TB:(i + 1) * TB, :]).then_inc(s_x[i], 16)
            sp.dma_start(ident[:, :], cst["ident"]).then_inc(s_w, 16)
            sp.dma_start(flip, cst["flip"]).then_inc(s_w, 16)
            sp.dma_start(masks[:, :, :], cst["masks"]).then_inc(s_w, 16)
            sp.dma_start(WQKV, w["qkvT"]).then_inc(s_w, 16)
            sp.dma_start(CWB.rearrange("p s j c -> p (s j c)"),
                         bass.AP(tensor=w["cw"].tensor, offset=0, ap=[[0, P], [1, 12 * P]])).then_inc(s_w, 16)
            sp.dma_start(bwT, w["bT"]).then_inc(s_w, 16)
            sp.dma_start(w1x, w["w1xT"]).then_inc(s_w, 16)
            sp.dma_start(wo[:, :], w["oT"]).then_inc(s_w, 16)
            sp.dma_start(w2p[:, 0:4], w["w2T"]).then_inc(s_w, 16)
            sp.dma_start(hdr[:, 0:4], bass.AP(tensor=w["b2"].tensor, offset=0, ap=[[0, P], [1, 4]])).then_inc(s_w, 16)
            sp.dma_start(hdr[:, 4:5], bass.AP(tensor=w["temp"].tensor, offset=0, ap=[[0, P], [1, 1]])).then_inc(s_w, 16)
            for h in range(H):
                e = slice(DK * h, DK * h + DK)
                sp.dma_start(hdr[e, 5:6], bass.AP(tensor=w["res"].tensor, offset=h, ap=[[0, DK], [1, 1]])).then_inc(s_w, 16)
                sp.dma_start(hdr[e, 6:7], w["norm"]).then_inc(s_w, 16)
            sp.dma_start(hdr[:, 7:8], w["b1"]).then_inc(s_w, 16)
            sp.wait_ge(s_w1s, 1)
            for h in range(H):
                sp.dma_start(w1s[DK * h:DK * h + 16, h, :], w["w1sT"]).then_inc(s_w, 16)
            for s in range(NSLAB):
                if s == NTR:
                    sp.wait_ge(act_job, JA.done("vR", B - 1))
                    sp.dma_start(vO[0:64], vE[64:128].rearrange("p t (h c) -> p (t h) c", h=H)).then_inc(s_vo, 16)
                    for b in range(B):
                        sp.dma_start(vO[64:128, b * GB + H:(b + 1) * GB, :],
                                     vE[0:64, b * TB:(b + 1) * TB - 1].rearrange("p t (h c) -> p (t h) c", h=H)).then_inc(s_vo, 16)
                if s >= NTR:
                    if s % 2:
                        sp.wait_ge(pe_v, JV.done("fir", (s - NTR) // 2, 1))
                    else:
                        sp.wait_ge(s_tu, (s - NTR) // 2 + 1)
                src = bass.AP(tensor=w["fir"].tensor, offset=2 * H * s * 2 * 3 * KL,
                              ap=[[1, P], [3 * KL, 2 * 2 * H], [1, KL]])
                sp.dma_start(TR[:, s % NTR].rearrange("p h d (f m) -> p (h d f) m", f=2), src).then_inc(s_t[s % NTR], 16)
            sp.wait_ge(pe_v, JV.done("lg", B - 1))
            for b in range(B):
                sp.dma_start(XR[:, b * TB:(b + 1) * TB, :], xr[:, b * TB:(b + 1) * TB, :]).then_inc(s_x[b], 16)
            xo = rows(x_out, D)
            for b in range(B):
                sp.wait_ge(dve_job, JV.done("o", b))
                sp.dma_start(xo[:, b * TB:(b + 1) * TB, :], XR[:, b * TB:(b + 1) * TB, :]).then_inc(s_out, 16)
            sp.wait_ge(s_out, 16 * B)

        @block.gpsimd
        def _(pool):
            pool.memset(eps[:, 0:1], LN_EPS)
            pool.memset(eps[:, 1:2], 1e-6)
            pool.memset(eps[:, 2:3], 1.0)
            pool.memset(w2p[:, 4:], 0.0).then_inc(s_pad, 1)
            pool.memset(w1s[:, :, :], 0.0).then_inc(s_w1s, 1)
            pool.memset(xnT[:, :, 0:TAPS - 1], 0.0).then_inc(s_pad, 2)
            pool.wait_ge(s_w, 16 * NW)
            for s in range(3):
                for j in range(TAPS):
                    ins = pool.tensor_tensor(WC[:, s, j, :], WQKV[:, s, :], CWB[:, s, j, :], ALU.mult)
            ins.then_inc(s_wc, 2)
            pool.wait_ge(s_wc, 2)
            pool.wait_ge(pe_a, JA.done("kq", 1, B - 1))
            pool.memset(vO[64:128].rearrange("p (b n) c -> p b n c", b=B)[:, :, 0:H, :], 0.0).then_inc(s_voz, 1)
            pool.wait_ge(s_bk, 1)
            pool.wait_ge(s_voz, 1)
            for b in range(B):
                gs = slice(b * GB, b * GB + GB)
                pool.wait_ge(dve_job, JV.done("kk", 2 * b + 1))
                pool.tensor_tensor(MS[:, gs, :], MS[:, gs, :], bk[:, 1, gs].to_broadcast([P, GB, C]),
                                   ALU.mult).then_inc(s_msb, 1)
            eliminate(pool, slice(3, 4), s_pool, s_elp)
            pool.wait_ge(s_el, 1)
            pool.wait_ge(s_elp, 1)
            pool.wait_ge(pe_v, JV.done("fir", NSLAB // 2 - 1, 1))
            pool.wait_ge(s_kh, 1)
            for b in range(B):
                gs = slice(b * GB, b * GB + GB)
                pool.tensor_tensor(VK[:, gs, 0, :], VH[:, gs, :], bk[:, 0, gs].to_broadcast([P, GB, C]), ALU.mult)
                pool.tensor_tensor(VK[:, gs, 1, :], AK[:, gs, 1, :], bk[:, 1, gs].to_broadcast([P, GB, C]),
                                   ALU.mult).then_inc(s_vk, 1)
            gate_pool(pool)

        @block.scalar
        def _(act):
            jobs = Jobs()

            def bank(name, *rest):
                i = jobs.next()
                assert JA.named[(name, *rest)] == i, (name, rest)
                act.wait_ge(pe_a, i + 1)
                return banks_a[i % RING]

            def copy(out, in_):
                return act.activation(out, in_, ACT.Copy)

            act.wait_ge(s_pad, 3)
            act.wait_ge(s_sd, 1)
            act.activation(rstd[:, :], mv[:, :, 1], ACT.Sqrt, bias=eps[:, 0:1]).then_inc(s_rs, 1)
            for b in range(B):
                copy(xnT[:, b, TAPS - 1:], bank("xnT", b)[:, :]).then_inc(act_job, 1)
            act.wait_ge(s_ln, NT)
            for b in range(B):
                act.activation(VT[:, b * L:(b + 1) * L], bank("v", b)[:, :], ACT.Silu).then_inc(act_job, 1)
            act.wait_ge(s_beta0, 1)
            act.activation(beta[:, :], beta[:, :], ACT.Sigmoid).then_inc(s_beta1, 1)
            for b in range(B + 1):
                if b < B:
                    for s in range(2):
                        act.activation(KQ[:, b * GB:(b + 1) * GB, s, :],
                                       bank("kq", s, b)[:, :].rearrange("p (g c) -> p g c", c=C), ACT.Silu).then_inc(act_job, 1)
                if b:
                    act.wait_ge(s_kt, b)
                    act.activation(QKH[:, (b - 1) % 4], QKH[:, (b - 1) % 4], ACT.Square).then_inc(s_sq, 1)
            act.wait_ge(s_rd, B)
            act.activation(rn[:, :, :], rn[:, :, :], ACT.Sqrt, bias=eps[:, 1:2]).then_inc(s_nrm, 1)

            for q in range(C // 4):
                copy(ME.rearrange("p h r c -> p (h r) c")[:, :, 4 * q:4 * q + 4].rearrange("p n c -> p c n"),
                     bank("me", q)[:, :].rearrange("p (c n) -> p c n", c=4)).then_inc(act_job, 1)
            act.wait_ge(s_rd, B)
            for name, dst in (("vE", v0), ("vR", vE)):
                for b in range(B):
                    copy(dst[:, b * TB:(b + 1) * TB, :].rearrange("p t c -> p (t c)"), bank(name, b)[:, :]).then_inc(act_job, 1)
            for q in range(C // 4):
                copy(TT[:, :, 4 * q:4 * q + 4].rearrange("p g r -> p r g"),
                     bank("tt", q)[:, :].rearrange("p (r g) -> p r g", r=4)).then_inc(act_job, 1)
            def ku(b):
                copy(KQ[:, b * GB:(b + 1) * GB, 0, :], bank("ku", b)[:, :].rearrange("p (g c) -> p g c", c=C)).then_inc(act_job, 1)
            for q in range(G // 8):
                copy(VK[:, 8 * q:8 * q + 8, :, :].rearrange("p g s c -> p (g s c)"), bank("uw", q)[:, :]).then_inc(act_job, 1)
            for b in range(B):
                ku(b)
            gate_act(act, bank, copy)

        @block.vector
        def _(dve):
            jobs = Jobs()
            link_n = [0]

            def link(ins):
                link_n[0] += 1
                ins.then_inc(s_dve, 1)
                dve.wait_ge(s_dve, link_n[0])

            def bank(name, *rest):
                i = jobs.next()
                assert JV.named[(name, *rest)] == i, (name, rest)
                dve.wait_ge(pe_v, i + 1)
                return banks_v[i % RING]

            bc = lambda ap, n=GB: ap.to_broadcast([P, n, C])
            for b in range(B):
                dve.wait_ge(s_x[b], 16)
                for t in range(b * TB, b * TB + TB):
                    ins = dve.bn_stats(stats6[:, t, :], X[:, t, :])
                link(ins)
                for t in range(b * TB, b * TB + TB):
                    ins = dve.bn_aggr(mv[:, t, :], stats6[:, t, :])
            ins.then_inc(s_sd, 1)
            dve.wait_ge(s_rs, 1)
            link(dve.reciprocal(rstd[:, :], rstd[:, :]))
            for t in range(NT):
                dve.tensor_scalar(xn[:, t, :], X[:, t, :], mv[:, t, 0:1], rstd[:, t:t + 1], ALU.subtract, ALU.mult).then_inc(s_ln, 1)
            dve.wait_ge(s_w, 16 * NW)
            dve.tensor_copy(bw.rearrange("p (h r) -> p h r", h=H), bwT.to_broadcast([P, H, DK])).then_inc(s_bw, 1)
            for b in range(B):
                if b:
                    dve.wait_ge(dve_job, JV.done("beta", b - 1))
                link(dve.transpose(OSCR, bank("beta", b)[:, :]))
                dve.tensor_copy(beta[:, b * GB:(b + 1) * GB], OSCR.rearrange("p (g c) -> p g c", c=C)[:, :, 0]).then_inc(dve_job, 1)
            dve.wait_ge(dve_job, JV.done("beta", B - 1))
            dve.tensor_copy(beta[:, :], beta[:, :]).then_inc(s_beta0, 1)
            for b in range(B):
                dve.wait_ge(act_job, JA.done("v", b))
                dve.transpose(VH[:, b * GB:(b + 1) * GB, :].rearrange("p g d -> p (g d)"), VT[:, b * L:(b + 1) * L])
            dve.wait_ge(s_beta1, 1)
            dve.tensor_scalar(beta[:, :], beta[:, :], 1e-6, None, ALU.max).then_inc(s_beta, 1)
            for b in range(B + 1):
                gs = slice(b * GB, b * GB + GB)
                if b < B:
                    dve.wait_ge(act_job, JA.done("kq", 1, b))
                    if b >= 4:
                        dve.wait_ge(s_rd, b - 3)
                    dve.transpose(QKH[:, b % 4, 0], KQ[:, gs, 0, :])
                    dve.transpose(QKH[:, b % 4, 1], KQ[:, gs, 1, :]).then_inc(s_kt, 1)
                if b:
                    dve.wait_ge(s_sq, b)
                    dve.tensor_reduce(rn[:, :, (b - 1) * GB:b * GB], QKH[:, (b - 1) % 4], AX.X, ALU.add).then_inc(s_rd, 1)
            dve.wait_ge(s_rd, B)
            dve.wait_ge(s_nrm, 1)
            link(dve.reciprocal(rn[:, :, :], rn[:, :, :]))
            link(dve.tensor_tensor(bk[:, 0, :], beta[:, :], rn[:, 0, :], ALU.mult))
            dve.tensor_tensor(bk[:, 1, :], bk[:, 0, :], rn[:, 0, :], ALU.mult).then_inc(s_bk, 1)
            for q in range(G // 8):
                gs = slice(8 * q, 8 * q + 8)
                kk = bank("kk", q)[:, :].rearrange("p (g s c) -> p g s c", g=8, s=2)
                dve.tensor_tensor(MS[:, gs, :], kk[:, :, 0, :], masks[:, 0:1, :].to_broadcast([P, 8, C]), ALU.mult)
                dve.tensor_tensor(AK[:, gs, 0, :], kk[:, :, 1, :], masks[:, 1:2, :].to_broadcast([P, 8, C]), ALU.mult).then_inc(dve_job, 1)
            dve.wait_ge(pe_a, JA.done("me", C // 4 - 1))
            link(dve.memset(reg(3), 0.0))
            for h in range(H):
                ins = dve.memset(reg(3)[:, h * C:h * C + (C - 1) * (P + 1) + 1:P + 1], 1.0)
            ins.then_inc(s_tz, 1)
            def filtered(n):
                q, half = n // 2, n % 2
                if n == 0:
                    dve.wait_ge(pe_a, JA.done("vR", B - 1))
                src = bank("fir", q, half)[:, :].rearrange("p (d f m) -> p d f m", d=4, f=2)
                for f in range(2):
                    dst = (LLG, LS)[f].rearrange("p (t r i) d -> p r d i t", r=2, i=2)
                    ins = dve.transpose(dst[:, half, 4 * q:4 * q + 4], src[:, :, f, :])
                ins.then_inc(dve_job, 1)

            eliminate(dve, slice(0, 3), s_elim, s_el, lambda j: filtered(j - FIR0) if 0 <= j - FIR0 < NSLAB else None)
            dve.wait_ge(pe_v, JV.done("fir", NSLAB // 2 - 1, 1))
            for b in range(B):
                gs = slice(b * GB, b * GB + GB)
                ins = dve.transpose(AK[:, gs, 1, :], KQ[:, gs, 0, :])
            ins.then_inc(s_kh, 1)
            for q in range(G // 8):
                gs = slice(8 * q, 8 * q + 8)
                qa = bank("qa", q)[:, :].rearrange("p (g s c) -> p g s c", g=8, s=2)
                dve.tensor_tensor(KQ[:, gs, 1, :], KQ[:, gs, 1, :], qa[:, :, 0, :], ALU.subtract)
                dve.tensor_tensor(AT[:, gs, :], masks[:, 2:3, :].to_broadcast([P, 8, C]), qa[:, :, 1, :], ALU.subtract).then_inc(dve_job, 1)
                if q == 0:
                    dve.wait_ge(dve_job, JV.done("kk", G // 8 - 1))
                for n in range(3 * q, 3 * q + 3):
                    k, b = (0, 1, 3)[n // 16], n % 8
                    gs = slice(b * GB, b * GB + GB)
                    if n % 16 < 8:
                        dve.tensor_reduce(S1[:, k, gs], XS[k][:, gs, :], AX.X, ALU.add)
                    else:
                        dve.tensor_reduce(MM[:, k, gs], XS[k][:, gs, :], AX.X, ALU.add, apply_absolute_value=True)
            S4 = SS.rearrange("p (b i) c -> p i b c", b=B)
            B4 = KQ[:, :, 0, :].rearrange("p (b i) c -> p i b c", b=B)
            dve.wait_ge(act_job, JA.done("ku", B - 1))
            dve.tensor_copy(S4[:, 1], B4[:, 0]).then_inc(s_scan, 1)
            D4 = DH.rearrange("p (b i) c -> p i b c", b=B)
            R4 = rn[:, 1, :].rearrange("p (b i) -> p i b", b=B)

            by_chunk = lambda sums: sums[:, 2, :].rearrange("p (b i) -> p i b", b=B)

            def output(i):
                dve.tensor_tensor(D4[:, i], bank("dh", i)[:, 0:B * C].rearrange("p (b c) -> p b c", c=C), bc(R4[:, i], B),
                                  ALU.mult).then_inc(dve_job, 1)

            def output_sums(i):
                dve.wait_ge(dve_job, JV.done("dh", i))
                dve.tensor_reduce(by_chunk(S1)[:, i], D4[:, i], AX.X, ALU.add)
                dve.tensor_reduce(by_chunk(MM)[:, i], D4[:, i], AX.X, ALU.add, apply_absolute_value=True)

            def output_squares(i):
                dve.wait_ge(s_sqd, i + 1)
                return dve.tensor_reduce(by_chunk(S2)[:, i], B4[:, i], AX.X, ALU.add)


            output(0)
            for i in range(1, GB - 1):
                ps = bank("scan", i)[:, 0:B * C].rearrange("p (b c) -> p b c", c=C)
                dve.tensor_tensor(S4[:, i + 1], ps, B4[:, i], ALU.add).then_inc(dve_job, 1)
                for n in range(2 * (i - 1), min(2 * i, 3 * B)):
                    k, b = (0, 1, 3)[n // B], n % B
                    gs = slice(b * GB, b * GB + GB)
                    dve.wait_ge(s_sqx, n // B + 1)
                    ins = dve.tensor_reduce(S2[:, k, gs], SQX[k][:, gs, :], AX.X, ALU.add)
                    if k != 1 and b == B - 1:
                        ins.then_inc(s_r2, 1)
                output(i)
                output_sums(i - 1)
                if i >= 2:
                    output_squares(i - 2)
            output(GB - 1)
            output_sums(GB - 2)
            output_squares(GB - 3)
            output_sums(GB - 1)
            output_squares(GB - 2)
            output_squares(GB - 1).then_inc(s_st, 1)
            STk = ST[:, :, 0:16].rearrange("p g (k s) -> p s k g", s=4)
            dve.wait_ge(s_st, 1)
            dve.tensor_scalar(STk[:, 0], S1, 1.0 / DK, None, ALU.mult)
            link(dve.tensor_scalar(STk[:, 2], MM, 1.0 / DK, None, ALU.mult))
            link(dve.tensor_tensor(MM, STk[:, 0], STk[:, 0], ALU.mult))
            link(dve.scalar_tensor_tensor(STk[:, 1], S2, 1.0 / DK, MM, ALU.mult, ALU.subtract))
            dve.wait_ge(s_bst, 1)
            dve.wait_ge(s_l2, 1)
            for b in range(B):
                gs = slice(b * GB, b * GB + GB)
                dve.transpose(STT[:, gs, :], ST[:, gs, :]).then_inc(s_stt, 1)
            dve.wait_ge(s_hdr2, 4)
            link(dve.tensor_scalar(hdr[:, 10:11], hdr[:, 4:5], 0.0, hdr[:, 8:9], ALU.max, ALU.add))
            dve.reciprocal(hdr[:, 10:11], hdr[:, 10:11])
            dve.tensor_scalar(wo[:, :], wo[:, :], hdr[:, 6:7], None, ALU.mult)
            dve.wait_ge(s_stt, B)

            def shares(n):
                b0, b1 = groups[n]
                for b in range(b0, b1):
                    gs = slice(b * GB, b * GB + GB)
                    dve.transpose(LG[:, gs, :].rearrange("p g s -> p (g s)"), bank("lg", b)[:, :]).then_inc(dve_job, 1)
                    dve.wait_ge(dve_job, JV.done("lg", b))
                    ins = dve.tensor_tensor(PR[:, gs, :], LG[:, gs, 0:4], hdr[:, None, 0:4].to_broadcast([P, GB, 4]), ALU.add)
                link(ins)
                gs = slice(b0 * GB, b1 * GB)
                pr, r1, r2 = PR[:, gs, :], R1[:, gs], R2[:, gs]
                shape = [P, (b1 - b0) * GB, 4]
                link(dve.tensor_reduce(r1, pr, AX.X, ALU.max))
                dve.tensor_tensor(pr, pr, r1.to_broadcast(shape), ALU.subtract).then_inc(s_e, 1)
                dve.wait_ge(s_ex, n + 1)
                for again in range(2):
                    link(dve.tensor_reduce(r1, pr, AX.X, ALU.add))
                    link(dve.reciprocal(r2, r1))
                    link(dve.tensor_tensor(pr, pr, r2.to_broadcast(shape), ALU.mult))
                    if not again:
                        link(dve.tensor_scalar(pr, pr, PROB_FLOOR, None, ALU.max))
                dve.tensor_scalar(pr[:, :, 0], pr[:, :, 0], hdr[:, 9:10], None, ALU.add).then_inc(s_p, 1)
                dve.wait_ge(s_p, n + 1)

            def mix(n):
                b0, b1 = groups[n]
                for b in range(b0, b1):
                    gs = slice(b * GB, b * GB + GB)
                    dve.tensor_tensor(OH[:, gs, :], XS[0][:, gs, :], bc(PR[:, gs, 0:1]), ALU.mult)
                    link(dve.tensor_tensor(LG[:, gs, :], XS[2][:, gs, :], bc(PR[:, gs, 2:3]), ALU.mult))
                    link(dve.tensor_tensor(OH[:, gs, :], OH[:, gs, :], LG[:, gs, :], ALU.add))
                    dve.wait_ge(s_o2, b + 1)
                    dve.tensor_tensor(OH[:, gs, :], OH[:, gs, :], O2[:, gs, :], ALU.add).then_inc(s_mix, 1)

            def sums(n):
                b0, b1 = groups[n]
                for b in range(b0, b1):
                    gs = slice(b * GB, b * GB + GB)
                    dve.wait_ge(s_o, b + 1)
                    ins = dve.tensor_reduce(R1[:, gs], OSQ[:, gs, :], AX.X, ALU.add)
                ins.then_inc(s_ms, 1)

            def finish(n):
                b0, b1 = groups[n]
                dve.wait_ge(s_rms, n + 1)
                link(dve.reciprocal(R2[:, b0 * GB:b1 * GB], R1[:, b0 * GB:b1 * GB]))
                for b in range(b0, b1):
                    gs = slice(b * GB, b * GB + GB)
                    link(dve.tensor_tensor(OH[:, gs, :], OH[:, gs, :], bc(R2[:, gs]), ALU.mult))
                    dve.transpose(OT[:, b * L:(b + 1) * L], OH[:, gs, :].rearrange("p g d -> p (g d)")).then_inc(s_oT, 1)

            for n in range(len(groups)):
                shares(n)
                if n:
                    sums(n - 1)
                mix(n)
                if n:
                    finish(n - 1)
            sums(len(groups) - 1)
            finish(len(groups) - 1)
            for b in range(B):
                dve.wait_ge(s_x[b], 32)
                xb = XR[:, b * TB:(b + 1) * TB, :].rearrange("p t d -> p (t d)")
                dve.tensor_tensor(xb, xb, bank("o", b)[:, :], ALU.add).then_inc(dve_job, 1)


E_ = 32
F = 128
CAP = -(-T * 5 // (4 * E_))
SLOTS = E_ * CAP
CH = 4
CT = CH * CAP // P


def moe(nc, sems, s_x, x0, X, mv, x_in, x_out, w, cst, xbuf, ybuf, tag):
    ctx = ExitStack()
    with ctx:
        sb = lambda name, shape, dt=F32: ctx.enter_context(nc.sbuf_tensor(f"{tag}_{name}", shape, dt))
        sem = lambda name: sems.enter_context(nc.semaphore(f"{tag}_{name}"))
        XT = sb("XT", [P, NT, D])
        first = x_in is not None
        tr = sb("tr", [P, SLOTS])
        wg, wu, wd = (sb(n, [P, E_, F]) for n in ("wg", "wu", "wd"))
        BR = sb("BR", [P, SLOTS // P, D])
        YA, YB = sb("YA", [P, E_, D]), sb("YB", [CAP - P, E_, D])
        GY = BR[:, 0:NT, :]
        wr, ident, eps = sb("wr", [P, E_]), sb("ident", [P, P]), sb("eps", [P, 1])
        tri, ones = sb("tri", [P, P], BF16), sb("ones", [P, P], BF16)
        trif = sb("trif", [P, P])
        stats6, rstd = sb("stats6", [P, NT, 6]), sb("rstd", [P, NT])
        rank, dump = sb("rank", [P, E_]), sb("dump", [P, NT])
        LG, EX = sb("LG", [P, NT, E_]), sb("EX", [P, NT, E_])
        OL = sb("OL", [P, NT, E_])
        OH, PO = sb("OH", [P, NT, E_], BF16), sb("PO", [P, NT, E_], BF16)
        row = sb("row", [P, 8, NT])
        mx, best, pos, slot, acc, gate, sidx, gidx = (row[:, i, :] for i in range(8))
        si, gi = sb("si", [P, NT], I32), sb("gi", [P, NT], I32)
        SG, hT = sb("SG", [P, 2, CAP]), sb("hT", [P, 4, CAP])
        zero = sb("zero", [P, 1280])
        banks_a = [ctx.enter_context(nc.psum_tensor(f"{tag}_pa{i}", [P, 512], F32)) for i in range(RING)]
        banks_v = [ctx.enter_context(nc.psum_tensor(f"{tag}_pv{i}", [P, 512], F32)) for i in range(RING)]
        pe_a, pe_v, act_job, dve_job = (sem(n) for n in ("pe_a", "pe_v", "act_job", "dve_job"))
        s_gy = [sem(f"gy{b}") for b in range(B)]
        s_c, s_w, s_z, s_zf, s_sd, s_rs, s_ln, s_dve, s_bf, s_lg, s_ex, s_oh, s_idx, s_sc, s_sg, s_y, s_xs, s_out = (
            sem(n) for n in ("c", "w", "z", "zf", "sd", "rs", "ln", "dve", "bf", "lg", "ex", "oh", "idx", "sc", "sg", "y", "xs", "out"))
        JA, JV = Jobs(), Jobs()
        block = ctx.enter_context(nc.Block())

        @block.tensor
        def _(pe):
            def bank_a(*name):
                i = JA.next(*name)
                if i >= RING:
                    pe.wait_ge(act_job, i - RING + 1)
                return banks_a[i % RING]

            def bank_v(*name):
                i = JV.next(*name)
                if i >= RING:
                    pe.wait_ge(dve_job, i - RING + 1)
                return banks_v[i % RING]

            pe.wait_ge(s_c, 16 * 5)
            def tokens(k):
                for b in range(4 * k, 4 * k + 4):
                    bank = bank_a("xT", b)
                    for j in range(TB):
                        pe.wait_ge(s_ln, b * TB + j + 1)
                        mm = pe.transpose(bank[:, j * P:(j + 1) * P], XT[:, b * TB + j, :], ident[:, :])
                    mm.then_inc(pe_a, 1)

            tokens(0)
            pe.wait_ge(s_bf, 2)
            for k in range(2):
                bank = bank_v("lg", k)
                for t in range(16 * k, 16 * k + 16):
                    if t % TB == 0:
                        pe.wait_ge(act_job, JA.done("xT", t // TB))
                    mm = pe.matmul(bank[:, (t % 16) * E_:(t % 16 + 1) * E_], tr[:, t * P:(t + 1) * P], wr[:, :], start=True, stop=True)
                mm.then_inc(pe_v, 1)
                if k == 0:
                    tokens(1)
                pe.wait_ge(s_oh, k + 1)
                bank = bank_v("pos", k)
                ts = slice(16 * k, 16 * k + 16)
                pe.matmul(bank[:, :], tri[:, :], OH[:, ts, :].rearrange("p t e -> p (t e)"), start=True, stop=False)
                pe.matmul(bank[:, :], ones[:, :], PO[:, ts, :].rearrange("p t e -> p (t e)"), start=False, stop=True).then_inc(pe_v, 1)
            pe.wait_ge(s_w, 16 * 3)

            def down(e):
                if e % 2 == 0:
                    down.bank = bank_a("y", e // 2)
                o = (e % 2) * 2 * D
                pe.wait_ge(dve_job, JV.done("gu", e))
                pe.matmul(down.bank[:, o:o + D], hT[:, e % 4, 0:P], wd[:, e, :], start=True, stop=True)
                mm = pe.matmul(down.bank[0:CAP - P, o + D:o + 2 * D], hT[:, e % 4, P:CAP], wd[:, e, :], start=True, stop=True)
                if e % 2:
                    mm.then_inc(pe_a, 1)

            def turn(c):
                pe.wait_ge(s_x[c], x0 + 16 + 16 * first)
                for k in range(0, CT, 4):
                    bank = bank_a("bt", c, k)
                    for j in range(k, min(k + 4, CT)):
                        mm = pe.transpose(bank[:, (j - k) * P:(j - k + 1) * P], BR[:, CT * c + j, :], ident[:, :])
                    mm.then_inc(pe_a, 1)

            turn(0)
            for e in range(E_):
                if e % CH == 2 and e + CH < E_:
                    turn(e // CH + 1)
                if e % CH == 0:
                    pe.wait_ge(act_job, JA.done("bt", e // CH, CT - CT % 4 if CT % 4 else CT - 4))
                bank = bank_v("gu", e)
                pe.matmul(bank[:, 0:CAP], wg[:, e, :], tr[:, e * CAP:(e + 1) * CAP], start=True, stop=True)
                pe.matmul(bank[:, CAP:2 * CAP], wu[:, e, :], tr[:, e * CAP:(e + 1) * CAP], start=True, stop=True).then_inc(pe_v, 1)
                if e >= 2:
                    down(e - 2)
            down(E_ - 2)
            down(E_ - 1)

        @block.sync
        def _(sp):
            for b in range(B if first else 0):
                xr = rows(x_in, D)
                sp.dma_start(X[:, b * TB:(b + 1) * TB, :], xr[:, b * TB:(b + 1) * TB, :]).then_inc(s_x[b], 16)
            for dst, src in ((ident, "ident"), (trif, "tri"), (rank, "rank"), (dump, "dump")):
                sp.dma_start(dst[:, :], cst[src]).then_inc(s_c, 16)
            sp.dma_start(wr[:, :], w["router"]).then_inc(s_c, 16)
            if first:
                sp.wait_ge(s_z, 2)
                sp.dma_start(xbuf[0:SLOTS, :].rearrange("(p r) d -> p (r d)", p=P)[:, 0:2560],
                             zero[:, None, :].to_broadcast([P, 2, 1280])).then_inc(s_zf, 16)
                sp.dma_start(xbuf[0:SLOTS, :].rearrange("(p r) d -> p (r d)", p=P)[:, 2560:5120],
                             zero[:, None, :].to_broadcast([P, 2, 1280])).then_inc(s_zf, 16)
                sp.dma_start(ybuf[SLOTS:SLOTS + 1, :], zero[0:1, 0:D]).then_inc(s_zf, 16)
            for dst, src in ((wg, "gate"), (wu, "up"), (wd, "down")):
                sp.dma_start(dst[:, :, :], w[src].rearrange("e h f -> h e f")).then_inc(s_w, 16)
            sp.wait_ge(s_sc, 16 * NT)
            for c in range(E_ // CH):
                sp.dma_start(BR[:, CT * c:CT * c + CT, :],
                             xbuf[c * CT * P:(c + 1) * CT * P, :].rearrange("(t p) d -> p t d", p=P)).then_inc(s_x[c], 16)
            yr = ybuf[0:SLOTS, :].rearrange("(e s) d -> s e d", s=CAP)
            for c in range(E_ // CH):
                es = slice(CH * c, CH * c + CH)
                sp.wait_ge(act_job, JA.done("y", (CH * c + CH) // 2 - 1))
                sp.dma_start(yr[0:P, es, :], YA[:, es, :]).then_inc(s_y, 16)
                sp.dma_start(yr[P:CAP, es, :], YB[:, es, :]).then_inc(s_y, 16)
            if x_out is None:
                return
            xo = rows(x_out, D)
            for b in range(B):
                sp.wait_ge(s_xs, b + 1)
                sp.dma_start(xo[:, b * TB:(b + 1) * TB, :], X[:, b * TB:(b + 1) * TB, :]).then_inc(s_out, 16)
            sp.wait_ge(s_out, 16 * B)

        @block.gpsimd
        def _(pool):
            pool.memset(eps[:, :], LN_EPS).then_inc(s_z, 1)
            if first:
                pool.memset(zero[:, :], 0.0).then_inc(s_z, 1)
            pool.memset(ones[:, :], 1.0).then_inc(s_bf, 1)
            pool.wait_ge(s_c, 16 * 5)
            pool.tensor_copy(tri[:, :], trif[:, :]).then_inc(s_bf, 1)
            if first:
                pool.wait_ge(s_zf, 16 * 3)
            for t in range(NT):
                if t % 16 == 0:
                    pool.wait_ge(s_idx, t // 16 + 1)
                pool.indirect_dma_start(xbuf, bass.IndirectOffsetOnAxis(ap=si[:, t:t + 1], axis=0), XT[:, t, :], None).then_inc(s_sc, 16)
            pool.wait_ge(s_y, 16 * 2 * E_ // CH)
            for t in range(NT):
                pool.indirect_dma_start(GY[:, t, :], None, ybuf, bass.IndirectOffsetOnAxis(ap=gi[:, t:t + 1], axis=0)).then_inc(s_gy[t // TB], 16)

        @block.scalar
        def _(act):
            jobs = Jobs()

            def bank(name, *rest):
                i = jobs.next()
                assert JA.named[(name, *rest)] == i, (name, rest)
                act.wait_ge(pe_a, i + 1)
                return banks_a[i % RING]

            def copy(out, in_):
                return act.activation(out, in_, ACT.Copy)

            act.wait_ge(s_z, 1)
            for k in range(2):
                ts = slice(16 * k, 16 * k + 16)
                if first:
                    act.wait_ge(s_sd, k + 1)
                act.activation(rstd[:, ts], mv[:, ts, 1], ACT.Sqrt, bias=eps[:, 0:1]).then_inc(s_rs, 1)
            for k in range(2):
                for b in range(4 * k, 4 * k + 4):
                    copy(tr[:, b * L:(b + 1) * L], bank("xT", b)[:, :]).then_inc(act_job, 1)
                act.wait_ge(s_lg, k + 1)
                act.activation(EX[:, 16 * k:16 * k + 16, :], LG[:, 16 * k:16 * k + 16, :], ACT.Exp).then_inc(s_ex, 1)

            def turn(c):
                for k in range(0, CT, 4):
                    n = min(4, CT - k) * P
                    if c == 0 and k == 0:
                        act.wait_ge(pe_v, JV.done("lg", 1))
                    copy(tr[:, (c * CT + k) * P:(c * CT + k) * P + n], bank("bt", c, k)[:, 0:n]).then_inc(act_job, 1)

            def y(q):
                src = bank("y", q)[:, :].rearrange("p (e s d) -> p e s d", e=2, s=2)
                copy(YA[:, 2 * q:2 * q + 2, :], src[:, :, 0, :])
                copy(YB[:, 2 * q:2 * q + 2, :], src[0:CAP - P, :, 1, :]).then_inc(act_job, 1)

            turn(0)
            for e in range(E_):
                if e >= 3 and e % 2:
                    y((e - 3) // 2)
                if e % CH == 2 and e + CH < E_:
                    turn(e // CH + 1)
                act.wait_ge(pe_v, JV.done("gu", e))
                if e >= 2:
                    act.wait_ge(dve_job, JV.done("gu", e - 2))
                act.activation(SG[:, e % 2, :], banks_v[JV.named[("gu", e)] % RING][:, 0:CAP], ACT.Silu).then_inc(s_sg, 1)
            y(E_ // 2 - 1)

        @block.vector
        def _(dve):
            jobs = Jobs()
            link_n = [0]

            def link(ins):
                link_n[0] += 1
                ins.then_inc(s_dve, 1)
                dve.wait_ge(s_dve, link_n[0])

            def bank(name, *rest):
                i = jobs.next()
                assert JV.named[(name, *rest)] == i, (name, rest)
                dve.wait_ge(pe_v, i + 1)
                return banks_v[i % RING]

            def statistics(b):
                for t in range(b * TB, b * TB + TB):
                    ins = dve.bn_stats(stats6[:, t, :], X[:, t, :])
                link(ins)
                for t in range(b * TB, b * TB + TB):
                    ins = dve.bn_aggr(mv[:, t, :], stats6[:, t, :])
                return ins

            for b in range(B if first else 0):
                dve.wait_ge(s_x[b], x0 + 16)
                ins = statistics(b)
                if b % 4 == 3:
                    ins.then_inc(s_sd, 1)
            for k in range(2):
                dve.wait_ge(s_rs, k + 1)
                link(dve.reciprocal(rstd[:, 16 * k:16 * k + 16], rstd[:, 16 * k:16 * k + 16]))
                for t in range(16 * k, 16 * k + 16):
                    dve.tensor_scalar(XT[:, t, :], X[:, t, :], mv[:, t, 0:1], rstd[:, t:t + 1], ALU.subtract, ALU.mult).then_inc(s_ln, 1)
            dve.wait_ge(s_c, 16 * 5)
            link(dve.memset(PO[:, 0, :], 0.0))
            for k in range(2):
                ts = slice(16 * k, 16 * k + 16)
                n = [P, 16, E_]
                src = bank("lg", k)[:, :].rearrange("p (t e) -> p t e", e=E_)
                link(dve.tensor_reduce(mx[:, ts], src, AX.X, ALU.max))
                dve.tensor_tensor(LG[:, ts, :], src, mx[:, ts].to_broadcast(n), ALU.subtract).then_inc(dve_job, 1)
                dve.wait_ge(dve_job, JV.done("lg", k))
                dve.tensor_scalar(OL[:, ts, :], LG[:, ts, :], 0.0, None, ALU.is_equal).then_inc(s_lg, 1)
                dve.wait_ge(s_lg, k + 1)
                link(dve.tensor_tensor(OL[:, ts, :], OL[:, ts, :], rank[:, None, :].to_broadcast(n), ALU.mult))
                link(dve.tensor_reduce(best[:, ts], OL[:, ts, :], AX.X, ALU.max))
                link(dve.tensor_tensor(OH[:, ts, :], OL[:, ts, :], best[:, ts].to_broadcast(n), ALU.is_equal))
                for t in range(max(16 * k, 1), 16 * k + 16):
                    ins = dve.tensor_tensor(PO[:, t, :], PO[:, t - 1, :], OH[:, t - 1, :], ALU.add)
                    if t % 16 < 15:
                        link(ins)
                ins.then_inc(s_oh, 1)
                dve.wait_ge(s_oh, k + 1)
                dve.wait_ge(s_ex, k + 1)
                link(dve.tensor_reduce(gate[:, ts], EX[:, ts, :], AX.X, ALU.add))
                link(dve.reciprocal(gate[:, ts], gate[:, ts]))
                dve.tensor_tensor(EX[:, ts, :], bank("pos", k)[:, :].rearrange("p (t e) -> p t e", e=E_), OH[:, ts, :], ALU.mult).then_inc(dve_job, 1)
                dve.wait_ge(dve_job, JV.done("pos", k))
                link(dve.tensor_reduce(pos[:, ts], EX[:, ts, :], AX.X, ALU.add))
                dve.tensor_scalar(acc[:, ts], pos[:, ts], float(CAP), None, ALU.is_le)
                link(dve.scalar_tensor_tensor(slot[:, ts], best[:, ts], -float(CAP), pos[:, ts], ALU.mult, ALU.add))
                link(dve.tensor_scalar(slot[:, ts], slot[:, ts], float(SLOTS - 1), None, ALU.add))
                dve.tensor_tensor(sidx[:, ts], slot[:, ts], dump[:, ts], ALU.subtract)
                link(dve.tensor_scalar(gidx[:, ts], slot[:, ts], -float(SLOTS), None, ALU.add))
                dve.tensor_tensor(sidx[:, ts], sidx[:, ts], acc[:, ts], ALU.mult)
                dve.tensor_tensor(gate[:, ts], gate[:, ts], acc[:, ts], ALU.mult)
                link(dve.tensor_tensor(gidx[:, ts], gidx[:, ts], acc[:, ts], ALU.mult))
                link(dve.tensor_tensor(sidx[:, ts], sidx[:, ts], dump[:, ts], ALU.add))
                dve.tensor_scalar(gi[:, ts], gidx[:, ts], float(SLOTS), None, ALU.add)
                dve.tensor_copy(si[:, ts], sidx[:, ts]).then_inc(s_idx, 1)
            for b in range(B):
                ts = slice(b * TB, b * TB + TB)
                ins = dve.tensor_tensor(X[:, ts, :], X[:, ts, :], XT[:, ts, :], ALU.add)
            link(ins)
            for e in range(E_):
                src = bank("gu", e)
                dve.wait_ge(s_sg, e + 1)
                if e >= 4:
                    dve.wait_ge(pe_a, JA.done("y", (e - 4) // 2))
                dve.tensor_tensor(hT[:, e % 4, :], src[:, CAP:2 * CAP], SG[:, e % 2, :], ALU.mult).then_inc(dve_job, 1)
            for b in range(B):
                dve.wait_ge(s_gy[b], 16 * TB)
                for t in range(b * TB, b * TB + TB):
                    ins = dve.scalar_tensor_tensor(X[:, t, :], GY[:, t, :], gate[:, t:t + 1], X[:, t, :], ALU.mult, ALU.add)
                ins.then_inc(s_xs, 1)
                if x_out is None:
                    dve.wait_ge(s_xs, b + 1)
                    statistics(b)


HB, DB = 16, D // 16
CLAMP = 1e5
Q_PART = (0, 0, 1, 1, 0, 2)
K_PART = (0, 1, 0, 1, 2, 0)
NTERM = len(Q_PART)
MAXROW = NTERM * DB
SEC = (0, 512, 896, 1152)
PW = 1280


def attn_b(nc, sems, X, mv, w, cst, stack):
    ctx = ExitStack()
    with ctx:
        sb = lambda name, shape, dt=F32: ctx.enter_context(nc.sbuf_tensor(f"b_{name}", shape, dt))
        sem = lambda name: sems.enter_context(nc.semaphore(f"b_{name}"))
        xn, xnT = sb("xn", [P, 2 * TB, D]), sb("xnT", [P, 2, L])
        wp = sb("wp", [P, 5, D])
        rope = sb("rope", [P, 4, L])
        WO = sb("WO", [P, D])
        ident, eps = sb("ident", [P, P]), sb("eps", [P, 1])
        identb, mqf, mq, mk = sb("identb", [P, P], BF16), sb("mqf", [P, 2, P]), sb("mq", [P, P], BF16), sb("mk", [P, P], BF16)
        stats6, rstd = sb("stats6", [P, NT, 6]), sb("rstd", [P, NT])
        RT = sb("RT", [P, 2, 2, L])
        PS = sb("PS", [P, 2, 2, 3, L], BF16)
        QS, KS = sb("QS", [P, 2, HB, L], BF16), sb("KS", [P, 2, HB, L], BF16)
        zr = sb("zr", [3, L], BF16)
        VX = sb("VX", [P, 3, TB, HB, 32])
        PB = sb("PB", [P, 8, PW])
        MX, MR = sb("MX", [P, TB, HB]), sb("MR", [P, TB, HB])
        N3 = sb("N3", [P, TB, 3, HB], BF16)
        NMT = sb("NMT", [3 * HB, L], BF16)
        OT, RC, OTK, OTT = sb("OT", [P, 2, L]), sb("RC", [P, TB, 4]), sb("OTK", [P, TB, D]), sb("OTT", [P, L])
        banks_a = [ctx.enter_context(nc.psum_tensor(f"b_pa{i}", [P, 512], F32)) for i in range(RING)]
        banks_v = [ctx.enter_context(nc.psum_tensor(f"b_pv{i}", [P, 512], F32)) for i in range(RING)]
        pe_a, pe_v, act_job, dve_job = (sem(n) for n in ("pe_a", "pe_v", "act_job", "dve_job"))
        (s_c, s_set, s_cb, s_rs, s_ln, s_dve, s_sp, s_sa, s_ps, s_nm, s_cp, s_cd, s_qz, s_vx) = (
            sem(n) for n in ("c", "set", "cb", "rs", "ln", "dve", "sp", "sa", "ps", "nm", "cp", "cd", "qz", "vx"))
        s_st = [sem(f"st{i}") for i in range(2)]
        s_ld = [sem(f"ld{i}") for i in range(2)]
        s_mr = [sem(f"mr{i}") for i in range(2)]
        JA, JV = Jobs(), Jobs()
        NC = 5
        LOADS = 16 * (2 * NTERM + 1)

        amax = [(q, h, n) for q, n in ((0, 4), (1, 2), (2, 1), (3, 1)) for h in range(0, HB, n)]

        def steps():
            yield "xT", 0, 0
            yield "xT", 1, 0
            for b in range(2):
                for k in range(4):
                    yield "qk", b, k
                    if k % 2:
                        yield "split", b, 5 * (k // 2)
                yield "v", b, 0
            for i in range(len(amax)):
                yield "max", 0, i
            yield "take", 0, 0
            yield "turn", 0, 0
            for b in range(B):
                for h in range(HB):
                    yield "probs", b, h
                    if b + 1 < B and 3 <= h < 14:
                        for i in range(len(amax) * (h - 3) // 11, len(amax) * (h - 2) // 11):
                            yield "max", b + 1, i
                    if h == 13 and b + 1 < B:
                        yield "take", b + 1, 0
                    if h == 14 and b + 1 < B:
                        yield "turn", b + 1, 0
                    if h == 15 and b + 3 < B or b == 0 and h == 0:
                        c = b + 3 if h else 2
                        yield "xT", c, 0
                        yield "qk", c, 0
                        yield "qk", c, 1
                    if b + 2 < B:
                        if h == 1:
                            yield "qk", b + 2, 2
                        if h == 2:
                            yield "qk", b + 2, 3
                        if h == 6:
                            yield "v", b + 2, 0
                        if 2 <= h < 7:
                            yield "split", b + 2, h - 2
                        if 4 <= h < 9:
                            yield "split", b + 2, 5 + h - 4
                    c, j = (b, h // 4 - 1) if h >= 4 else (b - 1, 3)
                    if c >= 0 and h % 4 == 1:
                        yield "values", c, j
                    if c >= 0 and h % 4 == 3:
                        yield "norm", c, j
                    if b and h == 4:
                        yield "oT", b - 1, 0
                    if b and h == 5:
                        yield "out", b - 1, 0
                if b + 2 < B:
                    yield "load", b + 2, 0
            yield "values", B - 1, 3
            yield "norm", B - 1, 3
            yield "oT", B - 1, 0
            yield "out", B - 1, 0

        def load(sp, b):
            s = b % 2
            sp.wait_ge(s_st[s], 32 * (b // 2 + 1))
            sp.wait_ge(s_set, 3 + s)
            sp.wait_ge(s_qz, 1 + s)
            if b >= 2:
                sp.wait_ge(pe_a, JA.done("sc", b - 2, HB - 1, 2))
            for t in range(NTERM):
                e = slice(DB * t, DB * t + DB)
                for k, (S, part) in enumerate(((QS, Q_PART), (KS, K_PART))):
                    sp.dma_start(S[e, s, :, :], stack[s, k, part[t]].rearrange("(h d) t -> d h t", d=DB)).then_inc(s_ld[s], 16)
            sp.dma_start(QS[MAXROW:MAXROW + 3, s, :, :], zr[:, None, :].to_broadcast([3, HB, L])).then_inc(s_ld[s], 16)

        block = ctx.enter_context(nc.Block())

        @block.tensor
        def _(pe):
            def bank_a(*name):
                i = JA.next(*name)
                if i >= RING:
                    pe.wait_ge(act_job, i - RING + 1)
                return banks_a[i % RING]

            def bank_v(*name):
                i = JV.next(*name)
                if i >= RING:
                    pe.wait_ge(dve_job, i - RING + 1)
                return banks_v[i % RING]

            pe.wait_ge(s_c, 16 * NC)
            for step, b, i in steps():
                s = b % 2
                if step == "xT":
                    bank = bank_a("xT", b)
                    for j in range(TB):
                        pe.wait_ge(s_ln, b * TB + j + 1)
                        mm = pe.transpose(bank[:, j * P:(j + 1) * P], xn[:, s * TB + j, :], ident[:, :])
                    mm.then_inc(pe_a, 1)
                elif step == "qk":
                    pe.wait_ge(act_job, JA.done("xT", b))
                    bank = bank_v("qk", b, i)
                    pe.matmul(bank[:, :], wp[:, i, :], xnT[:, s, :], start=True, stop=True).then_inc(pe_v, 1)
                elif step == "v":
                    bank = bank_a("v", b)
                    for j in range(TB):
                        mm = pe.matmul(bank[:, j * P:(j + 1) * P], xnT[:, s, j * P:(j + 1) * P], wp[:, 4, :], start=True, stop=True)
                    mm.then_inc(pe_a, 1)
                elif step == "max":
                    q, h0, n = amax[i]
                    if i == 0:
                        pe.wait_ge(s_cb, 3)
                        pe.wait_ge(s_ld[s], LOADS * (b // 2 + 1))
                    bank = bank_v("max", b, i)
                    wd = (q + 1) * P
                    for h in range(h0, h0 + n):
                        o = (h - h0) * wd
                        pe.matmul(bank[:, o:o + wd], QS[:, s, h, q * P:wd], KS[:, s, h, 0:wd], start=True, stop=False)
                        mm = pe.matmul(bank[:, o + q * P:o + wd], identb[:, :], mq[:, :], start=False, stop=True)
                    mm.then_inc(pe_v, 1)
                elif step == "turn":
                    bank = bank_a("nm", b)
                    pe.wait_ge(s_nm, b + 1)
                    for j in range(TB):
                        mm = pe.transpose(bank[:, 0:256].bitcast(BF16)[0:3 * HB, j * P:(j + 1) * P],
                                          N3[:, j, :, :].rearrange("p a h -> p (a h)"), identb[:, :])
                    mm.then_inc(pe_a, 1)
                elif step == "probs":
                    h = i
                    if h == 0:
                        pe.wait_ge(s_mr[s], 48 * (b // 2 + 1))
                    for part in ((0,), (1,), (2, 3)):
                        bank = bank_a("sc", b, h, part[0])
                        o = 0
                        for kt in part:
                            n = L - kt * P
                            pe.matmul(bank[:, o:o + n], KS[:, s, h, kt * P:(kt + 1) * P], QS[:, s, h, kt * P:L], start=True, stop=False)
                            mm = pe.matmul(bank[:, o:o + P], identb[:, :], mk[:, :], start=False, stop=True)
                            o += n
                        mm.then_inc(pe_a, 1)
                elif step == "values":
                    bank = bank_a("pv", b, i)
                    n = b * HB + 4 * i + 4
                    pe.wait_ge(s_cd, n)
                    pe.wait_ge(s_cp, n)
                    for kt in range(TB):
                        for j in range(4):
                            h = 4 * i + j
                            mm = pe.matmul(bank[32 * j:32 * j + 32, kt * P:L], VX[:, b % 3, kt, h, :],
                                           PB[:, h % 8, SEC[kt]:SEC[kt] + L - kt * P], start=kt == 0, stop=kt == TB - 1)
                    mm.then_inc(pe_a, 1)
                elif step == "norm":
                    bank = bank_v("den", b, i)
                    pe.wait_ge(act_job, JA.done("pv", b, i))
                    for j in range(TB):
                        mm = pe.transpose(bank[:, j * P:(j + 1) * P], OT[:, i % 2, j * P:(j + 1) * P], ident[:, :])
                    mm.then_inc(pe_v, 1)
                elif step == "oT":
                    bank = bank_a("oT", b)
                    pe.wait_ge(dve_job, JV.done("den", b, 3))
                    for j in range(TB):
                        mm = pe.transpose(bank[:, j * P:(j + 1) * P], OTK[:, j, :], ident[:, :])
                    mm.then_inc(pe_a, 1)
                elif step == "out":
                    bank = bank_v("out", b)
                    pe.wait_ge(act_job, JA.done("oT", b))
                    for j in range(TB):
                        mm = pe.matmul(bank[:, j * P:(j + 1) * P], OTT[:, j * P:(j + 1) * P], WO[:, :], start=True, stop=True)
                    mm.then_inc(pe_v, 1)

        @block.sync
        def _(sp):
            sp.dma_start(ident[:, :], cst["ident"]).then_inc(s_c, 16)
            sp.dma_start(mqf[:, :, :], cst["causal"]).then_inc(s_c, 16)
            sp.dma_start(rope[:, :, :], cst["rope"]).then_inc(s_c, 16)
            sp.dma_start(wp[:, :, :], w["qkv"]).then_inc(s_c, 16)
            sp.dma_start(WO[:, :], w["o"]).then_inc(s_c, 16)
            for step, b, i in steps():
                s = b % 2
                if step == "split" and (i % 5 == 4 or b < 2):
                    k = i // 5
                    sp.wait_ge(s_ps, 2 * b + k + 1)
                    if b >= 2:
                        sp.wait_ge(s_ld[s], LOADS * (b // 2))
                    sp.dma_start(stack[s, k].rearrange("a p t -> p a t"), PS[:, s, k, :, :]).then_inc(s_st[s], 16)
                elif step == "load" or step == "v" and b < 2:
                    load(sp, b)
                elif step == "turn":
                    sp.wait_ge(act_job, JA.done("nm", b))
                    for a in range(3):
                        sp.dma_start(QS[MAXROW + a:MAXROW + a + 1, s, :, :], NMT[a * HB:(a + 1) * HB, :]).then_inc(s_mr[s], 16)


        @block.gpsimd
        def _(pool):
            pool.memset(eps[:, :], LN_EPS).then_inc(s_set, 1)
            pool.memset(zr[:, :], 0.0).then_inc(s_set, 1)
            pool.memset(VX[:, :, :, :, :], 0.0).then_inc(s_vx, 1)
            pool.wait_ge(s_vx, 1)
            pool.memset(VX[:, :, :, :, DB], 1.0).then_inc(s_vx, 1)
            for s in range(2):
                pool.memset(KS[:, s], 1.0).then_inc(s_set, 1)
            pool.wait_ge(s_c, 16 * NC)
            pool.tensor_copy(identb[:, :], ident[:, :]).then_inc(s_cb, 1)
            pool.tensor_copy(mq[:, :], mqf[:, 0, :]).then_inc(s_cb, 1)
            pool.tensor_copy(mk[:, :], mqf[:, 1, :]).then_inc(s_cb, 1)
            def clamp(n):
                b, h = n // HB, n % HB
                pool.wait_ge(act_job, JA.done("sc", b, h, 0))
                e = PB[:, h % 8, 0:512]
                pool.tensor_scalar(e, e, 1.0, None, ALU.min).then_inc(s_cp, 1)

            for step, b, i in steps():
                s = b % 2
                if step == "split" and b >= 2:
                    k, j = i // 5, i % 5
                    m = 2 * (b - 2) + k
                    a, r, part = RT[:, k, 0, :], RT[:, k, 1, :], PS[:, s, k, :, :]
                    if j == 0:
                        pool.wait_ge(dve_job, JV.done("qk", b, 2 * k + 1))
                        pool.tensor_tensor(a, a, r, ALU.add).then_inc(s_sp, 1)
                    elif j == 2:
                        pool.wait_ge(s_sa, 2 * m + 1)
                        pool.tensor_tensor(r, a, part[:, 0, :], ALU.subtract).then_inc(s_sp, 1)
                    elif j == 4:
                        pool.wait_ge(s_sa, 2 * m + 2)
                        pool.tensor_tensor(part[:, 2, :], r, part[:, 1, :], ALU.subtract).then_inc(s_ps, 1)
                elif step == "probs" and b + i:
                    clamp(b * HB + i - 1)
                elif step == "values" and b == B - 1 and i == 3:
                    clamp(B * HB - 1)

        @block.scalar
        def _(act):
            jobs = Jobs()

            def bank(name, *rest):
                i = jobs.next()
                assert JA.named[(name, *rest)] == i, (name, rest)
                act.wait_ge(pe_a, i + 1)
                return banks_a[i % RING]

            def copy(out, in_):
                return act.activation(out, in_, ACT.Copy)

            act.wait_ge(s_set, 1)
            act.activation(rstd[:, :], mv[:, :, 1], ACT.Sqrt, bias=eps[:, 0:1]).then_inc(s_rs, 1)
            for step, b, i in steps():
                s = b % 2
                if step == "xT":
                    if b >= 2:
                        act.wait_ge(pe_a, JA.done("v", b - 2))
                    copy(xnT[:, s, :], bank("xT", b)[:, :]).then_inc(act_job, 1)
                elif step == "v":
                    if b == 0:
                        act.wait_ge(s_vx, 2)
                    if b >= 3:
                        act.wait_ge(pe_a, JA.done("pv", b - 3, 3))
                    copy(VX[:, b % 3, :, :, 0:DB].rearrange("p k h d -> p (k h) d"),
                         bank("v", b)[:, :].rearrange("p (n d) -> p n d", d=DB)).then_inc(act_job, 1)
                elif step == "split" and b >= 2 and i % 5 in (1, 3):
                    k, j = i // 5, i % 5 // 2
                    if j == 0:
                        act.wait_ge(s_st[s], 32 * (b // 2))
                    act.wait_ge(s_sp, 2 * (2 * (b - 2) + k) + j + 1)
                    copy(PS[:, s, k, j, :], RT[:, k, j, :]).then_inc(s_sa, 1)
                elif step == "turn":
                    if b:
                        act.wait_ge(s_mr[1 - s], 48 * ((b - 1) // 2 + 1))
                    copy(NMT[:, :], bank("nm", b)[:, 0:256].bitcast(BF16)[0:3 * HB, :]).then_inc(act_job, 1)
                elif step == "probs":
                    n = b * HB + i
                    if n >= 8:
                        act.wait_ge(pe_a, JA.done("pv", (n - 8) // HB, (n - 8) % HB // 4))
                    for o, e, part in ((0, 512, 0), (512, 896, 1), (896, PW, 2)):
                        act.activation(PB[:, i % 8, o:e], bank("sc", b, i, part)[:, 0:e - o], ACT.Exp).then_inc(act_job, 1)
                elif step == "values":
                    n = 4 * b + i
                    if n >= 2:
                        act.wait_ge(pe_v, JV.done("den", (n - 2) // 4, (n - 2) % 4))
                    copy(OT[:, i % 2, :], bank("pv", b, i)[:, :]).then_inc(act_job, 1)
                elif step == "oT":
                    if b:
                        act.wait_ge(pe_v, JV.done("out", b - 1))
                    copy(OTT[:, :], bank("oT", b)[:, :]).then_inc(act_job, 1)

        @block.vector
        def _(dve):
            jobs = Jobs()
            link_n = [0]

            def link(ins):
                link_n[0] += 1
                ins.then_inc(s_dve, 1)
                dve.wait_ge(s_dve, link_n[0])

            def bank(name, *rest):
                i = jobs.next()
                assert JV.named[(name, *rest)] == i, (name, rest)
                dve.wait_ge(pe_v, i + 1)
                return banks_v[i % RING]

            def clamp(n):
                b, h = n // HB, n % HB
                dve.wait_ge(act_job, JA.done("sc", b, h, 2))
                e = PB[:, h % 8, 512:PW]
                dve.tensor_scalar(e, e, 1.0, None, ALU.min).then_inc(s_cd, 1)

            dve.wait_ge(s_rs, 1)
            link(dve.reciprocal(rstd[:, :], rstd[:, :]))
            for step, b, i in steps():
                s = b % 2
                if step == "xT":
                    if b == 1:
                        dve.memset(QS[:, 0].rearrange("p h t -> p (h t)").bitcast(F32), 0.0).then_inc(s_qz, 1)
                    if b >= 2:
                        dve.wait_ge(pe_a, JA.done("xT", b - 2))
                    for t in range(b * TB, b * TB + TB):
                        dve.tensor_scalar(xn[:, t % (2 * TB), :], X[:, t, :], mv[:, t, 0:1], rstd[:, t:t + 1],
                                          ALU.subtract, ALU.mult).then_inc(s_ln, 1)
                elif step == "v" and b == 0:
                    dve.memset(QS[:, 1].rearrange("p h t -> p (h t)").bitcast(F32), 0.0).then_inc(s_qz, 1)
                elif step == "qk":
                    if i == 0:
                        dve.wait_ge(s_c, 16 * NC)
                    if b:
                        dve.wait_ge(s_ps, 2 * b)
                    dve.tensor_tensor(RT[:, i // 2, i % 2, :], bank("qk", b, i)[:, :], rope[:, i, :], ALU.mult).then_inc(dve_job, 1)
                elif step == "split" and b < 2:
                    k = i // 5
                    dve.wait_ge(dve_job, JV.done("qk", b, 2 * k + 1))
                    a, r, part = RT[:, k, 0, :], RT[:, k, 1, :], PS[:, s, k, :, :]
                    link(dve.tensor_tensor(a, a, r, ALU.add))
                    link(dve.tensor_copy(part[:, 0, :], a))
                    link(dve.tensor_tensor(r, a, part[:, 0, :], ALU.subtract))
                    link(dve.tensor_copy(part[:, 1, :], r))
                    dve.tensor_tensor(part[:, 2, :], r, part[:, 1, :], ALU.subtract).then_inc(s_ps, 1)
                elif step == "max":
                    q, h0, n = amax[i]
                    dve.tensor_reduce(MX[:, q, h0:h0 + n],
                                      bank("max", b, i)[:, 0:n * (q + 1) * P].rearrange("p (h k) -> p h k", h=n),
                                      AX.X, ALU.max).then_inc(dve_job, 1)
                elif step == "take":
                    dve.wait_ge(dve_job, JV.done("max", b, len(amax) - 1))
                    if b:
                        dve.wait_ge(pe_a, JA.done("nm", b - 1))
                    link(dve.tensor_scalar(MR[:, :, :], MX[:, :, :], -CLAMP, CLAMP, ALU.max, ALU.min))
                    link(dve.tensor_scalar(MX[:, :, :], MR[:, :, :], -1.0, None, ALU.mult))
                    link(dve.tensor_copy(N3[:, :, 0, :], MX[:, :, :]))
                    link(dve.tensor_tensor(MR[:, :, :], MX[:, :, :], N3[:, :, 0, :], ALU.subtract))
                    link(dve.tensor_copy(N3[:, :, 1, :], MR[:, :, :]))
                    dve.tensor_tensor(N3[:, :, 2, :], MR[:, :, :], N3[:, :, 1, :], ALU.subtract).then_inc(s_nm, 1)
                elif step == "probs" and b + i:
                    clamp(b * HB + i - 1)
                elif step == "values" and b == B - 1 and i == 3:
                    clamp(B * HB - 1)
                elif step == "norm":
                    src = bank("den", b, i)[:, :].rearrange("p (t j r) -> p t j r", t=TB, j=4)
                    if i or b:
                        dve.wait_ge(dve_job, JV.done("den", b, i) - 1)
                    link(dve.reciprocal(RC[:, :, :], src[:, :, :, DB]))
                    if i == 0 and b:
                        dve.wait_ge(pe_a, JA.done("oT", b - 1))
                    dve.tensor_tensor(OTK[:, :, 4 * DB * i:4 * DB * (i + 1)].rearrange("p t (j d) -> p t j d", j=4),
                                      src[:, :, :, 0:DB], RC[:, :, :].to_broadcast([P, TB, 4, DB]), ALU.mult).then_inc(dve_job, 1)
                elif step == "out":
                    xb = X[:, b * TB:(b + 1) * TB, :].rearrange("p t d -> p (t d)")
                    dve.tensor_tensor(xb, xb, bank("out", b)[:, :], ALU.add).then_inc(dve_job, 1)
                    dve.wait_ge(dve_job, JV.done("out", b))
                    for t in range(b * TB, b * TB + TB):
                        ins = dve.bn_stats(stats6[:, t, :], X[:, t, :])
                    link(ins)
                    for t in range(b * TB, b * TB + TB):
                        dve.bn_aggr(mv[:, t, :], stats6[:, t, :])


def layers(nc, x_in, x_out, wa, wb, wf, ca, cb, cf):
    x1 = nc.dram_tensor("x1", [T, D], F32).ap()
    xbuf = nc.dram_tensor("xbuf", [SLOTS + T, D], F32).ap()
    ybuf = nc.dram_tensor("ybuf", [SLOTS + 1, D], F32).ap()
    stack = nc.dram_tensor("stack", [2, 2, 3, P, L], BF16).ap()
    with ExitStack() as sems:
        s_x = [sems.enter_context(nc.semaphore(f"batch{b}")) for b in range(B)]
        attn_a(nc, sems, s_x, x_in, x1, wa, ca)
        with nc.sbuf_tensor("X", [P, NT, D], F32) as X, nc.sbuf_tensor("mv", [P, NT, 2], F32) as mv:
            moe(nc, sems, s_x, 32, X, mv, x1, None, wf, cf, xbuf, ybuf, "f1")
            attn_b(nc, sems, X, mv, wb, cb, stack)
            moe(nc, sems, s_x, 64, X, mv, None, x_out, wf, cf, xbuf, ybuf, "f2")


def kernel(**inputs):
    import concourse.bacc as _bacc
    from concourse.bass_utils import run_bass_kernel_spmd as _run

    x = np.ascontiguousarray(inputs["L0_attn_a_hidden_states"]).reshape(T, D)
    a = {n[len("L0_attn_a_"):]: np.asarray(v) for n, v in inputs.items() if n.startswith("L0_attn_a_")}
    b = {n[len("L0_attn_b_"):]: np.asarray(v) for n, v in inputs.items() if n.startswith("L0_attn_b_")}
    f = {n[len("L0_ffn_w_"):]: np.asarray(v) for n, v in inputs.items() if n.startswith("L0_ffn_w_")}

    fir = np.zeros((H, DK // 2, 2, 2, 3 * KL), np.float32)
    fir[..., 0, KL - 1:2 * KL - 1] = a["fir_long_w"].reshape(H, DK // 2, 2, KL)[..., ::-1]
    fir[..., 1, KL - 1:KL + 4] = a["fir_short_w"].reshape(H, DK // 2, 2, 5)[..., ::-1]
    fir = fir.transpose(1, 0, 2, 3, 4).reshape(P, 2, 3 * KL)
    swap = np.arange(D) ^ 1
    weights = {
        "a": {"qkvT": np.stack([a["q_w"].T, a["k_w"].T, a["v_w"].T], axis=1),
              "cw": np.stack([a["q_cw"].T, a["k_cw"].T, a["v_cw"].T]),
              "bT": a["b_w"].T, "w1xT": a["mlp1_w"][:, :D].T, "w1sT": a["mlp1_w"][:, D:].T,
              "oT": a["o_w"].T, "fir": fir, "w2T": a["mlp2_w"].T, "b2": a["mlp2_b"],
              "temp": a["logit_temp"], "res": a["conv_res_logit"],
              "norm": a["norm_w"].reshape(DK, 1), "b1": a["mlp1_b"].reshape(P, 1)},
        "b": {"qkv": np.stack([b["WQ"].T, b["WQ"][swap].T, b["WK"].T, b["WK"][swap].T, b["WV"].T], axis=1),
              "o": b["WO"].T},
        "f": f,
    }

    p, q = np.arange(P)[:, None], np.arange(P)[None]
    r, c = p % C, np.arange(C)[None]
    turns = np.float32(10000.0) ** -(((p % DB) // 2).astype(np.float32) / np.float32(DB // 2))
    angle = np.arange(L, dtype=np.float32)[None] * turns
    cos, sin = np.cos(angle), np.sin(angle) * np.where(p % 2 == 0, -1.0, 1.0)
    later = np.where(q > p, -1e30, 0.0)
    ident = p == q
    constants = {
        "a": {"ident": ident, "flip": p + q == P - 1, "masks": np.stack([-1.0 * (r > c), 1.0 * (c >= r), 1.0 * (c == r)], axis=1)},
        "b": {"ident": ident, "causal": np.stack([later, later.T], axis=1),
              "rope": np.stack([cos / np.sqrt(DB), sin / np.sqrt(DB), cos, sin], axis=1)},
        "f": {"ident": ident, "tri": p <= q, "rank": np.tile(np.arange(E_, 0, -1), (P, 1)),
              "dump": SLOTS + p + P * np.arange(NT)[None]},
    }

    nc = _bacc.Bacc("TRN2", target_bir_lowering=False, num_devices=1)
    arrays = {}

    def given(name, array):
        arrays[name] = np.ascontiguousarray(array)
        return nc.dram_tensor(name, array.shape, mybir.dt.from_np(array.dtype), kind="ExternalInput").ap()

    x_ap = given("in_x_dram", x)
    w = {k: {n: given(f"in_{k}_{n}_dram", v) for n, v in d.items()} for k, d in weights.items()}
    cst = {k: {n: given(f"const_{k}_{n}_dram", v.astype(np.float32)) for n, v in d.items()} for k, d in constants.items()}
    out = nc.dram_tensor("out_0_dram", (T, D), F32, kind="ExternalOutput").ap()
    layers(nc, x_ap, out, w["a"], w["b"], w["f"], cst["a"], cst["b"], cst["f"])
    got = _run(nc, [arrays], core_ids=[0])
    return got.results[0]["out_0_dram"].reshape(B, L, D)
```
